# Optimizing a Trainium2 kernel written in Bass

```python
import numpy as np
import jax
import jax.numpy as jnp

def _softmax(x, axis=-1):
    return jax.nn.softmax(x, axis=axis)

def _gelu(x):
    return jax.nn.gelu(x, approximate=True)

def _silu(x):
    return jax.nn.silu(x)

def _sigmoid(x):
    return jax.nn.sigmoid(x)

def _layernorm(x, axis=-1, eps=1e-05):
    m = jnp.mean(x, axis=axis, keepdims=True)
    v = jnp.var(x, axis=axis, keepdims=True)
    return (x - m) / jnp.sqrt(v + eps)

def _scatter_add(tgt, idx, src, axis=0):
    return tgt.at[idx].add(src)

def _segment_sum(src, seg, n):
    return jax.ops.segment_sum(src, seg, n)
kernel_name = 'mk_gnn_ffn_d2_gnn_r8_57d61c'

def setup_inputs(seed: int=0):
    np.random.seed(seed)
    _w = jnp.asarray

    def _rec_inputs():
        import jax
        import jax.numpy as jnp
        _gk = jax.random.key(seed)
        x = -0.0003713 + 1 * jax.random.normal(jax.random.fold_in(_gk, 1), (6250, 256), jnp.float32)
        src = jax.random.randint(jax.random.fold_in(_gk, 2), (100000,), 0, 6250, jnp.int32)
        dst = jnp.minimum((6250 * jax.random.uniform(jax.random.fold_in(_gk, 3), (100000,)) ** 2.0).astype(jnp.int32), 49999)
        _o = jnp.argsort(dst, stable=True)
        src = src[_o]
        dst = dst[_o]
        return (x, src, dst)
    x, src, dst = _rec_inputs()

    def _L0_gnn_setup():
        import jax, jax.numpy as jnp
        import numpy as np
        N_NODES = 6250
        N_EDGES = 100000
        F_IN = 256
        HEADS = 4
        C_OUT = 64
        NEG_SLOPE = 0.2
        key = jax.random.key(seed)
        ks = jax.random.split(key, 6)
        glorot_lin = (6.0 / (F_IN + HEADS * C_OUT)) ** 0.5
        glorot_att = (6.0 / (HEADS * C_OUT)) ** 0.5
        return {'x': jax.random.normal(ks[0], (N_NODES, F_IN), dtype=jnp.float32), 'edge_index': jax.random.randint(ks[1], (2, N_EDGES), 0, N_NODES, dtype=jnp.int64), 'W_l': jax.random.uniform(ks[2], (F_IN, HEADS * C_OUT), jnp.float32, -glorot_lin, glorot_lin), 'b_l': jnp.zeros((HEADS * C_OUT,), jnp.float32), 'W_r': jax.random.uniform(ks[3], (F_IN, HEADS * C_OUT), jnp.float32, -glorot_lin, glorot_lin), 'b_r': jnp.zeros((HEADS * C_OUT,), jnp.float32), 'att': jax.random.uniform(ks[4], (HEADS, C_OUT), jnp.float32, -glorot_att, glorot_att), 'bias': jnp.zeros((HEADS * C_OUT,), jnp.float32)}
    _L0_gnn_all = _L0_gnn_setup()
    _L0_gnn_in = {k: v for k, v in _L0_gnn_all.items() if k in ('W_l', 'b_l', 'W_r', 'b_r', 'att', 'bias')}
    del _L0_gnn_all

    def _L0_ffn_setup():
        import jax, jax.numpy as jnp
        import numpy as np
        B, A = (512, 8)
        IN, OUT = (256, 256)
        SH1, SH2 = (256, 128)
        EH1, EH2 = (128, 64)
        E, TOPK = (4, 2)

        def _shared_mlp(x, W1, b1, W2, b2, W3, b3):
            h = jax.nn.relu(x @ W1 + b1)
            h = jax.nn.relu(h @ W2 + b2)
            return h @ W3 + b3

        def _experts_mlp(x, eW1, eb1, eW2, eb2, eW3, eb3):
            h = jax.nn.relu(jnp.einsum('baf,efh->ebah', x, eW1) + eb1[:, None, None, :])
            h = jax.nn.relu(jnp.einsum('ebah,ehg->ebag', h, eW2) + eb2[:, None, None, :])
            o = jnp.einsum('ebag,ego->ebao', h, eW3) + eb3[:, None, None, :]
            return jnp.moveaxis(o, 0, -1)
        key = jax.random.key(seed)
        ks = jax.random.split(key, 16)
        s = 0.05
        return {'x': jax.random.normal(ks[0], (B, A, IN), jnp.float32), 'sW1': jax.random.normal(ks[1], (IN, SH1), jnp.float32) * s, 'sb1': jnp.zeros((SH1,), jnp.float32), 'sW2': jax.random.normal(ks[2], (SH1, SH2), jnp.float32) * s, 'sb2': jnp.zeros((SH2,), jnp.float32), 'sW3': jax.random.normal(ks[3], (SH2, OUT), jnp.float32) * s, 'sb3': jnp.zeros((OUT,), jnp.float32), 'eW1': jax.random.normal(ks[4], (E, IN, EH1), jnp.float32) * s, 'eb1': jnp.zeros((E, EH1), jnp.float32), 'eW2': jax.random.normal(ks[5], (E, EH1, EH2), jnp.float32) * s, 'eb2': jnp.zeros((E, EH2), jnp.float32), 'eW3': jax.random.normal(ks[6], (E, EH2, OUT), jnp.float32) * s, 'eb3': jnp.zeros((E, OUT), jnp.float32), 'gW': jax.random.normal(ks[7], (IN, E), jnp.float32) * s, 'gb': jnp.zeros((E,), jnp.float32)}
    _L0_ffn_all = _L0_ffn_setup()
    _L0_ffn_in = {k: v for k, v in _L0_ffn_all.items() if k in ('sW1', 'sb1', 'sW2', 'sb2', 'sW3', 'sb3', 'eW1', 'eb1', 'eW2', 'eb2', 'eW3', 'eb3', 'gW', 'gb')}
    del _L0_ffn_all

    def _L1_gnn_setup():
        import jax, jax.numpy as jnp
        import numpy as np
        N, E, D = (2500, 40000, 256)
        BN_EPS = 1e-05
        key = jax.random.key(seed)
        ks = jax.random.split(key, 6)
        s = 1.0 / np.sqrt(D)
        return {'x': jax.random.normal(ks[0], (N, D), dtype=jnp.float32), 'edge_index': jax.random.randint(ks[1], (2, E), 0, N, dtype=jnp.int64), 'W_proj': jax.random.normal(ks[2], (D, D), dtype=jnp.float32) * s, 'b_proj': jnp.zeros((D,), dtype=jnp.float32), 'W_l': jax.random.normal(ks[3], (D, D), dtype=jnp.float32) * s, 'b_l': jnp.zeros((D,), dtype=jnp.float32), 'W_r': jax.random.normal(ks[4], (D, D), dtype=jnp.float32) * s, 'gamma': jnp.ones((D,), dtype=jnp.float32), 'beta': jnp.zeros((D,), dtype=jnp.float32)}
    _L1_gnn_all = _L1_gnn_setup()
    _L1_gnn_in = {k: v for k, v in _L1_gnn_all.items() if k in ('W_proj', 'b_proj', 'W_l', 'b_l', 'W_r', 'gamma', 'beta')}
    del _L1_gnn_all

    def _L1_ffn_setup():
        import jax, jax.numpy as jnp
        import numpy as np
        B, S, D, F, E, K = (8, 256, 256, 1024, 8, 2)
        key = jax.random.key(seed)
        ks = jax.random.split(key, 10)
        s = 0.02
        return {'x': jax.random.normal(ks[0], (B, S, D), dtype=jnp.float32), 'Wr': jax.random.normal(ks[1], (D, E), dtype=jnp.float32) * s, 'W1s': jax.random.normal(ks[2], (D, F), dtype=jnp.float32) * s, 'b1s': jnp.zeros((F,), dtype=jnp.float32), 'W2s': jax.random.normal(ks[3], (F, D), dtype=jnp.float32) * s, 'b2s': jnp.zeros((D,), dtype=jnp.float32), 'W1p': jax.random.normal(ks[4], (E, D, F), dtype=jnp.float32) * s, 'b1p': jnp.zeros((E, F), dtype=jnp.float32), 'W2p': jax.random.normal(ks[5], (E, F, D), dtype=jnp.float32) * s, 'b2p': jnp.zeros((E, D), dtype=jnp.float32)}
    _L1_ffn_all = _L1_ffn_setup()
    _L1_ffn_in = {k: v for k, v in _L1_ffn_all.items() if k in ('Wr', 'W1s', 'b1s', 'W2s', 'b2s', 'W1p', 'b1p', 'W2p', 'b2p')}
    del _L1_ffn_all
    return {'x': x, 'src': src, 'dst': dst, 'L0_gnn_W_l': _L0_gnn_in['W_l'], 'L0_gnn_b_l': _L0_gnn_in['b_l'], 'L0_gnn_W_r': _L0_gnn_in['W_r'], 'L0_gnn_b_r': _L0_gnn_in['b_r'], 'L0_gnn_att': _L0_gnn_in['att'], 'L0_gnn_bias': _L0_gnn_in['bias'], 'L0_ffn_sW1': _L0_ffn_in['sW1'], 'L0_ffn_sb1': _L0_ffn_in['sb1'], 'L0_ffn_sW2': _L0_ffn_in['sW2'], 'L0_ffn_sb2': _L0_ffn_in['sb2'], 'L0_ffn_sW3': _L0_ffn_in['sW3'], 'L0_ffn_sb3': _L0_ffn_in['sb3'], 'L0_ffn_eW1': _L0_ffn_in['eW1'], 'L0_ffn_eb1': _L0_ffn_in['eb1'], 'L0_ffn_eW2': _L0_ffn_in['eW2'], 'L0_ffn_eb2': _L0_ffn_in['eb2'], 'L0_ffn_eW3': _L0_ffn_in['eW3'], 'L0_ffn_eb3': _L0_ffn_in['eb3'], 'L0_ffn_gW': _L0_ffn_in['gW'], 'L0_ffn_gb': _L0_ffn_in['gb'], 'L1_gnn_W_proj': _L1_gnn_in['W_proj'], 'L1_gnn_b_proj': _L1_gnn_in['b_proj'], 'L1_gnn_W_l': _L1_gnn_in['W_l'], 'L1_gnn_b_l': _L1_gnn_in['b_l'], 'L1_gnn_W_r': _L1_gnn_in['W_r'], 'L1_gnn_gamma': _L1_gnn_in['gamma'], 'L1_gnn_beta': _L1_gnn_in['beta'], 'L1_ffn_Wr': _L1_ffn_in['Wr'], 'L1_ffn_W1s': _L1_ffn_in['W1s'], 'L1_ffn_b1s': _L1_ffn_in['b1s'], 'L1_ffn_W2s': _L1_ffn_in['W2s'], 'L1_ffn_b2s': _L1_ffn_in['b2s'], 'L1_ffn_W1p': _L1_ffn_in['W1p'], 'L1_ffn_b1p': _L1_ffn_in['b1p'], 'L1_ffn_W2p': _L1_ffn_in['W2p'], 'L1_ffn_b2p': _L1_ffn_in['b2p']}

def reference(x, src, dst, L0_gnn_W_l, L0_gnn_b_l, L0_gnn_W_r, L0_gnn_b_r, L0_gnn_att, L0_gnn_bias, L0_ffn_sW1, L0_ffn_sb1, L0_ffn_sW2, L0_ffn_sb2, L0_ffn_sW3, L0_ffn_sb3, L0_ffn_eW1, L0_ffn_eb1, L0_ffn_eW2, L0_ffn_eb2, L0_ffn_eW3, L0_ffn_eb3, L0_ffn_gW, L0_ffn_gb, L1_gnn_W_proj, L1_gnn_b_proj, L1_gnn_W_l, L1_gnn_b_l, L1_gnn_W_r, L1_gnn_gamma, L1_gnn_beta, L1_ffn_Wr, L1_ffn_W1s, L1_ffn_b1s, L1_ffn_W2s, L1_ffn_b2s, L1_ffn_W1p, L1_ffn_b1p, L1_ffn_W2p, L1_ffn_b2p):
    import jax
    import jax.numpy as jnp

    def _L0_gnn_ref(x, edge_index, W_l, b_l, W_r, b_r, att, bias):
        import jax, jax.numpy as jnp
        import numpy as np
        N_NODES = 6250
        N_EDGES = 100000
        F_IN = 256
        HEADS = 4
        C_OUT = 64
        NEG_SLOPE = 0.2
        N = x.shape[0]
        H, C = att.shape
        x_l = (x @ W_l + b_l).reshape(N, H, C)
        x_r = (x @ W_r + b_r).reshape(N, H, C)
        loop = jnp.arange(N, dtype=edge_index.dtype)
        src = jnp.concatenate([edge_index[0], loop])
        dst = jnp.concatenate([edge_index[1], loop])
        e = jax.nn.leaky_relu(x_l[src] + x_r[dst], NEG_SLOPE)
        logits = jnp.einsum('ehc,hc->eh', e, att)
        m = jax.ops.segment_max(logits, dst, num_segments=N)
        a = jnp.exp(logits - m[dst])
        denom = jax.ops.segment_sum(a, dst, num_segments=N)
        alpha = a / denom[dst]
        out = jax.ops.segment_sum(alpha[:, :, None] * x_l[src], dst, num_segments=N)
        return out.reshape(N, H * C) + bias

    def _L0_ffn_ref(x, sW1, sb1, sW2, sb2, sW3, sb3, eW1, eb1, eW2, eb2, eW3, eb3, gW, gb):
        import jax, jax.numpy as jnp
        import numpy as np
        B, A = (512, 8)
        IN, OUT = (256, 256)
        SH1, SH2 = (256, 128)
        EH1, EH2 = (128, 64)
        E, TOPK = (4, 2)

        def _shared_mlp(x, W1, b1, W2, b2, W3, b3):
            h = jax.nn.relu(x @ W1 + b1)
            h = jax.nn.relu(h @ W2 + b2)
            return h @ W3 + b3

        def _experts_mlp(x, eW1, eb1, eW2, eb2, eW3, eb3):
            h = jax.nn.relu(jnp.einsum('baf,efh->ebah', x, eW1) + eb1[:, None, None, :])
            h = jax.nn.relu(jnp.einsum('ebah,ehg->ebag', h, eW2) + eb2[:, None, None, :])
            o = jnp.einsum('ebag,ego->ebao', h, eW3) + eb3[:, None, None, :]
            return jnp.moveaxis(o, 0, -1)
        all_out = _experts_mlp(x, eW1, eb1, eW2, eb2, eW3, eb3)
        shared = _shared_mlp(x, sW1, sb1, sW2, sb2, sW3, sb3)
        gates = jax.nn.softmax(x @ gW + gb, axis=-1)
        topv, topi = jax.lax.top_k(gates, TOPK)
        topw = jax.nn.softmax(topv, axis=-1)
        sel = jnp.take_along_axis(all_out, topi[:, :, None, :], axis=-1)
        gated = jnp.sum(sel * topw[:, :, None, :], axis=-1)
        return shared + gated

    def _L1_gnn_ref(x, edge_index, W_proj, b_proj, W_l, b_l, W_r, gamma, beta):
        import jax, jax.numpy as jnp
        import numpy as np
        N, E, D = (2500, 40000, 256)
        BN_EPS = 1e-05
        n = x.shape[0]
        loops = jnp.arange(n, dtype=edge_index.dtype)
        src = jnp.concatenate([edge_index[0], loops])
        dst = jnp.concatenate([edge_index[1], loops])
        xp = jax.nn.relu(x @ W_proj.T + b_proj)
        agg = jax.ops.segment_max(xp[src], dst, num_segments=n)
        out = agg @ W_l.T + b_l + x @ W_r.T
        out = jax.nn.relu(out)
        mean = jnp.mean(out, axis=0)
        var = jnp.var(out, axis=0)
        out = (out - mean) * jax.lax.rsqrt(var + BN_EPS) * gamma + beta
        return out

    def _L1_ffn_ref(x, Wr, W1s, b1s, W2s, b2s, W1p, b1p, W2p, b2p):
        import jax, jax.numpy as jnp
        import numpy as np
        B, S, D, F, E, K = (8, 256, 256, 1024, 8, 2)
        gelu = lambda t: jax.nn.gelu(t, approximate=False)
        shared = gelu(x @ W1s + b1s) @ W2s + b2s
        rw = jax.nn.softmax(x @ Wr, axis=-1)
        topw, topi = jax.lax.top_k(rw, K)
        topw = topw / jnp.sum(topw, axis=-1, keepdims=True)
        mask = jnp.sum(jax.nn.one_hot(topi, E, dtype=topw.dtype) * topw[..., None], axis=-2)
        h = gelu(jnp.einsum('bsd,edf->bsef', x, W1p) + b1p)
        priv = jnp.einsum('bsef,efd->bsed', h, W2p) + b2p
        routed = jnp.einsum('bsed,bse->bsd', priv, mask)
        return shared + routed
    edge_index = jnp.stack([src, dst])
    x = x + _L0_gnn_ref(_layernorm(x, axis=-1), edge_index, L0_gnn_W_l, L0_gnn_b_l, L0_gnn_W_r, L0_gnn_b_r, L0_gnn_att, L0_gnn_bias)
    x = x + _L0_ffn_ref(_layernorm(x, axis=-1)[None], L0_ffn_sW1, L0_ffn_sb1, L0_ffn_sW2, L0_ffn_sb2, L0_ffn_sW3, L0_ffn_sb3, L0_ffn_eW1, L0_ffn_eb1, L0_ffn_eW2, L0_ffn_eb2, L0_ffn_eW3, L0_ffn_eb3, L0_ffn_gW, L0_ffn_gb)[0]
    x = x + _L1_gnn_ref(_layernorm(x, axis=-1), edge_index, L1_gnn_W_proj, L1_gnn_b_proj, L1_gnn_W_l, L1_gnn_b_l, L1_gnn_W_r, L1_gnn_gamma, L1_gnn_beta)
    x = x + _L1_ffn_ref(_layernorm(x, axis=-1)[None], L1_ffn_Wr, L1_ffn_W1s, L1_ffn_b1s, L1_ffn_W2s, L1_ffn_b2s, L1_ffn_W1p, L1_ffn_b1p, L1_ffn_W2p, L1_ffn_b2p)[0]
    return x

_drawn_inputs = setup_inputs


def setup_inputs(seed=0):
    import zlib

    import numpy as np

    out = dict(_drawn_inputs(seed))
    spreads = {'L0_gnn_b_l': (0.0, 0.1),
     'L0_gnn_b_r': (0.0, 0.598),
     'L0_gnn_bias': (0.0, 0.1),
     'L0_ffn_sb1': (0.0, 0.303),
     'L0_ffn_sb2': (0.0, 0.1),
     'L0_ffn_sb3': (0.0, 0.1),
     'L0_ffn_eb1': (0.0, 0.712),
     'L0_ffn_eb2': (0.0, 0.355),
     'L0_ffn_eb3': (0.0, 0.1),
     'L0_ffn_gb': (0.0, 0.1),
     'L1_gnn_b_proj': (0.0, 0.1),
     'L1_gnn_b_l': (0.0, 0.1),
     'L1_gnn_gamma': (1.0, 0.2),
     'L1_gnn_beta': (0.0, 0.1),
     'L1_ffn_b1s': (0.0, 0.349),
     'L1_ffn_b2s': (0.0, 0.1),
     'L1_ffn_b1p': (0.0, 0.484),
     'L1_ffn_b2p': (0.0, 0.1)}
    factors = {}
    for name, (base, spread) in spreads.items():
        noise = np.random.default_rng([zlib.crc32(name.encode()), seed]).standard_normal(out[name].shape)
        drawn = base * np.exp(spread * noise) if base else spread * noise
        out[name] = jnp.asarray(drawn.astype(out[name].dtype))
    for name, factor in factors.items():
        out[name] = (out[name] * factor).astype(out[name].dtype)
    return out
```

```python
from contextlib import ExitStack

import numpy as np
import concourse.bass as bass
from concourse import mybir

F32, I32 = mybir.dt.float32, mybir.dt.int32
ALU = mybir.AluOpType
ACT = mybir.ActivationFunctionType
AX = mybir.AxisListType

P = 128
N, E, F = 6250, 100000, 256
KF = F // P
H, C = 4, 64
NT = -(-N // P)
NP = NT * P
TAIL = N - (NT - 1) * P
T = 7
NB = 4
EP = 784
CH = EP // T
ELAST = E - (P - 1) * EP
XW = F + H
SW = F + 2 * H
BIG = 1.0e6
NEG = -1.0e30
SLOPE = 0.2
LN_EPS = 1e-5
TU = 7
NG = NT // TU
GW = TU * P // 2
assert CH * T == EP and CH % NB == 0 and NG * TU == NT and 0 < ELAST < EP


class Chain:

    def __init__(self, eng, sem):
        self.eng, self.sem, self.n, self.base = eng, sem, 0, 0

    def __call__(self, ins):
        ins.then_inc(self.sem, 1)
        self.n += 1

    def wait(self):
        if isinstance(self.base, int) and self.base + self.n == 0:
            return
        self.eng.wait_ge(self.sem, self.base + self.n)

    def enter(self, i, per_trip):
        self.before, self.per_trip = self.base + self.n, per_trip
        self.base, self.n = self.before + i * per_trip, 0

    def leave(self, trips):
        assert self.n == self.per_trip, (self.n, self.per_trip)
        self.base, self.n = self.before + trips * self.per_trip, 0


def graph_block_kernel(nc, a, out, stage=9):
    ctx = ExitStack()
    with ctx:
        def dram(name, shape, dt=F32):
            return nc.dram_tensor(name, shape, dt, kind="Internal").ap()

        def sem(name):
            return ctx.enter_context(nc.semaphore(name))

        def sb(name, shape, dt=F32, c=ctx):
            return c.enter_context(nc.sbuf_tensor(name, shape, dt))

        def ps(name, shape, c):
            return c.enter_context(nc.psum_tensor(name, shape, F32))

        xl_tab, xr_tab = dram("xl_tab", (NP, XW)), dram("xr_tab", (NP, XW))
        xp_tab = dram("xp_tab", (NP, F))
        dst_rows = dram("dst_rows", (P, EP))
        soft_tab = dram("soft_tab", (P * EP + 1, SW))
        soft_carry = dram("soft_carry", (P + 1, SW))
        max_tab = dram("max_tab", (P * EP + 1, F))
        max_carry = dram("max_carry", (P + 1, F))

        X = sb("X", [P, NT, F])
        ident = sb("ident", [P, P])
        ones = sb("ones", [P, P])
        node = sb("node", [P, NT])
        idx_end = sb("idx_end", [P, NT], I32)
        idx_carry = sb("idx_carry", [P, NT], I32)
        dl_col = sb("dl_col", [P, 1])
        dl_row = sb("dl_row", [P, P])
        src_i, dst_i = sb("src_i", [P, EP], I32), sb("dst_i", [P, EP], I32)
        keep, pen = sb("keep", [P, EP]), sb("pen", [P, EP])

        c_v, c_a, c_t, c_p = sem("dve_step"), sem("act_step"), sem("pe_step"), sem("pool_step")
        settle = sem("wait_stood_alone")
        loaded, stored = sem("loaded"), sem("stored")
        total = {"loaded": 0, "stored": 0, "v": 0, "a": 0, "t": 0, "p": 0}

        def load(eng, dst, src):
            eng.dma_start(dst, src).then_inc(loaded, 16)
            total["loaded"] += 16

        def store(eng, dst, src):
            eng.dma_start(dst, src).then_inc(stored, 16)
            total["stored"] += 16

        def chain(eng, s, key):
            c = Chain(eng, s)
            c.n = total[key]
            return c

        def alone(eng):
            eng.sem_inc(settle, 1)

        def prime(eng, *sems):
            for s in sems:
                eng.sem_inc(s, 1)

        def done(eng, s, n):
            eng.wait_ge(s, n + 1)

        def row(vec, n):
            return vec.rearrange("(a n) -> a n", a=1).broadcast_to([P, n])

        s_id, s_dst = sem("ident_ready"), sem("dst_ready")
        s_rows = [sem("dst_row_landed0"), sem("dst_row_landed1")]
        s_ridx, s_rused = sem("row_index_ready"), sem("dst_row_counted")
        with ExitStack() as c:
            node_b = sb("node_b", [P, NT, P], c=c)
            dst_f = sb("dst_f", [P, EP], c=c)
            rows = sb("rows", [P, 2, EP], c=c)
            scr = sb("scr", [P, EP], c=c)
            below, upto = sb("below", [P, NT], c=c), sb("upto", [P, NT], c=c)
            cnt_lt, cnt_le = sb("cnt_lt", [P, NT], c=c), sb("cnt_le", [P, NT], c=c)
            fa, fb = sb("fa", [P, NT], c=c), sb("fb", [P, NT], c=c)
            rowi = sb("rowi", [P, NT], I32, c=c)
            dlb = ps("dlb", [P, P], c)
            block = c.enter_context(nc.Block())

            @block.sync
            def _(sp):
                sp.wait_ge(s_id, 6)
                load(sp, X[:, 0:NT - 1, :], a["x"][0:(NT - 1) * P, :].rearrange("(t p) f -> p t f", p=P))
                load(sp, X[0:TAIL, NT - 1, :], a["x"][(NT - 1) * P:N, :])
                for t, v in ((src_i, a["src"]), (dst_i, a["dst"])):
                    load(sp, t[0:P - 1, :], v[0:(P - 1) * EP].rearrange("(p e) -> p e", p=P - 1))
                    load(sp, t[P - 1:P, 0:ELAST], v[(P - 1) * EP:E].rearrange("(p e) -> p e", p=1))
                sp.wait_ge(s_dst, 1)
                store(sp, dst_rows, dst_f[:, :])

            @block.gpsimd
            def _(pool):
                p = chain(pool, c_p, "p")
                nc.gpsimd.memset(X[:, NT - 1, :], 0.0).then_inc(s_id, 1)
                nc.gpsimd.memset(src_i[:, ELAST:], 0).then_inc(s_id, 1)
                nc.gpsimd.memset(dst_i[:, ELAST:], int(BIG)).then_inc(s_id, 1)
                nc.gpsimd.memset(ones[:, :], 1.0).then_inc(s_id, 1)
                p(nc.gpsimd.memset(ident[:, :], 0.0))
                p.wait()
                nc.gpsimd.affine_select(out=ident[:, :], in_=ident[:, :], compare_op=ALU.not_equal, fill=1.0,
                                        base=0, pattern=[[-1, P]], channel_multiplier=1).then_inc(s_id, 1)
                nc.gpsimd.iota(node[:, :], [[P, NT]], base=0, channel_multiplier=1,
                               allow_small_or_imprecise_dtypes=True).then_inc(s_id, 1)
                pool.wait_ge(s_ridx, 1)
                pool.wait_ge(stored, total["stored"])
                for t in range(NT):
                    if t >= 2:
                        pool.wait_ge(s_rused, t - 1)
                    pool.indirect_dma_start(rows[:, t % 2, :], None, dst_rows,
                                            bass.IndirectOffsetOnAxis(rowi[:, t:t + 1], 0)).then_inc(s_rows[t % 2], 16)
                total["p"] = p.n

            @block.tensor
            def _(pe):
                pe.wait_ge(s_id, 6)
                pe.wait_ge(s_dst, 2)
                nc.tensor.matmul(dlb[:, :], dl_col[:, 0:1].broadcast_to([P, P]), ident[:, :],
                                 start=True, stop=True).then_inc(c_t, 1)
                total["t"] = 1

            @block.vector
            def _(dve):
                v = chain(dve, c_v, "v")
                dve.wait_ge(loaded, total["loaded"])
                nc.vector.tensor_copy(dst_f[:, :], dst_i[:, :]).then_inc(s_dst, 1)
                dve.wait_ge(s_dst, 1)
                nc.vector.tensor_copy(dl_col[:, :], dst_f[:, EP - 1:EP]).then_inc(s_dst, 1)
                v(nc.vector.memset(keep[:, 0:1], 0.0))
                v(nc.vector.tensor_tensor(keep[:, 1:EP], dst_f[:, 1:EP], dst_f[:, 0:EP - 1], ALU.is_equal))
                v.wait()
                v(nc.vector.tensor_scalar(pen[:, :], keep[:, :], 1.0, -NEG, ALU.subtract, ALU.mult))
                dve.wait_ge(s_dst, 2)
                v(nc.vector.tensor_scalar(scr[:, :], dst_f[:, :], float(N - 1), None, ALU.min))
                v.wait()
                v(nc.vector.tensor_copy(dst_i[:, :], scr[:, :]))
                dve.wait_ge(c_t, 1)
                v(nc.vector.tensor_copy(dl_row[:, :], dlb[:, :]))
                v.wait()
                dve.wait_ge(s_id, 6)
                dlv = dl_row[:, :].unsqueeze(1).broadcast_to([P, NT, P])
                nov = node[:, :].unsqueeze(2).broadcast_to([P, NT, P])
                for op, dst in ((ALU.is_lt, below), (ALU.is_le, upto)):
                    v(nc.vector.tensor_tensor(node_b[:, :, :], dlv, nov, op))
                    v.wait()
                    v(nc.vector.tensor_reduce(dst[:, :], node_b[:, :, :], AX.X, ALU.add))
                    v.wait()
                nc.vector.tensor_copy(rowi[:, :], upto[:, :]).then_inc(s_ridx, 1)
                for t in range(NT):
                    dve.wait_ge(s_rows[t % 2], 16 * (t // 2 + 1))
                    v.wait()
                    v(nc.vector.tensor_scalar(scr[:, :], rows[:, t % 2, :], node[:, t:t + 1], 0.0, ALU.is_lt, ALU.add,
                                              accum_out=cnt_lt[:, t:t + 1]))
                    v.wait()
                    nc.vector.tensor_scalar(scr[:, :], rows[:, t % 2, :], node[:, t:t + 1], 0.0, ALU.is_le, ALU.add,
                                            accum_out=cnt_le[:, t:t + 1]).then_inc(s_rused, 1)
                    dve.wait_ge(s_rused, t + 1)
                steps = [
                    lambda: nc.vector.tensor_tensor(fa[:, :], cnt_le[:, :], cnt_lt[:, :], ALU.is_gt),
                    lambda: nc.vector.tensor_scalar(fb[:, :], upto[:, :], float(EP), -1.0 - P * EP, ALU.mult, ALU.add),
                    lambda: nc.vector.tensor_tensor(fb[:, :], fb[:, :], cnt_le[:, :], ALU.add),
                    lambda: nc.vector.tensor_tensor(fb[:, :], fb[:, :], fa[:, :], ALU.mult),
                    lambda: nc.vector.tensor_scalar(fb[:, :], fb[:, :], float(P * EP), None, ALU.add),
                    lambda: nc.vector.tensor_copy(idx_end[:, :], fb[:, :]),
                    lambda: nc.vector.tensor_tensor(fa[:, :], upto[:, :], below[:, :], ALU.is_gt),
                    lambda: nc.vector.tensor_scalar(fb[:, :], upto[:, :], -1.0 - P, None, ALU.add),
                    lambda: nc.vector.tensor_tensor(fb[:, :], fb[:, :], fa[:, :], ALU.mult),
                    lambda: nc.vector.tensor_scalar(fb[:, :], fb[:, :], float(P), None, ALU.add),
                    lambda: nc.vector.tensor_copy(idx_carry[:, :], fb[:, :]),
                ]
                for s in steps:
                    v.wait()
                    v(s())
                v.wait()
                total["v"] = v.n

        def norm_phase(name, width, tokens, ph):
            s_var, s_std, s_rstd = sem(f"{name}_var_ready"), sem(f"{name}_std_ready"), sem(f"{name}_rstd_ready")
            s_xn, s_tp, s_ev = sem(f"{name}_xn_ready"), sem(f"{name}_transposed"), sem(f"{name}_xT_ready")
            s_xt, s_mm, s_use = sem(f"{name}_xT_kept"), sem(f"{name}_product"), sem(f"{name}_product_used")
            with ExitStack() as c:
                st6 = sb("st6" + name, [P, NT, 6], c=c)
                mean, rstd, tmp = (sb(n + name, [P, NT], c=c) for n in ("mean", "rstd", "tmp"))
                xn = sb("xn" + name, [P, 2, F], c=c)
                xts = sb("xts" + name, [P, 2, KF, P], c=c)
                w = sb("w" + name, [P, KF, width], c=c)
                xt_ps = [ps(f"xt_ps{b}" + name, [P, 512], c) for b in range(2)]
                mm_ps = [ps(f"mm_ps{b}" + name, [P, 512], c) for b in range(2)]
                xt_ps0 = xt_ps[0]
                ex = ph(c, w, xt_ps0)
                block = c.enter_context(nc.Block())

                def xt_view(b):
                    return xt_ps[b][:, 0:F].rearrange("p (k n) -> p k n", k=KF)

                @block.sync
                def _(sp):
                    ex["loads"](sp)
                    if "rows" in ex:
                        ex["rows"](sp, s_use)

                @block.vector
                def _(dve):
                    v = chain(dve, c_v, "v")
                    prime(dve, s_use, s_xn)
                    with dve.Fori(0, NG) as g:
                        v.enter(g, TU)
                        for j in range(TU):
                            v(nc.vector.bn_stats(st6[:, bass.ds(g * TU + j, 1), :], X[:, bass.ds(g * TU + j, 1), :]))
                        v.leave(NG)
                    v.wait()
                    v(nc.vector.tensor_tensor(mean[:, :], st6[:, :, 1], st6[:, :, 4], ALU.add))
                    v(nc.vector.tensor_tensor(tmp[:, :], st6[:, :, 1], st6[:, :, 4], ALU.subtract))
                    v.wait()
                    v(nc.vector.tensor_tensor(tmp[:, :], tmp[:, :], tmp[:, :], ALU.mult))
                    v(nc.vector.tensor_tensor(rstd[:, :], st6[:, :, 2], st6[:, :, 5], ALU.add))
                    v.wait()
                    v(nc.vector.tensor_scalar(rstd[:, :], rstd[:, :], 1.0 / F, LN_EPS, ALU.mult, ALU.add))
                    v(nc.vector.tensor_scalar(mean[:, :], mean[:, :], 0.5, None, ALU.mult))
                    v.wait()
                    nc.vector.scalar_tensor_tensor(out=rstd[:, :], in0=tmp[:, :], scalar=0.25, in1=rstd[:, :],
                                                   op0=ALU.mult, op1=ALU.add).then_inc(s_var, 1)
                    dve.wait_ge(s_std, 1)
                    nc.vector.reciprocal(rstd[:, :], tmp[:, :]).then_inc(s_rstd, 1)
                    dve.wait_ge(s_rstd, 1)
                    with dve.Fori(0, NG) as g:
                        v.enter(g, TU * ex["steps"])
                        for j in range(TU):
                            t, b = g * TU + j, j % 2
                            done(dve, s_tp, t - 1 if j >= 2 else g * TU)
                            nc.vector.tensor_scalar(xn[:, b:b + 1, :], X[:, bass.ds(t, 1), :], mean[:, bass.ds(t, 1)],
                                                    rstd[:, bass.ds(t, 1)], ALU.subtract, ALU.mult).then_inc(s_xn, 1)
                            if j >= 1:
                                done(dve, s_mm, t)
                                ex["consume"](v, dve, mm_ps[(j - 1) % 2], g, j - 1, s_use)
                        done(dve, s_mm, g * TU + TU)
                        ex["consume"](v, dve, mm_ps[(TU - 1) % 2], g, TU - 1, s_use)
                        v.leave(NG)
                    v.wait()
                    if "last" in ex:
                        ex["last"](v, dve)
                    total["v"] = v.base + v.n

                @block.scalar
                def _(act):
                    prime(act, s_ev)
                    act.wait_ge(s_var, 1)
                    nc.scalar.activation(tmp[:, :], rstd[:, :], ACT.Sqrt).then_inc(s_std, 1)
                    if "act" in ex:
                        ex["act"](act)
                    with act.Fori(0, NG) as g:
                        for j in range(TU):
                            t, b = g * TU + j, j % 2
                            done(act, s_tp, t + 1)
                            if tokens is not None:
                                done(act, s_xt, t - 1 if j >= 2 else g * TU)
                            done(act, s_mm, t - 1 if j >= 2 else g * TU)
                            nc.scalar.activation(xts[:, b, :, :], xt_view(b), ACT.Copy).then_inc(s_ev, 1)

                @block.gpsimd
                def _(pool):
                    prime(pool, s_xt)
                    if "pool" in ex:
                        ex["pool"](pool)
                    if tokens is not None:
                        with pool.Fori(0, NG) as g:
                            for j in range(TU):
                                t, b = g * TU + j, j % 2
                                done(pool, s_ev, t + 1)
                                alone(pool)
                                nc.gpsimd.tensor_copy(tokens[:, :, bass.ds(t * P, P)], xts[:, b, :, :]).then_inc(s_xt, 1)

                @block.tensor
                def _(pe):
                    prime(pe, s_tp, s_mm)
                    pe.wait_ge(loaded, total["loaded"])
                    if "pe" in ex:
                        ex["pe"](pe)
                    with pe.Fori(0, NG) as g:
                        for j in range(TU):
                            t, b = g * TU + j, j % 2
                            done(pe, s_xn, t + 1)
                            done(pe, s_ev, t - 1 if j >= 2 else g * TU)
                            for k in range(KF):
                                m = nc.tensor.transpose(xt_ps[b][:, k * P:(k + 1) * P], xn[:, b, k * P:(k + 1) * P], ident[:, :])
                            m.then_inc(s_tp, 1)
                            done(pe, s_ev, t + 1)
                            done(pe, s_use, t - 1 if j >= 2 else g * TU)
                            for k in range(KF):
                                m = nc.tensor.matmul(mm_ps[b][:, 0:width], xts[:, b, k, :], w[:, k, :],
                                                     start=(k == 0), stop=(k == KF - 1))
                            m.then_inc(s_mm, 1)

        USES = [(TU + 1) // 2, TU // 2]

        att_b = sb("att_b", [P, F])
        s_pst = [sem("proj_stored0"), sem("proj_stored1")]

        def proj(c, w, bank):
            bias = sb("proj_bias", [P, 2 * F], c=c)
            rowb, am = sb("proj_row", [P, 2, 2, XW], c=c), sb("proj_att", [P, 2, 2, F], c=c)

            def loads(sp):
                load(sp, w[:, :, 0:F], a["L0_gnn_W_l"].rearrange("(k p) n -> p k n", p=P))
                load(sp, w[:, :, F:2 * F], a["L0_gnn_W_r"].rearrange("(k p) n -> p k n", p=P))
                for b, n in enumerate(("L0_gnn_b_l", "L0_gnn_b_r")):
                    sp.dma_start(bias[:, b * F:(b + 1) * F], row(a[n], F)).then_inc(s_pst[b], 32)
                load(sp, att_b[:, :], row(a["L0_gnn_att"].rearrange("h c -> (h c)"), F))

            def consume(v, dve, mm, g, j, s_use):
                b = j % 2
                r, m = rowb[:, b, :, :], am[:, b, :, :]
                dve.wait_ge(s_pst[b], 32 * (g * USES[b] + j // 2 + 1))
                if j == 0:
                    dve.wait_ge(s_pst[1], 32)
                    dve.wait_ge(loaded, total["loaded"])
                v(nc.vector.tensor_tensor(r[:, :, 0:F], mm[:, 0:2 * F].rearrange("p (s f) -> p s f", s=2),
                                          bias[:, :].rearrange("p (s f) -> p s f", s=2), ALU.add))
                v.wait()
                for k in range(2):
                    v(nc.vector.scalar_tensor_tensor(out=m[:, k, :], in0=r[:, k, 0:F], scalar=SLOPE, in1=att_b[:, :],
                                                     op0=ALU.mult, op1=ALU.mult))
                v.wait()
                nc.vector.tensor_reduce(r[:, :, F:XW], m.rearrange("p s (h c) -> p s h c", h=H), AX.X,
                                        ALU.add).then_inc(s_use, 1)

            def rows(sp, s_use):
                with sp.Fori(0, NG) as g:
                    for j in range(TU):
                        t, b = g * TU + j, j % 2
                        done(sp, s_use, t + 1)
                        for k, tab in enumerate((xl_tab, xr_tab)):
                            sp.dma_start(tab[bass.ds(t * P, P), :], rowb[:, b, k, :]).then_inc(s_pst[b], 16)
                for b in range(2):
                    sp.wait_ge(s_pst[b], 32 * (NG * USES[b] + 1))
            return {"loads": loads, "consume": consume, "steps": 3, "rows": rows}

        norm_phase("proj", 2 * F, None, proj)

        s_row = [sem(f"rows_landed{b}") for b in range(NB)]
        s_free, s_idx = sem("rows_free"), sem("gather_index_ready")
        s_z, s_relu, s_d, s_exp = sem("z_ready"), sem("relu_ready"), sem("exponents_ready"), sem("exp_ready")
        s_st, s_stored = sem("state_ready"), [sem("state_stored0"), sem("state_stored1")]
        s_neutral, s_num = sem("neutral_ready"), sem("numerator_step")
        TRIPS = CH // NB
        soft_rows = soft_tab[0:P * EP, :].rearrange("(p e) f -> p e f", p=P)
        last_state = sb("last_state", [P, SW])
        neutral = sb("neutral", [1, SW])
        with ExitStack() as c:
            xl = sb("xl", [P, NB, T, XW], c=c)
            xr = sb("xr", [P, NB, T, XW], c=c)
            z = sb("z", [P, 3, T * F], c=c)
            lin, logit = sb("lin", [P, T, H], c=c), sb("logit", [P, 2, T, H], c=c)
            lg = sb("lg", [P, H, T], c=c)
            mx = sb("mx", [P, 2, H, T + 1], c=c)
            ex_in, ex_out = sb("ex_in", [P, 2, 2, H, T], c=c), sb("ex_out", [P, 2, 2, H, T], c=c)
            state = sb("state", [P, 2, T, SW], c=c)
            si, di = sb("si", [P, NB, T], I32, c=c), sb("di", [P, NB, T], I32, c=c)
            block = c.enter_context(nc.Block())

            @block.gpsimd
            def _(pool):
                nc.gpsimd.memset(neutral[0:1, 0:F + H], 0.0).then_inc(s_neutral, 1)
                nc.gpsimd.memset(neutral[0:1, F + H:SW], NEG).then_inc(s_neutral, 1)
                with pool.Fori(0, TRIPS) as i:
                    for b in range(NB):
                        pool.wait_ge(s_free, i * NB + b + 1)
                        alone(pool)
                        e0 = (i * NB + b) * T
                        nc.gpsimd.tensor_copy(si[:, b, :], src_i[:, bass.ds(e0, T)]).then_inc(s_idx, 1)
                        nc.gpsimd.tensor_copy(di[:, b, :], dst_i[:, bass.ds(e0, T)]).then_inc(s_idx, 1)
                        pool.wait_ge(s_idx, 2 * (i * NB + b + 1))
                        alone(pool)
                        for t in range(T):
                            for buf, ix, tab in ((xl, si, xl_tab), (xr, di, xr_tab)):
                                pool.indirect_dma_start(buf[:, b, t, :], None, tab,
                                                        bass.IndirectOffsetOnAxis(ix[:, b, t:t + 1], 0)).then_inc(s_row[b], 16)

            @block.scalar
            def _(act):
                with act.Fori(0, TRIPS) as i:
                    def relu(k):
                        act.wait_ge(s_z, i * NB + k + 1)
                        nc.scalar.activation(z[:, k % 3, :], z[:, k % 3, :], ACT.Relu, scale=1.0 - SLOPE).then_inc(s_relu, 1)
                    relu(0)
                    for k in range(NB):
                        if k + 1 < NB:
                            relu(k + 1)
                        act.wait_ge(s_d, i * NB + k + 1)
                        nc.scalar.activation(ex_out[:, k % 2], ex_in[:, k % 2], ACT.Exp).then_inc(s_exp, 1)

            @block.sync
            def _(sp):
                sp.wait_ge(s_neutral, 2)
                sp.dma_start(soft_tab[P * EP:P * EP + 1, :], neutral[0:1, :]).then_inc(s_stored[0], 16)
                sp.dma_start(soft_carry[P:P + 1, :], neutral[0:1, :]).then_inc(s_stored[1], 16)
                with sp.Fori(0, TRIPS) as i:
                    for k in range(NB):
                        sp.wait_ge(s_st, i * NB + k + 1)
                        sp.dma_start(soft_rows[:, bass.ds((i * NB + k) * T, T), :], state[:, k % 2, :, :]).then_inc(s_stored[k % 2], 16)
                for b in range(2):
                    sp.wait_ge(s_stored[b], 16 * (CH // 2 + 1))

            @block.vector
            def _(dve):
                v = chain(dve, c_v, "v")
                v(nc.vector.memset(state[:, 1, T - 1, 0:F + H], 0.0))
                v(nc.vector.memset(state[:, 1, T - 1, F + H:SW], NEG))
                v(nc.vector.memset(mx[:, 1, :, T:T + 1], NEG))
                v.wait()
                dve.sem_inc(s_free, NB)
                with dve.Fori(0, TRIPS) as i:
                    v.enter(i, NB * 16)
                    def add(k):
                        dve.wait_ge(s_row[k], 32 * T * (i + 1))
                        v.wait()
                        nc.vector.tensor_tensor(z[:, k % 3, :].rearrange("p (t f) -> p t f", t=T), xl[:, k, :, 0:F],
                                                xr[:, k, :, 0:F], ALU.add).then_inc(s_z, 1)
                    def logits(k):
                        zk = z[:, k % 3, :].rearrange("p (t f) -> p t f", t=T)
                        v(nc.vector.tensor_tensor(lin[:, :, :], xl[:, k, :, F:XW], xr[:, k, :, F:XW], ALU.add))
                        v(nc.vector.tensor_copy(mx[:, k % 2, :, 0:1], mx[:, (k + 1) % 2, :, T:T + 1]))
                        dve.wait_ge(s_relu, i * NB + k + 1)
                        v(nc.vector.tensor_tensor(zk, zk, att_b[:, :].unsqueeze(1).broadcast_to([P, T, F]), ALU.mult))
                        v.wait()
                        v(nc.vector.tensor_reduce(logit[:, 0, :, :], zk.rearrange("p t (h c) -> p t h c", h=H), AX.X, ALU.add))
                        v.wait()
                        v(nc.vector.tensor_tensor(lg[:, :, :], logit[:, 0, :, :].rearrange("p t h -> p h t"),
                                                  lin[:, :, :].rearrange("p t h -> p h t"), ALU.add))
                        v.wait()
                        pk = pen[:, bass.ds((i * NB + k) * T, T)]
                        for h in range(H):
                            v(nc.vector.tensor_tensor_scan(mx[:, k % 2, h, 1:T + 1], pk, lg[:, h, :],
                                                           mx[:, k % 2, h, 0:1], ALU.add, ALU.max))
                        v.wait()
                        m0, m1 = mx[:, k % 2, :, 0:T], mx[:, k % 2, :, 1:T + 1]
                        v(nc.vector.tensor_tensor(ex_in[:, k % 2, 0], lg[:, :, :], m1, ALU.subtract))
                        v(nc.vector.tensor_tensor(ex_in[:, k % 2, 1], m0, m1, ALU.subtract))
                        v.wait()
                        nc.vector.tensor_tensor(ex_in[:, k % 2, 1], ex_in[:, k % 2, 1],
                                                pk.unsqueeze(1).broadcast_to([P, H, T]), ALU.add).then_inc(s_d, 1)
                    def sums(k):
                        new, old = state[:, k % 2], state[:, (k + 1) % 2]
                        ea, ec = ex_out[:, k % 2, 0], ex_out[:, k % 2, 1]
                        pr = z[:, k % 3, :].rearrange("p (t h c) -> p t h c", t=T, h=H)
                        dve.wait_ge(s_exp, i * NB + k + 1)
                        nc.vector.tensor_tensor(pr, xl[:, k, :, 0:F].rearrange("p t (h c) -> p t h c", h=H),
                                                ea.rearrange("p h t -> p t h").unsqueeze(3).broadcast_to([P, T, H, C]),
                                                ALU.mult).then_inc(s_free, 1)
                        dve.wait_ge(s_stored[k % 2], 16 * (i * (NB // 2) + k // 2 + 1))
                        for h in range(H):
                            v(nc.vector.tensor_tensor_scan(new[:, :, F + h], ec[:, h, :], ea[:, h, :],
                                                           old[:, T - 1, F + h:F + h + 1], ALU.mult, ALU.add))
                        v(nc.vector.tensor_copy(new[:, :, F + H:SW], mx[:, k % 2, :, 1:T + 1].rearrange("p h t -> p t h")))
                        dve.wait_ge(s_free, i * NB + k + 1 + NB)
                        for t in range(T):
                            prev = old[:, T - 1] if t == 0 else new[:, t - 1]
                            for h in range(H):
                                n = (i * NB + k) * (T * H) + t * H + h
                                if t or k:
                                    dve.wait_ge(s_num, n - 3)
                                hs = slice(h * C, (h + 1) * C)
                                nc.vector.scalar_tensor_tensor(out=new[:, t, hs], in0=prev[:, hs], scalar=ec[:, h, t:t + 1],
                                                               in1=pr[:, t, h, :], op0=ALU.mult, op1=ALU.add).then_inc(s_num, 1)
                        dve.wait_ge(s_num, (i * NB + k + 1) * T * H)
                        v.wait()
                        dve.sem_inc(s_st, 1)
                    add(0)
                    for k in range(NB):
                        if k + 1 < NB:
                            add(k + 1)
                        logits(k)
                        if k >= 1:
                            sums(k - 1)
                    sums(NB - 1)
                    v.leave(TRIPS)
                v.wait()
                v(nc.vector.tensor_copy(last_state[:, :], state[:, 1, T - 1, :]))
                v.wait()
                total["v"] = v.base + v.n

        s_cst = sem("carry_step")
        with ExitStack() as c:
            tri = sb("tri", [P, P], c=c)
            same, cpen = sb("same", [P, P], c=c), sb("cpen", [P, P], c=c)
            mrow, wrow = sb("mrow", [P, H, P], c=c), sb("wrow", [P, H, P], c=c)
            wq = sb("wq", [P, H, P], c=c)
            cmax = sb("cmax", [P, H], c=c)
            crow = sb("crow", [P, SW], c=c)
            mp, tp, op = (ps(n, [P, 512], c) for n in ("mp", "tp", "op"))
            block = c.enter_context(nc.Block())

            @block.gpsimd
            def _(pool):
                nc.gpsimd.affine_select(out=tri[:, :], in_=ones[:, :], compare_op=ALU.is_ge, fill=0.0,
                                        base=0, pattern=[[-1, P]], channel_multiplier=1).then_inc(s_cst, 1)

            @block.tensor
            def _(pe):
                pe.wait_ge(s_cst, 1)
                for h in range(H):
                    m = nc.tensor.matmul(mp[:, h * P:(h + 1) * P], last_state[:, F + H + h:F + H + h + 1].broadcast_to([P, P]),
                                         ident[:, :], start=True, stop=True)
                m.then_inc(s_cst, 1)
                pe.wait_ge(s_cst, 4)
                for h in range(H):
                    m = nc.tensor.transpose(tp[:, h * P:(h + 1) * P], wrow[:, h, :], ident[:, :])
                m.then_inc(s_cst, 1)
                pe.wait_ge(s_cst, 6)
                for h in range(H):
                    nc.tensor.matmul(op[:, h * C:(h + 1) * C], wq[:, h, :], last_state[:, h * C:(h + 1) * C],
                                     start=True, stop=True)
                    m = nc.tensor.matmul(op[:, F + h:F + h + 1], wq[:, h, :], last_state[:, F + h:F + h + 1],
                                         start=True, stop=True)
                m.then_inc(s_cst, 1)

            @block.vector
            def _(dve):
                v = chain(dve, c_v, "v")
                dve.wait_ge(s_cst, 2)
                v(nc.vector.tensor_scalar(same[:, :], dl_row[:, :], dl_col[:, 0:1], None, ALU.is_equal))
                v.wait()
                v(nc.vector.tensor_tensor(same[:, :], same[:, :], tri[:, :], ALU.mult))
                v.wait()
                v(nc.vector.tensor_scalar(cpen[:, :], same[:, :], 1.0, -NEG, ALU.subtract, ALU.mult))
                v.wait()
                v(nc.vector.tensor_tensor(mrow[:, :, :], mp[:, :].rearrange("p (h q) -> p h q", h=H),
                                          cpen[:, :].unsqueeze(1).broadcast_to([P, H, P]), ALU.add))
                v.wait()
                v(nc.vector.tensor_reduce(cmax[:, :], mrow[:, :, :], AX.X, ALU.max))
                v.wait()
                nc.vector.tensor_tensor(mrow[:, :, :], mrow[:, :, :], cmax[:, :].unsqueeze(2).broadcast_to([P, H, P]),
                                        ALU.subtract).then_inc(s_cst, 1)
                dve.wait_ge(s_cst, 5)
                nc.vector.tensor_copy(wq[:, :, :], tp[:, :].rearrange("p (h q) -> p h q", h=H)).then_inc(s_cst, 1)
                dve.wait_ge(s_cst, 7)
                v(nc.vector.tensor_copy(crow[:, 0:F + H], op[:, 0:F + H]))
                nc.vector.tensor_copy(crow[:, F + H:SW], cmax[:, :]).then_inc(s_cst, 1)
                v.wait()
                total["v"] = v.n

            @block.scalar
            def _(act):
                act.wait_ge(s_cst, 3)
                nc.scalar.activation(wrow[:, :, :], mrow[:, :, :], ACT.Exp).then_inc(s_cst, 1)

            @block.sync
            def _(sp):
                sp.wait_ge(s_cst, 8)
                sp.wait_ge(c_v, total["v"])
                store(sp, soft_carry[0:P, :], crow[:, :])
                sp.wait_ge(stored, total["stored"])

        def group_loop(eng, trip):
            with eng.Fori(0, NG // 2) as i:
                trip(i * 2, 0)
                trip(i * 2 + 1, 1)
            assert NG % 2 == 1
            trip(NG - 1, 0)

        own_l = xl_tab.rearrange("(t p) f -> p t f", p=P)
        own_r = xr_tab.rearrange("(t p) f -> p t f", p=P)
        s_own = [sem("own_rows_landed0"), sem("own_rows_landed1")]
        s_seg = [sem("segment_rows_landed0"), sem("segment_rows_landed1")]
        s_sidx, s_mfree = sem("segment_index_ready"), sem("merge_buffer_free")
        s_mexp_in, s_mexp = sem("merge_exponents_ready"), sem("merge_exp_ready")
        with ExitStack() as c:
            ol, orr = sb("ol", [P, 2, TU, XW], c=c), sb("orr", [P, 2, TU, XW], c=c)
            ge, gc = sb("ge", [P, 2, TU, SW], c=c), sb("gc", [P, 2, TU, SW], c=c)
            ie, ic = sb("ie", [P, 2, TU], I32, c=c), sb("ic", [P, 2, TU], I32, c=c)
            bias = sb("gat_bias", [P, F], c=c)
            self_l, mtop, den = (sb(n, [P, TU, H], c=c) for n in ("self_l", "mtop", "den"))
            wexp = sb("wexp", [P, 3, TU, H], c=c)
            block = c.enter_context(nc.Block())

            @block.sync
            def _(sp):
                load(sp, bias[:, :], row(a["L0_gnn_bias"], F))
                def trip(g, b):
                    sp.wait_ge(s_mfree, g + 1)
                    for buf, tab in ((ol, own_l), (orr, own_r)):
                        sp.dma_start(buf[:, b, :, :], tab[:, bass.ds(g * TU, TU), :]).then_inc(s_own[b], 16)
                group_loop(sp, trip)

            @block.gpsimd
            def _(pool):
                def trip(g, b):
                    pool.wait_ge(s_mfree, g + 1)
                    alone(pool)
                    nc.gpsimd.tensor_copy(ie[:, b, :], idx_end[:, bass.ds(g * TU, TU)]).then_inc(s_sidx, 1)
                    nc.gpsimd.tensor_copy(ic[:, b, :], idx_carry[:, bass.ds(g * TU, TU)]).then_inc(s_sidx, 1)
                    pool.wait_ge(s_sidx, 2 * (g + 1))
                    alone(pool)
                    for j in range(TU):
                        for buf, ix, tab in ((ge, ie, soft_tab), (gc, ic, soft_carry)):
                            pool.indirect_dma_start(buf[:, b, j, :], None, tab,
                                                    bass.IndirectOffsetOnAxis(ix[:, b, j:j + 1], 0)).then_inc(s_seg[b], 16)
                group_loop(pool, trip)

            @block.scalar
            def _(act):
                def trip(g, b):
                    act.wait_ge(s_mexp_in, g + 1)
                    nc.scalar.activation(wexp[:, :, :, :], wexp[:, :, :, :], ACT.Exp).then_inc(s_mexp, 1)
                group_loop(act, trip)

            @block.vector
            def _(dve):
                v = chain(dve, c_v, "v")
                dve.wait_ge(loaded, total["loaded"])
                dve.sem_inc(s_mfree, 2)
                K = 22
                before = v.n
                def trip(g, b):
                    v.base, v.n = before + g * K, 0
                    fr, num = slice(0, F), lambda x: x[:, b, :, 0:F].rearrange("p t (h c) -> p t h c", h=H)
                    def step(ins):
                        v(ins)
                        v.wait()
                    dve.wait_ge(s_own[b], 16 * (g - b + 2))
                    v.wait()
                    step(nc.vector.tensor_tensor(orr[:, b], orr[:, b], ol[:, b], ALU.add))
                    step(nc.vector.tensor_scalar(orr[:, b, :, fr], orr[:, b, :, fr], 0.0, 1.0 - SLOPE, ALU.max, ALU.mult))
                    step(nc.vector.tensor_tensor(orr[:, b, :, fr], orr[:, b, :, fr],
                                                 att_b[:, :].unsqueeze(1).broadcast_to([P, TU, F]), ALU.mult))
                    step(nc.vector.tensor_reduce(self_l[:, :, :], num(orr), AX.X, ALU.add))
                    step(nc.vector.tensor_tensor(self_l[:, :, :], self_l[:, :, :], orr[:, b, :, F:XW], ALU.add))
                    dve.wait_ge(s_seg[b], 16 * TU * (g - b + 2))
                    me, mc = ge[:, b, :, F + H:SW], gc[:, b, :, F + H:SW]
                    step(nc.vector.tensor_tensor(mtop[:, :, :], me, mc, ALU.max))
                    step(nc.vector.tensor_tensor(mtop[:, :, :], mtop[:, :, :], self_l[:, :, :], ALU.max))
                    v(nc.vector.tensor_tensor(wexp[:, 0], me, mtop[:, :, :], ALU.subtract))
                    v(nc.vector.tensor_tensor(wexp[:, 1], mc, mtop[:, :, :], ALU.subtract))
                    v.wait()
                    nc.vector.tensor_tensor(wexp[:, 2], self_l[:, :, :], mtop[:, :, :], ALU.subtract).then_inc(s_mexp_in, 1)
                    dve.wait_ge(s_mexp, g + 1)
                    de, dc = ge[:, b, :, F:F + H], gc[:, b, :, F:F + H]
                    v(nc.vector.tensor_tensor(de, de, wexp[:, 0], ALU.mult))
                    step(nc.vector.tensor_tensor(dc, dc, wexp[:, 1], ALU.mult))
                    step(nc.vector.tensor_tensor(den[:, :, :], de, dc, ALU.add))
                    step(nc.vector.tensor_tensor(den[:, :, :], den[:, :, :], wexp[:, 2], ALU.add))
                    step(nc.vector.reciprocal(den[:, :, :], den[:, :, :]))
                    step(nc.vector.tensor_tensor(wexp[:, :, :, :], wexp[:, :, :, :],
                                                 den[:, :, :].unsqueeze(1).broadcast_to([P, 3, TU, H]), ALU.mult))
                    for k, x in enumerate((ge, gc, ol)):
                        v(nc.vector.tensor_tensor(num(x), num(x), wexp[:, k].unsqueeze(3).broadcast_to([P, TU, H, C]), ALU.mult))
                    xg = X[:, bass.ds(g * TU, TU), :]
                    step(nc.vector.tensor_tensor(xg, xg, bias[:, :].unsqueeze(1).broadcast_to([P, TU, F]), ALU.add))
                    step(nc.vector.tensor_tensor(ge[:, b, :, fr], ge[:, b, :, fr], gc[:, b, :, fr], ALU.add))
                    step(nc.vector.tensor_tensor(ge[:, b, :, fr], ge[:, b, :, fr], ol[:, b, :, fr], ALU.add))
                    step(nc.vector.tensor_tensor(xg, xg, ge[:, b, :, fr], ALU.add))
                    dve.sem_inc(s_mfree, 1)
                    assert v.n == K, v.n
                group_loop(dve, trip)
                total["v"] = before + NG * K

        XT = sb("XT", [P, KF, NP])
        gate = sb("gate", [P, NT, 8])

        def gated(name, ne, w_in, bias_in):
            def build(c, w, bank):
                gb = sb(f"{name}_gb", [P, 8], c=c)

                def loads(sp):
                    load(sp, w[:, :, :], w_in.rearrange("(k p) n -> p k n", p=P))
                    if bias_in is not None:
                        load(sp, gb[:, 0:ne], row(bias_in, ne))

                def consume(v, dve, mm, g, j, s_use):
                    t = bass.ds(g * TU + j, 1)
                    m = mm[:, 0:ne].unsqueeze(1)
                    if bias_in is not None:
                        if j == 0:
                            dve.wait_ge(loaded, total["loaded"])
                        nc.vector.tensor_tensor(gate[:, t, 0:ne], m, gb[:, 0:ne].unsqueeze(1), ALU.add).then_inc(s_use, 1)
                    else:
                        nc.vector.tensor_scalar(gate[:, t, 0:ne], m, 1.0, None, ALU.mult).then_inc(s_use, 1)

                def last(v, dve):
                    done(dve, s_gate_of[0], NT)
                return {"loads": loads, "consume": consume, "steps": 0, "last": last}
            s_gate_of = [None]

            def with_use(c, w, bank):
                ex = build(c, w, bank)
                inner = ex["consume"]

                def consume(v, dve, mm, g, j, s_use):
                    s_gate_of[0] = s_use
                    inner(v, dve, mm, g, j, s_use)
                ex["consume"] = consume
                return ex
            norm_phase(name, ne, XT, with_use)

        def route_phase(name, ne, soft_top, out_bias):
            s_ex, s_exd = sem(f"{name}_exponents_ready"), sem(f"{name}_exp_ready")
            s_tp, s_wt, s_bm, s_bu = (sem(f"{name}_{n}") for n in ("weights_transposed", "weightsT_ready", "bias_product", "bias_used"))
            s_z = sem(f"{name}_bias_zeroed")
            nr = ne + 1
            with ExitStack() as c:
                G = lambda n: sb(f"{name}_{n}", [P, NT, ne], c=c)
                pr, eq, s1, s2 = G("pr"), G("eq"), G("s1"), G("s2")
                R = lambda n: sb(f"{name}_{n}", [P, NT], c=c)
                r0, v1, v2, kk = R("r0"), R("v1"), R("v2"), R("kk")
                rank = sb(f"{name}_rank", [P, ne], c=c)
                wx = sb(f"{name}_wx", [P, NT, nr], c=c)
                stage_w = sb(f"{name}_stage", [P, 2, TU * nr], c=c)
                wts = sb(f"{name}_wts", [TU * nr, 2, P], c=c)
                bd = sb(f"{name}_bd", [TU * nr, TU, F], c=c)
                tp = ps(f"{name}_tp", [P, 512], c)
                bp = ps(f"{name}_bp", [P, TU, F], c)
                block = c.enter_context(nc.Block())

                @block.gpsimd
                def _(pool):
                    nc.gpsimd.memset(bd[:, :, :], 0.0).then_inc(s_z, 1)
                    nc.gpsimd.iota(rank[:, :], [[-1, ne]], base=ne, channel_multiplier=0,
                                   allow_small_or_imprecise_dtypes=True).then_inc(s_z, 1)

                @block.sync
                def _(sp):
                    sp.wait_ge(s_z, 2)
                    for j in range(TU):
                        eb, shared = out_bias
                        load(sp, bd[j * nr:j * nr + ne, j, :], eb)
                        load(sp, bd[j * nr + ne:(j + 1) * nr, j, :], shared.rearrange("(a n) -> a n", a=1))

                @block.vector
                def _(dve):
                    v = chain(dve, c_v, "v")
                    def step(ins):
                        v(ins)
                        v.wait()
                    g = gate[:, :, 0:ne]
                    wide = lambda x: x[:, :].unsqueeze(2).broadcast_to([P, NT, ne])
                    step(nc.vector.tensor_reduce(r0[:, :], g, AX.X, ALU.max))
                    nc.vector.tensor_tensor(pr[:, :, :], g, wide(r0), ALU.subtract).then_inc(s_ex, 1)
                    dve.wait_ge(s_exd, 1)
                    step(nc.vector.tensor_reduce(r0[:, :], pr[:, :, :], AX.X, ALU.add))
                    step(nc.vector.reciprocal(r0[:, :], r0[:, :]))
                    step(nc.vector.tensor_tensor(pr[:, :, :], pr[:, :, :], wide(r0), ALU.mult))
                    dve.wait_ge(s_z, 2)
                    rk = rank[:, :].unsqueeze(1).broadcast_to([P, NT, ne])
                    for val, sel in ((v1, s1), (v2, s2)):
                        step(nc.vector.tensor_reduce(val[:, :], pr[:, :, :], AX.X, ALU.max))
                        step(nc.vector.tensor_tensor(eq[:, :, :], pr[:, :, :], wide(val), ALU.is_equal))
                        step(nc.vector.tensor_tensor(eq[:, :, :], eq[:, :, :], rk, ALU.mult))
                        step(nc.vector.tensor_reduce(kk[:, :], eq[:, :, :], AX.X, ALU.max))
                        step(nc.vector.tensor_tensor(sel[:, :, :], rk, wide(kk), ALU.is_equal))
                        step(nc.vector.scalar_tensor_tensor(out=pr[:, :, :], in0=sel[:, :, :], scalar=-2.0, in1=pr[:, :, :],
                                                            op0=ALU.mult, op1=ALU.add))
                    if soft_top:
                        nc.vector.tensor_tensor(v2[:, :], v2[:, :], v1[:, :], ALU.subtract).then_inc(s_ex, 1)
                        dve.wait_ge(s_exd, 2)
                        step(nc.vector.memset(v1[:, :], 1.0))
                    step(nc.vector.tensor_tensor(r0[:, :], v1[:, :], v2[:, :], ALU.add))
                    step(nc.vector.reciprocal(r0[:, :], r0[:, :]))
                    step(nc.vector.tensor_tensor(s1[:, :, :], s1[:, :, :], wide(v1), ALU.mult))
                    step(nc.vector.tensor_tensor(s2[:, :, :], s2[:, :, :], wide(v2), ALU.mult))
                    step(nc.vector.tensor_tensor(s1[:, :, :], s1[:, :, :], s2[:, :, :], ALU.add))
                    step(nc.vector.tensor_tensor(g, s1[:, :, :], wide(r0), ALU.mult))
                    step(nc.vector.tensor_copy(wx[:, :, 0:ne], g))
                    step(nc.vector.memset(wx[:, :, ne:nr], 1.0))
                    before, K = v.n, 2
                    prime(dve, s_bu)
                    def trip(k, b):
                        v.base, v.n = before + k * K, 0
                        v(nc.vector.tensor_scalar(stage_w[:, b, :].rearrange("p (t e) -> p t e", t=TU),
                                                  wx[:, bass.ds(k * TU, TU), :], 1.0, None, ALU.mult))
                        dve.wait_ge(s_bm, k + 1)
                        xg = X[:, bass.ds(k * TU, TU), :]
                        v(nc.vector.tensor_tensor(xg, xg, bp[:, :, :], ALU.add))
                        dve.sem_inc(s_bu, 1)
                    group_loop(dve, trip)
                    total["v_before_bias"], total["v"] = before, before + NG * K

                @block.scalar
                def _(act):
                    act.wait_ge(s_ex, 1)
                    nc.scalar.activation(pr[:, :, :], pr[:, :, :], ACT.Exp).then_inc(s_exd, 1)
                    if soft_top:
                        act.wait_ge(s_ex, 2)
                        nc.scalar.activation(v2[:, :], v2[:, :], ACT.Exp).then_inc(s_exd, 1)
                    def trip(k, b):
                        act.wait_ge(s_tp, k + 1)
                        nc.scalar.activation(wts[:, b, :], tp[0:TU * nr, 0:P], ACT.Copy).then_inc(s_wt, 1)
                    group_loop(act, trip)

                @block.tensor
                def _(pe):
                    pe.wait_ge(loaded, total["loaded"])
                    def trip(k, b):
                        pe.wait_ge(c_v, total["v_before_bias"] + k * 2 + 1)
                        alone(pe)
                        nc.tensor.transpose(tp[0:TU * nr, 0:P], stage_w[:, b, :], ident[:, :]).then_inc(s_tp, 1)
                        pe.wait_ge(s_wt, k + 1)
                        done(pe, s_bu, k)
                        for j in range(TU):
                            m = nc.tensor.matmul(bp[:, j, :], wts[:, b, :], bd[:, j, :], start=True, stop=True)
                        m.then_inc(s_bm, 1)
                    group_loop(pe, trip)

        gated("gate0", 4, a["L0_ffn_gW"], a["L0_ffn_gb"])
        route_phase("route0", 4, True, (a["L0_ffn_eb3"], a["L0_ffn_sb3"]))

        s_a, s_ar, s_b, s_br, s_c, s_cu = (sem(n) for n in ("hidden1_product", "hidden1_ready", "hidden2_product",
                                                            "hidden2_ready", "output_product", "output_used"))
        s_bt = sem("ffn0_bias_step")
        with ExitStack() as c:
            NETS = [(2, P)] + [(1, 64)] * 4
            w1 = [sb(f"f0w1_{n}", [P, KF, ch * P], c=c) for n, (ch, _) in enumerate(NETS)]
            w2 = [sb(f"f0w2_{n}", [P, ch, h2], c=c) for n, (ch, h2) in enumerate(NETS)]
            w3 = [sb(f"f0w3_{n}", [h2, F], c=c) for n, (_, h2) in enumerate(NETS)]
            NB1 = 2 + 4 + 1 + 4
            brow, bcol = sb("f0brow", [NB1, P], c=c), sb("f0bcol", [P, NB1], c=c)
            h1 = sb("f0h1", [P, 2, 4, GW], c=c)
            h2 = sb("f0h2", [P, 2, 2 * GW], c=c)
            ap_ = [ps(f"f0a{b}", [P, 512], c) for b in range(2)]
            bp_ = [ps(f"f0b{b}", [P, 512], c) for b in range(2)]
            yp = ps("f0y", [P, TU, F], c)
            block = c.enter_context(nc.Block())
            A = [(n, hf, ch) for n, (chs, _) in enumerate(NETS) for hf in range(2) for ch in range(chs)]
            NA_, NB_, NC_ = len(A), 2 * len(NETS), len(NETS)
            first_a = {n: min(i for i, u in enumerate(A) if u[0] == n) for n in range(NC_)}
            last_a = {n: max(i for i, u in enumerate(A) if u[0] == n) for n in range(NC_)}
            ORDER = ["A0", "A1", "B0", "A2", "B1", "C0", "A3", "B2", "C1", "A4", "B3", "C2", "B4", "C3", "C4"]
            evac = [u for u in ORDER if u[0] in "AB"]

            @block.sync
            def _(sp):
                load(sp, w1[0][:, :, :], a["L0_ffn_sW1"].rearrange("(k p) n -> p k n", p=P))
                load(sp, w2[0][:, :, :], a["L0_ffn_sW2"].rearrange("(k p) n -> p k n", p=P))
                load(sp, w3[0][:, :], a["L0_ffn_sW3"])
                for n in range(4):
                    load(sp, w1[n + 1][:, :, :], a["L0_ffn_eW1"][n].rearrange("(k p) n -> p k n", p=P))
                    load(sp, w2[n + 1][:, 0, :], a["L0_ffn_eW2"][n])
                    load(sp, w3[n + 1][:, :], a["L0_ffn_eW3"][n])
                sp.wait_ge(s_bt, 1)
                load(sp, brow[0:2, :], a["L0_ffn_sb1"].rearrange("(a n) -> a n", a=2))
                load(sp, brow[2:6, :], a["L0_ffn_eb1"])
                load(sp, brow[6:7, :], a["L0_ffn_sb2"].rearrange("(a n) -> a n", a=1))
                load(sp, brow[7:11, 0:64], a["L0_ffn_eb2"])

            @block.gpsimd
            def _(pool):
                nc.gpsimd.memset(brow[:, :], 0.0).then_inc(s_bt, 1)

            @block.tensor
            def _(pe):
                pe.wait_ge(loaded, total["loaded"])
                nc.tensor.transpose(ap_[0][:, 0:NB1], brow[:, :], ident[0:NB1, 0:NB1]).then_inc(s_bt, 1)
                pe.wait_ge(s_bt, 3)
                prime(pe, s_a, s_b, s_c)
                with pe.Fori(0, NG) as g:
                    for u in ORDER:
                        n = int(u[1])
                        chs, wd = NETS[n]
                        if u[0] == "A":
                            for q in range(first_a[n], last_a[n] + 1):
                                _, hf, ch = A[q]
                                done(pe, s_ar, g * NA_ + q - 1 if q else g * NA_)
                                for k in range(KF):
                                    m = nc.tensor.matmul(ap_[q % 2][:, 0:GW], w1[n][:, k, ch * P:(ch + 1) * P],
                                                         XT[:, k, bass.ds(g * (2 * GW) + hf * GW, GW)],
                                                         start=(k == 0), stop=(k == KF - 1))
                                m.then_inc(s_a, 1)
                        elif u[0] == "B":
                            for hf in range(2):
                                q = 2 * n + hf
                                done(pe, s_ar, g * NA_ + first_a[n] + (hf + 1) * chs)
                                done(pe, s_br, g * NB_ + q - 1 if q else g * NB_)
                                for ch in range(chs):
                                    m = nc.tensor.matmul(bp_[hf][0:wd, 0:GW], w2[n][:, ch, :], h1[:, n % 2, hf * chs + ch, :],
                                                         start=(ch == 0), stop=(ch == chs - 1))
                                m.then_inc(s_b, 1)
                        else:
                            done(pe, s_br, g * NB_ + 2 * n + 2)
                            done(pe, s_cu, g * NC_ + n)
                            for j in range(TU):
                                m = nc.tensor.matmul(yp[:, j, :], h2[0:wd, n % 2, j * P:(j + 1) * P], w3[n][:, :],
                                                     start=True, stop=True)
                            m.then_inc(s_c, 1)

            @block.scalar
            def _(act):
                act.wait_ge(s_bt, 2)
                nc.scalar.activation(bcol[:, :], ap_[0][:, 0:NB1], ACT.Copy).then_inc(s_bt, 1)
                act.wait_ge(s_bt, 3)
                prime(act, s_ar, s_br)
                with act.Fori(0, NG) as g:
                    for u in evac:
                        n = int(u[1])
                        chs, wd = NETS[n]
                        if u[0] == "A":
                            for q in range(first_a[n], last_a[n] + 1):
                                _, hf, ch = A[q]
                                done(act, s_a, g * NA_ + q + 1)
                                done(act, s_b, g * NB_ + 2 * (n - 1) if n >= 2 else g * NB_)
                                bi = ch if n == 0 else 1 + n
                                nc.scalar.activation(h1[:, n % 2, hf * chs + ch, :], ap_[q % 2][:, 0:GW], ACT.Relu,
                                                     bias=bcol[:, bi:bi + 1]).then_inc(s_ar, 1)
                        else:
                            for hf in range(2):
                                done(act, s_b, g * NB_ + 2 * n + hf + 1)
                                done(act, s_c, g * NC_ + n - 1 if n >= 2 else g * NC_)
                                bi = 6 + n
                                nc.scalar.activation(h2[0:wd, n % 2, hf * GW:(hf + 1) * GW], bp_[hf][0:wd, 0:GW], ACT.Relu,
                                                     bias=bcol[0:wd, bi:bi + 1]).then_inc(s_br, 1)

            @block.vector
            def _(dve):
                v = chain(dve, c_v, "v")
                prime(dve, s_cu)
                with dve.Fori(0, NG) as g:
                    v.enter(g, NC_ * TU)
                    for n in range(NC_):
                        done(dve, s_c, g * NC_ + n + 1)
                        if n:
                            v.wait()
                        for j in range(TU):
                            xt = X[:, bass.ds(g * TU + j, 1), :]
                            y = yp[:, j:j + 1, :]
                            if n == 0:
                                v(nc.vector.tensor_tensor(xt, xt, y, ALU.add))
                            else:
                                v(nc.vector.scalar_tensor_tensor(out=xt, in0=y,
                                                                 scalar=gate[:, bass.ds(g * TU + j, 1), n - 1:n].rearrange("p a b -> p (a b)"),
                                                                 in1=xt, op0=ALU.mult, op1=ALU.add))
                        v.wait()
                        dve.sem_inc(s_cu, 1)
                    v.leave(NG)
                total["v"] = v.base + v.n

        s_xst = [sem("xp_stored0"), sem("xp_stored1")]
        s_pw = sem("proj_weight_step")

        def xp_phase(c, w, bank):
            wn = sb("wproj_rows", [P, KF, F], c=c)
            bias, rowb = sb("xp_bias", [P, F], c=c), sb("xp_row", [P, 2, F], c=c)

            def loads(sp):
                load(sp, wn[:, :, :], a["L1_gnn_W_proj"].rearrange("(o p) i -> p o i", p=P))
                for b in range(2):
                    sp.dma_start(bias[:, b * P:(b + 1) * P], row(a["L1_gnn_b_proj"][b * P:(b + 1) * P], P)).then_inc(s_xst[b], 16)

            def pe_(pe):
                for k in range(KF):
                    for o in range(KF):
                        m = nc.tensor.transpose(bank[:, (k * KF + o) * P:(k * KF + o + 1) * P],
                                                wn[:, o, k * P:(k + 1) * P], ident[:, :])
                m.then_inc(s_pw, 1)
                pe.wait_ge(s_pw, 2)

            def act_(act):
                act.wait_ge(s_pw, 1)
                nc.scalar.activation(w[:, :, :], bank[:, :].rearrange("p (k n) -> p k n", k=KF), ACT.Copy).then_inc(s_pw, 1)

            def consume(v, dve, mm, g, j, s_use):
                b = j % 2
                dve.wait_ge(s_xst[b], 16 * (g * USES[b] + j // 2 + 1))
                if j == 0:
                    dve.wait_ge(s_xst[1], 16)
                v(nc.vector.tensor_tensor(rowb[:, b, :], mm[:, 0:F], bias[:, :], ALU.add))
                v.wait()
                nc.vector.tensor_scalar(rowb[:, b, :], rowb[:, b, :], 0.0, None, ALU.max).then_inc(s_use, 1)

            def rows(sp, s_use):
                with sp.Fori(0, NG) as g:
                    for j in range(TU):
                        t, b = g * TU + j, j % 2
                        done(sp, s_use, t + 1)
                        sp.dma_start(xp_tab[bass.ds(t * P, P), :], rowb[:, b, :]).then_inc(s_xst[b], 16)
                for b in range(2):
                    sp.wait_ge(s_xst[b], 16 * (NG * USES[b] + 1))
            return {"loads": loads, "consume": consume, "steps": 1, "rows": rows, "pe": pe_, "act": act_}

        norm_phase("xp", F, XT, xp_phase)

        s_mrow = [sem(f"max_rows_landed{b}") for b in range(NB)]
        s_mst = [sem(f"max_stored{b}") for b in range(NB)]
        s_midx, s_mdone, s_mx, s_mz = (sem(n) for n in ("max_index_ready", "max_chunk_ready", "max_step", "max_neutral_ready"))
        max_rows = max_tab[0:P * EP, :].rearrange("(p e) f -> p e f", p=P)
        last_max = sb("last_max", [P, F])
        with ExitStack() as c:
            mb = sb("mb", [P, NB, T, F], c=c)
            si = sb("msi", [P, NB, T], I32, c=c)
            zero = sb("zero_row", [1, NB, F // 2], c=c)
            block = c.enter_context(nc.Block())

            @block.sync
            def _(sp):
                sp.wait_ge(s_mz, 1)
                for b in range(NB):
                    tab, r = ((max_tab, P * EP), (max_carry, P))[b // 2]
                    hb = slice((b % 2) * (F // 2), (b % 2 + 1) * (F // 2))
                    sp.dma_start(tab[r:r + 1, hb], zero[0:1, b, :]).then_inc(s_mst[b], 16)
                with sp.Fori(0, TRIPS) as i:
                    for k in range(NB):
                        sp.wait_ge(s_mdone, i * NB + k + 1)
                        sp.dma_start(max_rows[:, bass.ds((i * NB + k) * T, T), :], mb[:, k, :, :]).then_inc(s_mst[k], 16)
                for b in range(NB):
                    sp.wait_ge(s_mst[b], 16 * (TRIPS + 1))

            @block.gpsimd
            def _(pool):
                nc.gpsimd.memset(zero[:, :, :], 0.0).then_inc(s_mz, 1)
                with pool.Fori(0, TRIPS) as i:
                    for b in range(NB):
                        pool.wait_ge(s_mst[b], 16 * (i + 1))
                        alone(pool)
                        nc.gpsimd.tensor_copy(si[:, b, :], src_i[:, bass.ds((i * NB + b) * T, T)]).then_inc(s_midx, 1)
                        pool.wait_ge(s_midx, i * NB + b + 1)
                        alone(pool)
                        for t in range(T):
                            pool.indirect_dma_start(mb[:, b, t, :], None, xp_tab,
                                                    bass.IndirectOffsetOnAxis(si[:, b, t:t + 1], 0)).then_inc(s_mrow[b], 16)

            @block.vector
            def _(dve):
                v = chain(dve, c_v, "v")
                v(nc.vector.memset(last_max[:, :], 0.0))
                v.wait()
                with dve.Fori(0, TRIPS) as i:
                    for k in range(NB):
                        dve.wait_ge(s_mrow[k], 16 * T * (i + 1))
                        for t in range(T):
                            n = (i * NB + k) * T + t
                            prev = mb[:, k, t - 1, :] if t else last_max[:, :]
                            if t or k:
                                dve.wait_ge(s_mx, n)
                            e = n
                            nc.vector.scalar_tensor_tensor(out=mb[:, k, t, :], in0=prev, scalar=keep[:, bass.ds(e, 1)],
                                                           in1=mb[:, k, t, :], op0=ALU.mult, op1=ALU.max).then_inc(s_mx, 1)
                        dve.wait_ge(s_mx, (i * NB + k + 1) * T)
                        nc.vector.tensor_copy(last_max[:, :], mb[:, k, T - 1, :]).then_inc(s_mdone, 1)
                        dve.wait_ge(s_mdone, i * NB + k + 1)
                v.wait()
                total["v"] = v.n

        s_mc = sem("max_carry_step")
        with ExitStack() as c:
            kc = sb("kc", [P, P], c=c)
            cm = sb("cm", [P, KF, P], c=c)
            crow = sb("mcrow", [P, F], c=c)
            ft = ps("ft", [P, 512], c)
            bk = ps("bk", [P, 512], c)
            block = c.enter_context(nc.Block())

            @block.tensor
            def _(pe):
                for k in range(KF):
                    m = nc.tensor.transpose(ft[:, k * P:(k + 1) * P], last_max[:, k * P:(k + 1) * P], ident[:, :])
                m.then_inc(s_mc, 1)
                pe.wait_ge(s_mc, 3)
                for k in range(KF):
                    m = nc.tensor.transpose(bk[:, k * P:(k + 1) * P], cm[:, k, :], ident[:, :])
                m.then_inc(s_mc, 1)

            @block.vector
            def _(dve):
                v = chain(dve, c_v, "v")
                v(nc.vector.memset(kc[:, 0:1], 0.0))
                v(nc.vector.tensor_tensor(kc[:, 1:P], dl_row[:, 1:P], dl_row[:, 0:P - 1], ALU.is_equal))
                v.wait()
                dve.wait_ge(s_mc, 1)
                for k in range(KF):
                    nc.vector.tensor_tensor_scan(cm[:, k, :], kc[:, :], ft[:, k * P:(k + 1) * P], 0.0,
                                                 ALU.mult, ALU.max).then_inc(s_mc, 1)
                dve.wait_ge(s_mc, 4)
                nc.vector.tensor_copy(crow[:, :], bk[:, 0:F]).then_inc(s_mc, 1)
                v.wait()
                total["v"] = v.n

            @block.sync
            def _(sp):
                sp.wait_ge(s_mc, 5)
                store(sp, max_carry[0:P, :], crow[:, :])
                sp.wait_ge(stored, total["stored"])

        own_x = xp_tab.rearrange("(t p) f -> p t f", p=P)
        s_ow = [sem("own_xp_landed0"), sem("own_xp_landed1")]
        s_sg = [sem("max_segment_landed0"), sem("max_segment_landed1")]
        (s_ix, s_fr, s_ag, s_at, s_as, s_lp, s_lo, s_w2, s_gfree) = (sem(n) for n in (
            "max_segment_index_ready", "aggregate_buffer_free", "aggregate_ready", "aggregate_transposed",
            "aggregateT_ready", "layer_product", "layer_out_ready", "layer_weight_step", "aggregate_transposed_group"))
        with ExitStack() as c:
            ox = sb("ox", [P, 2, TU, F], c=c)
            ge, gc = sb("mge", [P, 2, TU, F], c=c), sb("mgc", [P, 2, TU, F], c=c)
            ie, ic = sb("mie", [P, 2, TU], I32, c=c), sb("mic", [P, 2, TU], I32, c=c)
            wn = sb("wlr_rows", [P, 2, KF, F], c=c)
            wt = sb("wlr_t", [P, 2, KF, F], c=c)
            bl = sb("bl", [P, KF], c=c)
            ags = sb("ags", [P, 2, KF, P], c=c)
            tb = [ps(f"ltb{b}", [P, 512], c) for b in range(2)]
            ob = [ps(f"lob{b}", [P, 512], c) for b in range(2)]
            block = c.enter_context(nc.Block())

            @block.sync
            def _(sp):
                load(sp, wn[:, 0], a["L1_gnn_W_l"].rearrange("(o p) i -> p o i", p=P))
                load(sp, wn[:, 1], a["L1_gnn_W_r"].rearrange("(o p) i -> p o i", p=P))
                with nc.allow_non_contiguous_dma(reason="256 values"):
                    load(sp, bl[:, :], a["L1_gnn_b_l"].rearrange("(k p) -> p k", p=P))
                def trip(g, b):
                    sp.wait_ge(s_fr, g + 1)
                    sp.dma_start(ox[:, b, :, :], own_x[:, bass.ds(g * TU, TU), :]).then_inc(s_ow[b], 16)
                group_loop(sp, trip)

            @block.gpsimd
            def _(pool):
                def trip(g, b):
                    pool.wait_ge(s_fr, g + 1)
                    alone(pool)
                    nc.gpsimd.tensor_copy(ie[:, b, :], idx_end[:, bass.ds(g * TU, TU)]).then_inc(s_ix, 1)
                    nc.gpsimd.tensor_copy(ic[:, b, :], idx_carry[:, bass.ds(g * TU, TU)]).then_inc(s_ix, 1)
                    pool.wait_ge(s_ix, 2 * (g + 1))
                    alone(pool)
                    for j in range(TU):
                        for buf, ix, tab in ((ge, ie, max_tab), (gc, ic, max_carry)):
                            pool.indirect_dma_start(buf[:, b, j, :], None, tab,
                                                    bass.IndirectOffsetOnAxis(ix[:, b, j:j + 1], 0)).then_inc(s_sg[b], 16)
                group_loop(pool, trip)

            @block.vector
            def _(dve):
                v = chain(dve, c_v, "v")
                before, K = v.n, 1
                def trip(g, b):
                    v.base, v.n = before + g * K, 0
                    dve.wait_ge(s_ow[b], 8 * (g - b + 2))
                    dve.wait_ge(s_sg[b], 16 * TU * (g - b + 2))
                    v(nc.vector.tensor_tensor(ge[:, b], ge[:, b], gc[:, b], ALU.max))
                    v.wait()
                    nc.vector.tensor_tensor(ge[:, b], ge[:, b], ox[:, b], ALU.max).then_inc(s_ag, 1)
                group_loop(dve, trip)
                total["v"] = before + NG * K

            @block.tensor
            def _(pe):
                pe.wait_ge(loaded, total["loaded"])
                for s in range(2):
                    for k in range(KF):
                        for o in range(KF):
                            m = nc.tensor.transpose(tb[s][:, (k * KF + o) * P:(k * KF + o + 1) * P],
                                                    wn[:, s, o, k * P:(k + 1) * P], ident[:, :])
                m.then_inc(s_w2, 1)
                pe.wait_ge(s_w2, 3)
                pe.sem_inc(s_fr, 2)
                prime(pe, s_at, s_lp)
                def trip(g, b):
                    pe.wait_ge(s_ag, g + 1)
                    for j in range(TU):
                        t, q = g * TU + j, j % 2
                        done(pe, s_as, t - 1 if j >= 2 else g * TU)
                        for k in range(KF):
                            m = nc.tensor.transpose(tb[q][:, k * P:(k + 1) * P], ge[:, b, j, k * P:(k + 1) * P], ident[:, :])
                        m.then_inc(s_at, 1)
                        done(pe, s_as, t + 1)
                        done(pe, s_lo, t - 1 if j >= 2 else g * TU)
                        for o in range(KF):
                            for k in range(KF):
                                nc.tensor.matmul(ob[q][:, o * P:(o + 1) * P], wt[:, 0, k, o * P:(o + 1) * P], ags[:, q, k, :],
                                                 start=(k == 0), stop=False)
                            for k in range(KF):
                                m = nc.tensor.matmul(ob[q][:, o * P:(o + 1) * P], wt[:, 1, k, o * P:(o + 1) * P],
                                                     XT[:, k, bass.ds(t * P, P)], start=False, stop=(k == KF - 1))
                        m.then_inc(s_lp, 1)
                    pe.wait_ge(s_as, g * TU + TU + 1)
                    pe.sem_inc(s_fr, 1)
                group_loop(pe, trip)

            @block.scalar
            def _(act):
                act.wait_ge(s_w2, 1)
                for s in range(2):
                    nc.scalar.activation(wt[:, s, :, :], tb[s][:, :].rearrange("p (k n) -> p k n", k=KF), ACT.Copy).then_inc(s_w2, 1)
                act.wait_ge(loaded, total["loaded"])
                prime(act, s_as, s_lo)
                def trip(g, b):
                    for j in range(TU):
                        t, q = g * TU + j, j % 2
                        done(act, s_at, t + 1)
                        done(act, s_lp, t - 1 if j >= 2 else g * TU)
                        nc.scalar.activation(ags[:, q, :, :], tb[q][:, 0:F].rearrange("p (k n) -> p k n", k=KF),
                                             ACT.Copy).then_inc(s_as, 1)
                        done(act, s_lp, t + 1)
                        alone(act)
                        for o in range(KF):
                            m = nc.scalar.activation(XT[:, o, bass.ds(t * P, P)], ob[q][:, o * P:(o + 1) * P], ACT.Relu,
                                                     bias=bl[:, o:o + 1])
                        m.then_inc(s_lo, 1)
                group_loop(act, trip)

        SC = 250
        assert N % SC == 0
        s_bst, s_bp, s_bq, s_nx, s_nt, s_nu = (sem(n) for n in ("bn_stats_step", "bn_var_ready", "bn_std_ready", "bn_scaled",
                                                               "bn_transposed", "bn_added"))
        with ExitStack() as c:
            st6 = sb("bn6", [P, KF, N // SC, 6], c=c)
            mv = sb("bnmv", [P, KF, 2], c=c)
            gm, bt = sb("gm", [P, KF], c=c), sb("bt", [P, KF], c=c)
            scl, shf = sb("scl", [P, KF], c=c), sb("shf", [P, KF], c=c)
            nx = sb("nx", [P, 2, KF, P], c=c)
            nb_ = [ps(f"bnb{b}", [P, 512], c) for b in range(2)]
            block = c.enter_context(nc.Block())

            @block.sync
            def _(sp):
                with nc.allow_non_contiguous_dma(reason="256 values each"):
                    load(sp, gm[:, :], a["L1_gnn_gamma"].rearrange("(k p) -> p k", p=P))
                    load(sp, bt[:, :], a["L1_gnn_beta"].rearrange("(k p) -> p k", p=P))

            @block.scalar
            def _(act):
                prime(act, s_nx)
                act.wait_ge(s_bp, 1)
                nc.scalar.activation(scl[:, :], mv[:, :, 1], ACT.Sqrt).then_inc(s_bq, 1)
                act.wait_ge(s_bp, 2)
                with act.Fori(0, NG) as g:
                    for j in range(TU):
                        t, q = g * TU + j, j % 2
                        done(act, s_nt, t - 1 if j >= 2 else g * TU)
                        alone(act)
                        for k in range(KF):
                            m = nc.scalar.activation(nx[:, q, k, :], XT[:, k, bass.ds(t * P, P)], ACT.Identity,
                                                     scale=scl[:, k:k + 1], bias=shf[:, k:k + 1])
                        m.then_inc(s_nx, 1)

            @block.tensor
            def _(pe):
                prime(pe, s_nt)
                with pe.Fori(0, NG) as g:
                    for j in range(TU):
                        t, q = g * TU + j, j % 2
                        done(pe, s_nx, t + 1)
                        done(pe, s_nu, t - 1 if j >= 2 else g * TU)
                        for k in range(KF):
                            m = nc.tensor.transpose(nb_[q][:, k * P:(k + 1) * P], nx[:, q, k, :], ident[:, :])
                        m.then_inc(s_nt, 1)

            @block.vector
            def _(dve):
                v = chain(dve, c_v, "v")
                prime(dve, s_nu)
                for k in range(KF):
                    for n in range(N // SC):
                        v(nc.vector.bn_stats(st6[:, k, n, :], XT[:, k, n * SC:(n + 1) * SC]))
                v.wait()
                for k in range(KF):
                    v(nc.vector.bn_aggr(mv[:, k, :], st6[:, k, :, :]))
                v.wait()
                nc.vector.tensor_scalar(mv[:, :, 1], mv[:, :, 1], 1e-5, None, ALU.add).then_inc(s_bp, 1)
                dve.wait_ge(s_bq, 1)
                dve.wait_ge(loaded, total["loaded"])
                for ins in (lambda: nc.vector.reciprocal(scl[:, :], scl[:, :]),
                            lambda: nc.vector.tensor_tensor(scl[:, :], scl[:, :], gm[:, :], ALU.mult),
                            lambda: nc.vector.tensor_tensor(shf[:, :], scl[:, :], mv[:, :, 0], ALU.mult)):
                    v(ins())
                    v.wait()
                nc.vector.tensor_tensor(shf[:, :], bt[:, :], shf[:, :], ALU.subtract).then_inc(s_bp, 1)
                with dve.Fori(0, NG) as g:
                    for j in range(TU):
                        t, q = g * TU + j, j % 2
                        done(dve, s_nt, t + 1)
                        xt = X[:, bass.ds(t, 1), :]
                        nc.vector.tensor_tensor(xt, xt, nb_[q][:, 0:F].unsqueeze(1), ALU.add).then_inc(s_nu, 1)
                done(dve, s_nu, NT)
                total["v"] = v.n

        gated("gate1", 8, a["L1_ffn_Wr"], None)
        route_phase("route1", 8, False, (a["L1_ffn_b2p"], a["L1_ffn_b2s"]))
        NE, FH = 8, 1024
        NF = FH // P
        s_wl = [sem("expert_weights_landed0"), sem("expert_weights_landed1")]
        s_h, s_hr, s_h2, s_y, s_yu, s_be = (sem(n) for n in ("hidden_product", "hidden_ready", "hidden_used", "expert_out_ready",
                                                             "expert_out_used", "expert_bias_step"))
        with ExitStack() as c:
            w1 = sb("f1w1", [P, 2, KF, FH], c=c)
            w2 = sb("f1w2", [P, 2, NF, F], c=c)
            brow, bcol = sb("f1brow", [(NE + 1) * NF, P], c=c), sb("f1bcol", [P, (NE + 1) * NF], c=c)
            bcur = sb("f1bcur", [P, 2, NF], c=c)
            ht = sb("f1ht", [P, 2, 2 * GW], c=c)
            hp = [ps(f"f1h{b}", [P, 2, 512], c) for b in range(2)]
            yp = ps("f1y", [P, TU, F], c)
            block = c.enter_context(nc.Block())

            def experts(eng, one):
                one(0, 0)
                with eng.Fori(0, NE // 2) as i:
                    one(i * 2 + 1, 1)
                    one(i * 2 + 2, 0)

            @block.sync
            def _(sp):
                load(sp, brow[0:NF, :], a["L1_ffn_b1s"].rearrange("(c p) -> c p", p=P))
                load(sp, brow[NF:, :], a["L1_ffn_b1p"].rearrange("e (c p) -> (e c) p", p=P))
                def weights(e, b):
                    if isinstance(e, int):
                        s1, s2 = a["L1_ffn_W1s"], a["L1_ffn_W2s"]
                    else:
                        sp.wait_ge(s_y, e * NG)
                        s1 = a["L1_ffn_W1p"][bass.ds(e - 1, 1)].rearrange("e k n -> (e k) n")
                        s2 = a["L1_ffn_W2p"][bass.ds(e - 1, 1)].rearrange("e k n -> (e k) n")
                    sp.dma_start(w1[:, b], s1.rearrange("(k p) n -> p k n", p=P)).then_inc(s_wl[b], 16)
                    sp.dma_start(w2[:, b], s2.rearrange("(k p) n -> p k n", p=P)).then_inc(s_wl[b], 16)
                experts(sp, weights)

            @block.tensor
            def _(pe):
                pe.wait_ge(loaded, total["loaded"])
                pe.sem_inc(s_y, NG)
                nc.tensor.transpose(hp[0][:, 0, 0:(NE + 1) * NF], brow[:, :], ident[0:(NE + 1) * NF, 0:(NE + 1) * NF]).then_inc(s_be, 1)
                pe.wait_ge(s_be, 2)
                prime(pe, s_h, s_h2)
                def expert(e, b):
                    pe.wait_ge(s_wl[b], 16 * (e - b + 2))
                    alone(pe)
                    with pe.Fori(0, NG) as g:
                        n = e * NG + g
                        for f in range(NF + 1):
                            if f < NF:
                                done(pe, s_hr, n * NF + f - 1 if f else n * NF)
                                for hf in range(2):
                                    for k in range(KF):
                                        m = nc.tensor.matmul(hp[f % 2][:, hf, 0:GW], w1[:, b, k, f * P:(f + 1) * P],
                                                             XT[:, k, bass.ds(g * (2 * GW) + hf * GW, GW)],
                                                             start=(k == 0), stop=(k == KF - 1))
                                m.then_inc(s_h, 1)
                            if f >= 1:
                                q = f - 1
                                done(pe, s_hr, n * NF + q + 1)
                                if q == 0:
                                    done(pe, s_yu, n)
                                for j in range(TU):
                                    m = nc.tensor.matmul(yp[:, j, :], ht[:, q % 2, j * P:(j + 1) * P], w2[:, b, q, :],
                                                         start=(q == 0 and j % 2 == 0),
                                                         stop=(q == NF - 1 and (j % 2 == 1 or j == TU - 1)))
                                m.then_inc(s_h2 if q < NF - 1 else s_y, 1)
                experts(pe, expert)

            @block.scalar
            def _(act):
                act.wait_ge(s_be, 1)
                nc.scalar.activation(bcol[:, :], hp[0][:, 0, 0:(NE + 1) * NF], ACT.Copy).then_inc(s_be, 1)
                act.wait_ge(s_be, 2)
                prime(act, s_hr)
                def expert(e, b):
                    if isinstance(e, int):
                        nc.scalar.activation(bcur[:, b, :], bcol[:, 0:NF], ACT.Copy).then_inc(s_be, 1)
                    else:
                        act.wait_ge(s_hr, e * NG * NF + 1)
                        alone(act)
                        nc.scalar.activation(bcur[:, b, :], bcol[:, bass.ds(e * NF, NF)], ACT.Copy).then_inc(s_be, 1)
                    act.wait_ge(s_be, e + 3)
                    alone(act)
                    with act.Fori(0, NG) as g:
                        n = e * NG + g
                        for f in range(NF):
                            done(act, s_h, n * NF + f + 1)
                            if f >= 2:
                                done(act, s_h2, n * (NF - 1) + f - 1)
                            elif f == 0:
                                done(act, s_h2, n * (NF - 1))
                            else:
                                act.wait_ge(s_y, NG + n)
                            nc.scalar.activation(ht[:, f % 2, :].rearrange("p (a n) -> p a n", a=2), hp[f % 2][:, :, 0:GW],
                                                 ACT.Gelu, bias=bcur[:, b, f:f + 1]).then_inc(s_hr, 1)
                experts(act, expert)

            @block.vector
            def _(dve):
                v = chain(dve, c_v, "v")
                prime(dve, s_yu)
                before, K = v.n, TU
                def expert(e, b):
                    with dve.Fori(0, NG) as g:
                        n = e * NG + g
                        v.base, v.n = before + n * K, 0
                        dve.wait_ge(s_y, NG + n + 1)
                        v.wait()
                        for j in range(TU):
                            xt = X[:, bass.ds(g * TU + j, 1), :]
                            y = yp[:, j:j + 1, :]
                            if isinstance(e, int):
                                v(nc.vector.tensor_tensor(xt, xt, y, ALU.add))
                            else:
                                wgt = gate[:, bass.ds(g * TU + j, 1), bass.ds(e - 1, 1)].rearrange("p a b -> p (a b)")
                                v(nc.vector.scalar_tensor_tensor(out=xt, in0=y, scalar=wgt, in1=xt, op0=ALU.mult, op1=ALU.add))
                        v.wait()
                        dve.sem_inc(s_yu, 1)
                experts(dve, expert)
                total["v"] = before + (NE + 1) * NG * K

        if stage == 1:
            pass
        s_out = sem("out_stored")
        with nc.Block() as block:
            @block.sync
            def _(sp):
                sp.dma_start(out[0:(NT - 1) * P, :].rearrange("(t p) f -> p t f", p=P), X[:, 0:NT - 1, :]).then_inc(s_out, 16)
                sp.dma_start(out[(NT - 1) * P:N, :], X[0:TAIL, NT - 1, :]).then_inc(s_out, 16)
                sp.wait_ge(s_out, 32)


_INS = ["x", "src", "dst",
        "L0_gnn_W_l", "L0_gnn_b_l", "L0_gnn_W_r", "L0_gnn_b_r", "L0_gnn_att", "L0_gnn_bias",
        "L0_ffn_sW1", "L0_ffn_sb1", "L0_ffn_sW2", "L0_ffn_sb2", "L0_ffn_sW3", "L0_ffn_sb3",
        "L0_ffn_eW1", "L0_ffn_eb1", "L0_ffn_eW2", "L0_ffn_eb2", "L0_ffn_eW3", "L0_ffn_eb3", "L0_ffn_gW", "L0_ffn_gb",
        "L1_gnn_W_proj", "L1_gnn_b_proj", "L1_gnn_W_l", "L1_gnn_b_l", "L1_gnn_W_r", "L1_gnn_gamma", "L1_gnn_beta",
        "L1_ffn_Wr", "L1_ffn_W1s", "L1_ffn_b1s", "L1_ffn_W2s", "L1_ffn_b2s", "L1_ffn_W1p", "L1_ffn_b1p",
        "L1_ffn_W2p", "L1_ffn_b2p"]


def kernel(**inputs):
    import numpy as _np
    import concourse.bacc as _bacc
    from concourse import mybir as _mybir
    from concourse.bass_utils import run_bass_kernel_spmd as _run

    nc = _bacc.Bacc("TRN2", target_bir_lowering=False, num_devices=1)
    arrays, aps = {}, {}
    for name in _INS:
        v = _np.ascontiguousarray(inputs[name])
        arrays[f"in_{name}"] = v
        aps[name] = nc.dram_tensor(f"in_{name}", v.shape, _mybir.dt.from_np(v.dtype), kind="ExternalInput").ap()
    out = nc.dram_tensor("out", (N, F), _mybir.dt.float32, kind="ExternalOutput").ap()
    graph_block_kernel(nc, aps, out)
    r = _run(nc, [arrays], core_ids=[0])
    return r.results[0]["out"]
```

```python
from contextlib import ExitStack

import numpy as np
import concourse.bass as bass
from concourse import mybir

F32, I32 = mybir.dt.float32, mybir.dt.int32
ALU = mybir.AluOpType
ACT = mybir.ActivationFunctionType
AX = mybir.AxisListType

P = 128
N, E, F = 6250, 100000, 256
KF = F // P
H, C = 4, 64
NT = -(-N // P)
NP = NT * P
TAIL = N - (NT - 1) * P
T = 7
NB = 4
EP = 784
CH = EP // T
ELAST = E - (P - 1) * EP
XW = F + H
SW = F + 2 * H
BIG = 1.0e6
NEG = -1.0e30
SLOPE = 0.2
LN_EPS = 1e-5
TU = 7
NG = NT // TU
GW = TU * P // 2
assert CH * T == EP and CH % NB == 0 and NG * TU == NT and 0 < ELAST < EP


class Chain:

    def __init__(self, eng, sem):
        self.eng, self.sem, self.n, self.base = eng, sem, 0, 0

    def __call__(self, ins):
        ins.then_inc(self.sem, 1)
        self.n += 1

    def wait(self):
        if isinstance(self.base, int) and self.base + self.n == 0:
            return
        self.eng.wait_ge(self.sem, self.base + self.n)

    def enter(self, i, per_trip):
        self.before, self.per_trip = self.base + self.n, per_trip
        self.base, self.n = self.before + i * per_trip, 0

    def leave(self, trips):
        assert self.n == self.per_trip, (self.n, self.per_trip)
        self.base, self.n = self.before + trips * self.per_trip, 0


def graph_block_kernel(nc, a, out, stage=9):
    ctx = ExitStack()
    with ctx:
        def dram(name, shape, dt=F32):
            return nc.dram_tensor(name, shape, dt, kind="Internal").ap()

        def sem(name):
            return ctx.enter_context(nc.semaphore(name))

        def sb(name, shape, dt=F32, c=ctx):
            return c.enter_context(nc.sbuf_tensor(name, shape, dt))

        def ps(name, shape, c):
            return c.enter_context(nc.psum_tensor(name, shape, F32))

        xl_tab, xr_tab = dram("xl_tab", (NP, XW)), dram("xr_tab", (NP, XW))
        xp_tab = dram("xp_tab", (NP, F))
        dst_rows = dram("dst_rows", (P, EP))
        soft_tab = dram("soft_tab", (P * EP + 1, SW))
        soft_carry = dram("soft_carry", (P + 1, SW))
        max_tab = dram("max_tab", (P * EP + 1, F))
        max_carry = dram("max_carry", (P + 1, F))

        X = sb("X", [P, NT, F])
        ident = sb("ident", [P, P])
        ones = sb("ones", [P, P])
        node = sb("node", [P, NT])
        idx_end = sb("idx_end", [P, NT], I32)
        idx_carry = sb("idx_carry", [P, NT], I32)
        dl_col = sb("dl_col", [P, 1])
        dl_row = sb("dl_row", [P, P])
        src_i, dst_i = sb("src_i", [P, EP], I32), sb("dst_i", [P, EP], I32)
        keep, pen = sb("keep", [P, EP]), sb("pen", [P, EP])

        c_v, c_a, c_t, c_p = sem("dve_step"), sem("act_step"), sem("pe_step"), sem("pool_step")
        settle = sem("wait_stood_alone")
        loaded, stored = sem("loaded"), sem("stored")
        total = {"loaded": 0, "stored": 0, "v": 0, "a": 0, "t": 0, "p": 0}

        def load(eng, dst, src):
            eng.dma_start(dst, src).then_inc(loaded, 16)
            total["loaded"] += 16

        def store(eng, dst, src):
            eng.dma_start(dst, src).then_inc(stored, 16)
            total["stored"] += 16

        def chain(eng, s, key):
            c = Chain(eng, s)
            c.n = total[key]
            return c

        def alone(eng):
            eng.sem_inc(settle, 1)

        def prime(eng, *sems):
            for s in sems:
                eng.sem_inc(s, 1)

        def done(eng, s, n):
            eng.wait_ge(s, n + 1)

        def row(vec, n):
            return vec.rearrange("(a n) -> a n", a=1).broadcast_to([P, n])

        s_id, s_dst = sem("ident_ready"), sem("dst_ready")
        att_b = sb("att_b", [P, F])
        upto, below = sb("upto", [P, NT]), sb("below", [P, NT])
        rowi = sb("rowi", [P, NT], I32)
        limits = sb("limits", [P, 3, NT])
        with ExitStack() as c:
            node_b = sb("node_b", [P, NT, P], c=c)
            dst_f = sb("dst_f", [P, EP], c=c)
            scr = sb("scr", [P, EP], c=c)
            dlb = ps("dlb", [P, P], c)
            block = c.enter_context(nc.Block())

            @block.sync
            def _(sp):
                sp.wait_ge(s_id, 6)
                load(sp, X[:, 0:NT - 1, :], a["x"][0:(NT - 1) * P, :].rearrange("(t p) f -> p t f", p=P))
                load(sp, X[0:TAIL, NT - 1, :], a["x"][(NT - 1) * P:N, :])
                for t, v in ((src_i, a["src"]), (dst_i, a["dst"])):
                    load(sp, t[0:P - 1, :], v[0:(P - 1) * EP].rearrange("(p e) -> p e", p=P - 1))
                    load(sp, t[P - 1:P, 0:ELAST], v[(P - 1) * EP:E].rearrange("(p e) -> p e", p=1))
                sp.wait_ge(s_dst, 1)
                store(sp, dst_rows, dst_f[:, :])
                sp.wait_ge(stored, total["stored"])

            @block.gpsimd
            def _(pool):
                p = chain(pool, c_p, "p")
                nc.gpsimd.memset(X[:, NT - 1, :], 0.0).then_inc(s_id, 1)
                nc.gpsimd.memset(src_i[:, ELAST:], 0).then_inc(s_id, 1)
                nc.gpsimd.memset(dst_i[:, ELAST:], int(BIG)).then_inc(s_id, 1)
                nc.gpsimd.memset(ones[:, :], 1.0).then_inc(s_id, 1)
                p(nc.gpsimd.memset(ident[:, :], 0.0))
                p.wait()
                nc.gpsimd.affine_select(out=ident[:, :], in_=ident[:, :], compare_op=ALU.not_equal, fill=1.0,
                                        base=0, pattern=[[-1, P]], channel_multiplier=1).then_inc(s_id, 1)
                nc.gpsimd.iota(node[:, :], [[P, NT]], base=0, channel_multiplier=1,
                               allow_small_or_imprecise_dtypes=True).then_inc(s_id, 1)
                total["p"] = p.n

            @block.tensor
            def _(pe):
                pe.wait_ge(s_id, 6)
                pe.wait_ge(s_dst, 2)
                nc.tensor.matmul(dlb[:, :], dl_col[:, 0:1].broadcast_to([P, P]), ident[:, :],
                                 start=True, stop=True).then_inc(c_t, 1)
                total["t"] = 1

            @block.vector
            def _(dve):
                v = chain(dve, c_v, "v")
                dve.wait_ge(loaded, total["loaded"])
                nc.vector.tensor_copy(dst_f[:, :], dst_i[:, :]).then_inc(s_dst, 1)
                dve.wait_ge(s_dst, 1)
                nc.vector.tensor_copy(dl_col[:, :], dst_f[:, EP - 1:EP]).then_inc(s_dst, 1)
                v(nc.vector.memset(keep[:, 0:1], 0.0))
                v(nc.vector.tensor_tensor(keep[:, 1:EP], dst_f[:, 1:EP], dst_f[:, 0:EP - 1], ALU.is_equal))
                v.wait()
                v(nc.vector.tensor_scalar(pen[:, :], keep[:, :], 1.0, -NEG, ALU.subtract, ALU.mult))
                dve.wait_ge(s_dst, 2)
                v(nc.vector.tensor_scalar(scr[:, :], dst_f[:, :], float(N - 1), None, ALU.min))
                v.wait()
                v(nc.vector.tensor_copy(dst_i[:, :], scr[:, :]))
                dve.wait_ge(c_t, 1)
                v(nc.vector.tensor_copy(dl_row[:, :], dlb[:, :]))
                v.wait()
                dve.wait_ge(s_id, 6)
                dlv = dl_row[:, :].unsqueeze(1).broadcast_to([P, NT, P])
                nov = node[:, :].unsqueeze(2).broadcast_to([P, NT, P])
                for op, dst in ((ALU.is_lt, below), (ALU.is_le, upto)):
                    v(nc.vector.tensor_tensor(node_b[:, :, :], dlv, nov, op))
                    v.wait()
                    v(nc.vector.tensor_reduce(dst[:, :], node_b[:, :, :], AX.X, ALU.add))
                    v.wait()
                v(nc.vector.tensor_copy(rowi[:, :], upto[:, :]))
                for k in range(3):
                    v(nc.vector.tensor_scalar(limits[:, k, :], node[:, :], 1.0 - k, None, ALU.add))
                v.wait()
                total["v"] = v.n

        def norm_phase(name, width, tokens, ph, keep=None):
            s_var, s_std, s_rstd = sem(f"{name}_var_ready"), sem(f"{name}_std_ready"), sem(f"{name}_rstd_ready")
            s_xn, s_tp, s_ev = sem(f"{name}_xn_ready"), sem(f"{name}_transposed"), sem(f"{name}_xT_ready")
            s_xt, s_mm, s_use = sem(f"{name}_xT_kept"), sem(f"{name}_product"), sem(f"{name}_product_used")
            with ExitStack() as c:
                st6 = sb("st6" + name, [P, NT, 6], c=c)
                mean, rstd = keep or (sb(n + name, [P, NT], c=c) for n in ("mean", "rstd"))
                tmp = sb("tmp" + name, [P, NT], c=c)
                xn = sb("xn" + name, [P, 3, F], c=c)
                xts = sb("xts" + name, [P, 3, KF, P], c=c)
                w = sb("w" + name, [P, KF, width], c=c)
                xt_ps = [ps(f"xt_ps{b}" + name, [P, 512], c) for b in range(2)]
                mm_ps = [ps(f"mm_ps{b}" + name, [P, 512], c) for b in range(2)]
                xt_ps0 = xt_ps[0]
                ex = ph(c, w, xt_ps0)
                block = c.enter_context(nc.Block())

                def xt_view(b):
                    return xt_ps[b][:, 0:F].rearrange("p (k n) -> p k n", k=KF)

                @block.sync
                def _(sp):
                    ex["loads"](sp)
                    if "rows" in ex:
                        ex["rows"](sp, s_use)

                @block.vector
                def _(dve):
                    v = chain(dve, c_v, "v")
                    prime(dve, s_use, s_xn)
                    with dve.Fori(0, NG) as g:
                        v.enter(g, TU)
                        for j in range(TU):
                            v(nc.vector.bn_stats(st6[:, bass.ds(g * TU + j, 1), :], X[:, bass.ds(g * TU + j, 1), :]))
                        v.leave(NG)
                    v.wait()
                    v(nc.vector.tensor_tensor(mean[:, :], st6[:, :, 1], st6[:, :, 4], ALU.add))
                    v(nc.vector.tensor_tensor(tmp[:, :], st6[:, :, 1], st6[:, :, 4], ALU.subtract))
                    v.wait()
                    v(nc.vector.tensor_tensor(tmp[:, :], tmp[:, :], tmp[:, :], ALU.mult))
                    v(nc.vector.tensor_tensor(rstd[:, :], st6[:, :, 2], st6[:, :, 5], ALU.add))
                    v.wait()
                    v(nc.vector.tensor_scalar(rstd[:, :], rstd[:, :], 1.0 / F, LN_EPS, ALU.mult, ALU.add))
                    v(nc.vector.tensor_scalar(mean[:, :], mean[:, :], 0.5, None, ALU.mult))
                    v.wait()
                    nc.vector.scalar_tensor_tensor(out=rstd[:, :], in0=tmp[:, :], scalar=0.25, in1=rstd[:, :],
                                                   op0=ALU.mult, op1=ALU.add).then_inc(s_var, 1)
                    dve.wait_ge(s_std, 1)
                    nc.vector.reciprocal(rstd[:, :], tmp[:, :]).then_inc(s_rstd, 1)
                    dve.wait_ge(s_rstd, 1)
                    with dve.Fori(0, NG) as g:
                        v.enter(g, TU * ex["steps"])
                        def normalize(j):
                            t, b = g * TU + j, j % 3
                            done(dve, s_tp, t - 2 if j >= 3 else g * TU)
                            nc.vector.tensor_scalar(xn[:, b:b + 1, :], X[:, bass.ds(t, 1), :], mean[:, bass.ds(t, 1)],
                                                    rstd[:, bass.ds(t, 1)], ALU.subtract, ALU.mult).then_inc(s_xn, 1)
                        normalize(0)
                        normalize(1)
                        for j in range(TU):
                            if j + 2 < TU:
                                normalize(j + 2)
                            done(dve, s_mm, g * TU + j + 1)
                            ex["consume"](v, dve, mm_ps[j % 2], g, j, s_use)
                        v.leave(NG)
                    v.wait()
                    if "last" in ex:
                        ex["last"](v, dve)
                    total["v"] = v.base + v.n

                @block.scalar
                def _(act):
                    prime(act, s_ev)
                    act.wait_ge(s_var, 1)
                    nc.scalar.activation(tmp[:, :], rstd[:, :], ACT.Sqrt).then_inc(s_std, 1)
                    if "act" in ex:
                        ex["act"](act)
                    with act.Fori(0, NG) as g:
                        for j in range(TU):
                            t, b = g * TU + j, j % 3
                            done(act, s_tp, t + 1)
                            if tokens is not None:
                                done(act, s_xt, t - 2 if j >= 3 else g * TU)
                            done(act, s_mm, t - 2 if j >= 3 else g * TU)
                            nc.scalar.activation(xts[:, b, :, :], xt_view(j % 2), ACT.Copy).then_inc(s_ev, 1)
                            if "act_tile" in ex:
                                ex["act_tile"](act, g, j)

                @block.gpsimd
                def _(pool):
                    prime(pool, s_xt)
                    if "pool" in ex:
                        ex["pool"](pool)
                    if tokens is not None:
                        with pool.Fori(0, NG) as g:
                            for j in range(TU):
                                t, b = g * TU + j, j % 3
                                done(pool, s_ev, t + 1)
                                alone(pool)
                                nc.gpsimd.tensor_copy(tokens[:, :, bass.ds(t * P, P)], xts[:, b, :, :]).then_inc(s_xt, 1)

                @block.tensor
                def _(pe):
                    prime(pe, s_tp, s_mm)
                    pe.wait_ge(loaded, total["loaded"])
                    if "pe" in ex:
                        ex["pe"](pe)
                    with pe.Fori(0, NG) as g:
                        def turn(j):
                            t = g * TU + j
                            done(pe, s_xn, t + 1)
                            done(pe, s_ev, t - 1 if j >= 2 else g * TU)
                            for k in range(KF):
                                m = nc.tensor.transpose(xt_ps[j % 2][:, k * P:(k + 1) * P], xn[:, j % 3, k * P:(k + 1) * P],
                                                        ident[:, :])
                            m.then_inc(s_tp, 1)
                        turn(0)
                        for j in range(TU):
                            t, b = g * TU + j, j % 2
                            if j + 1 < TU:
                                turn(j + 1)
                            done(pe, s_ev, t + 1)
                            done(pe, s_use, t - 1 if j >= 2 else g * TU)
                            for k in range(KF):
                                m = nc.tensor.matmul(mm_ps[b][:, 0:width], xts[:, j % 3, k, :], w[:, k, :],
                                                     start=(k == 0), stop=(k == KF - 1))
                            m.then_inc(s_mm, 1)

        USES = [(TU + 1) // 2, TU // 2]

        s_rows = [sem(f"dst_row_landed{b}") for b in range(3)]
        s_ridx, s_counted = sem("row_index_ready"), sem("dst_row_counted")
        s_pst = [sem("proj_stored0"), sem("proj_stored1")]

        def proj(c, w, bank):
            bias = sb("proj_bias", [P, 2 * F], c=c)
            rows = sb("rows", [P, 3, EP], c=c)
            scr = sb("relu_scratch", [P, EP], c=c)
            ri = sb("ri", [P, TU], I32, c=c)
            rsum = sb("rsum", [P, 3, NT], c=c)
            fa, fb = sb("fa", [P, NT], c=c), sb("fb", [P, NT], c=c)
            cnt_lt, cnt_le = sb("cnt_lt", [P, NT], c=c), sb("cnt_le", [P, NT], c=c)
            rowb, am = sb("proj_row", [P, 2, 2, XW], c=c), sb("proj_att", [P, 2, 2, F], c=c)

            def loads(sp):
                load(sp, w[:, :, 0:F], a["L0_gnn_W_l"].rearrange("(k p) n -> p k n", p=P))
                load(sp, w[:, :, F:2 * F], a["L0_gnn_W_r"].rearrange("(k p) n -> p k n", p=P))
                for b, n in enumerate(("L0_gnn_b_l", "L0_gnn_b_r")):
                    sp.dma_start(bias[:, b * F:(b + 1) * F], row(a[n], F)).then_inc(s_pst[b], 32)
                load(sp, att_b[:, :], row(a["L0_gnn_att"].rearrange("h c -> (h c)"), F))

            def consume(v, dve, mm, g, j, s_use):
                b = j % 2
                r, m = rowb[:, b, :, :], am[:, b, :, :]
                dve.wait_ge(s_pst[b], 32 * (g * USES[b] + j // 2 + 1))
                if j == 0:
                    dve.wait_ge(s_pst[1], 32)
                    dve.wait_ge(loaded, total["loaded"])
                v(nc.vector.tensor_tensor(r[:, :, 0:F], mm[:, 0:2 * F].rearrange("p (s f) -> p s f", s=2),
                                          bias[:, :].rearrange("p (s f) -> p s f", s=2), ALU.add))
                v.wait()
                for k in range(2):
                    v(nc.vector.scalar_tensor_tensor(out=m[:, k, :], in0=r[:, k, 0:F], scalar=SLOPE, in1=att_b[:, :],
                                                     op0=ALU.mult, op1=ALU.mult))
                v.wait()
                nc.vector.tensor_reduce(r[:, :, F:XW], m.rearrange("p s (h c) -> p s h c", h=H), AX.X,
                                        ALU.add).then_inc(s_use, 1)

            def store_rows(sp, s_use):
                with sp.Fori(0, NG) as g:
                    for j in range(TU):
                        t, b = g * TU + j, j % 2
                        done(sp, s_use, t + 1)
                        for k, tab in enumerate((xl_tab, xr_tab)):
                            sp.dma_start(tab[bass.ds(t * P, P), :], rowb[:, b, k, :]).then_inc(s_pst[b], 16)
                for b in range(2):
                    sp.wait_ge(s_pst[b], 32 * (NG * USES[b] + 1))

            def gather_rows(pool):
                pool.sem_inc(s_counted, 9)
                with pool.Fori(0, NG) as g:
                    pool.wait_ge(s_counted, (g * TU + 3) * 3)
                    alone(pool)
                    nc.gpsimd.tensor_copy(ri[:, :], rowi[:, bass.ds(g * TU, TU)]).then_inc(s_ridx, 1)
                    pool.wait_ge(s_ridx, g + 1)
                    alone(pool)
                    for j in range(TU):
                        pool.wait_ge(s_counted, (g * TU + j + 1) * 3 if j else (g * TU + 3) * 3)
                        alone(pool)
                        pool.indirect_dma_start(rows[:, j % 3, :], None, dst_rows,
                                                bass.IndirectOffsetOnAxis(ri[:, j:j + 1], 0)).then_inc(s_rows[j % 3], 16)

            def count(act, g, j):
                b = j % 3
                act.wait_ge(s_rows[b], 16 * (g * (3 if b == 0 else 2) + j // 3 + 1))
                alone(act)
                for k in range(3):
                    act.wait_ge(s_counted, (g * TU + j + 3) * 3 + k)
                    alone(act)
                    nc.scalar.activation(scr[:, :], rows[:, b, :], ACT.Relu, bias=limits[:, k, bass.ds(g * TU + j, 1)],
                                         scale=-1.0, accum_out=rsum[:, k, bass.ds(g * TU + j, 1)]).then_inc(s_counted, 1)

            def index(v, dve):
                dve.wait_ge(s_counted, 3 * (NT + 3))
                v(nc.vector.tensor_tensor(cnt_le[:, :], rsum[:, 0, :], rsum[:, 1, :], ALU.subtract))
                v(nc.vector.tensor_tensor(cnt_lt[:, :], rsum[:, 1, :], rsum[:, 2, :], ALU.subtract))
                steps = [
                    lambda: nc.vector.tensor_tensor(fa[:, :], cnt_le[:, :], cnt_lt[:, :], ALU.is_gt),
                    lambda: nc.vector.tensor_scalar(fb[:, :], upto[:, :], float(EP), -1.0 - P * EP, ALU.mult, ALU.add),
                    lambda: nc.vector.tensor_tensor(fb[:, :], fb[:, :], cnt_le[:, :], ALU.add),
                    lambda: nc.vector.tensor_tensor(fb[:, :], fb[:, :], fa[:, :], ALU.mult),
                    lambda: nc.vector.tensor_scalar(fb[:, :], fb[:, :], float(P * EP), None, ALU.add),
                    lambda: nc.vector.tensor_copy(idx_end[:, :], fb[:, :]),
                    lambda: nc.vector.tensor_tensor(fa[:, :], upto[:, :], below[:, :], ALU.is_gt),
                    lambda: nc.vector.tensor_scalar(fb[:, :], upto[:, :], -1.0 - P, None, ALU.add),
                    lambda: nc.vector.tensor_tensor(fb[:, :], fb[:, :], fa[:, :], ALU.mult),
                    lambda: nc.vector.tensor_scalar(fb[:, :], fb[:, :], float(P), None, ALU.add),
                    lambda: nc.vector.tensor_copy(idx_carry[:, :], fb[:, :]),
                ]
                for s in steps:
                    v.wait()
                    v(s())
                v.wait()
            return {"loads": loads, "consume": consume, "steps": 3, "rows": store_rows, "pool": gather_rows,
                    "act_tile": count, "last": index}

        norm_phase("proj", 2 * F, None, proj)

        s_row = [sem(f"rows_landed{b}") for b in range(NB)]
        s_free, s_idx = sem("rows_free"), sem("gather_index_ready")
        s_z, s_relu, s_d, s_exp = sem("z_ready"), sem("relu_ready"), sem("exponents_ready"), sem("exp_ready")
        s_st, s_stored = sem("state_ready"), [sem("state_stored0"), sem("state_stored1")]
        s_neutral, s_num = sem("neutral_ready"), sem("numerator_step")
        TRIPS = CH // NB
        soft_rows = soft_tab[0:P * EP, :].rearrange("(p e) f -> p e f", p=P)
        last_state = sb("last_state", [P, SW])
        neutral = sb("neutral", [1, SW])
        with ExitStack() as c:
            xl = sb("xl", [P, NB, T, XW], c=c)
            xr = sb("xr", [P, NB, T, XW], c=c)
            z = sb("z", [P, 3, T * F], c=c)
            lin, logit = sb("lin", [P, T, H], c=c), sb("logit", [P, 2, T, H], c=c)
            lg = sb("lg", [P, H, T], c=c)
            mx = sb("mx", [P, 2, H, T + 1], c=c)
            ex_in, ex_out = sb("ex_in", [P, 2, 2, H, T], c=c), sb("ex_out", [P, 2, 2, H, T], c=c)
            state = sb("state", [P, 2, T, SW], c=c)
            si, di = sb("si", [P, NB, T], I32, c=c), sb("di", [P, NB, T], I32, c=c)
            zp = [ps(f"zp{b}", [P, T, F], c) for b in range(2)]
            block = c.enter_context(nc.Block())

            @block.tensor
            def _(pe):
                pe.sem_inc(s_z, 1)
                with pe.Fori(0, TRIPS) as i:
                    for k in range(NB):
                        pe.wait_ge(s_row[k], 32 * T * (i + 1))
                        pe.wait_ge(s_relu, i * NB + k + 1)
                        for t in range(0, T, 2):
                            w = slice(t, min(t + 2, T))
                            nc.tensor.matmul(zp[k % 2][:, w, :], ident[:, :], xl[:, k, w, 0:F], start=True, stop=False)
                            m = nc.tensor.matmul(zp[k % 2][:, w, :], ident[:, :], xr[:, k, w, 0:F], start=False, stop=True)
                        m.then_inc(s_z, 1)

            @block.gpsimd
            def _(pool):
                nc.gpsimd.memset(neutral[0:1, 0:F + H], 0.0).then_inc(s_neutral, 1)
                nc.gpsimd.memset(neutral[0:1, F + H:SW], NEG).then_inc(s_neutral, 1)
                with pool.Fori(0, TRIPS) as i:
                    for b in range(NB):
                        pool.wait_ge(s_free, i * NB + b + 1)
                        alone(pool)
                        e0 = (i * NB + b) * T
                        nc.gpsimd.tensor_copy(si[:, b, :], src_i[:, bass.ds(e0, T)]).then_inc(s_idx, 1)
                        nc.gpsimd.tensor_copy(di[:, b, :], dst_i[:, bass.ds(e0, T)]).then_inc(s_idx, 1)
                        pool.wait_ge(s_idx, 2 * (i * NB + b + 1))
                        alone(pool)
                        for t in range(T):
                            for buf, ix, tab in ((xl, si, xl_tab), (xr, di, xr_tab)):
                                pool.indirect_dma_start(buf[:, b, t, :], None, tab,
                                                        bass.IndirectOffsetOnAxis(ix[:, b, t:t + 1], 0)).then_inc(s_row[b], 16)

            @block.scalar
            def _(act):
                act.sem_inc(s_relu, 2)
                with act.Fori(0, TRIPS) as i:
                    def relu(k):
                        done(act, s_z, i * NB + k + 1)
                        act.wait_ge(s_st, i * NB + k + 1 if k != 0 else i * NB + 3)
                        nc.scalar.activation(z[:, k % 3, :], zp[k % 2][:, :, :].rearrange("p t f -> p (t f)"), ACT.Relu,
                                             scale=1.0 - SLOPE).then_inc(s_relu, 1)
                    relu(0)
                    for k in range(NB):
                        if k + 1 < NB:
                            relu(k + 1)
                        act.wait_ge(s_d, i * NB + k + 1)
                        nc.scalar.activation(ex_out[:, k % 2], ex_in[:, k % 2], ACT.Exp).then_inc(s_exp, 1)

            @block.sync
            def _(sp):
                sp.wait_ge(s_neutral, 2)
                sp.dma_start(soft_tab[P * EP:P * EP + 1, :], neutral[0:1, :]).then_inc(s_stored[0], 16)
                sp.dma_start(soft_carry[P:P + 1, :], neutral[0:1, :]).then_inc(s_stored[1], 16)
                with sp.Fori(0, TRIPS) as i:
                    for k in range(NB):
                        sp.wait_ge(s_st, i * NB + k + 4)
                        sp.dma_start(soft_rows[:, bass.ds((i * NB + k) * T, T), :], state[:, k % 2, :, :]).then_inc(s_stored[k % 2], 16)
                for b in range(2):
                    sp.wait_ge(s_stored[b], 16 * (CH // 2 + 1))

            @block.vector
            def _(dve):
                v = chain(dve, c_v, "v")
                v(nc.vector.memset(state[:, 1, T - 1, 0:F + H], 0.0))
                v(nc.vector.memset(state[:, 1, T - 1, F + H:SW], NEG))
                v(nc.vector.memset(mx[:, 1, :, T:T + 1], NEG))
                v.wait()
                dve.sem_inc(s_free, NB)
                dve.sem_inc(s_st, 3)
                with dve.Fori(0, TRIPS) as i:
                    v.enter(i, NB * 16)
                    def logits(k):
                        zk = z[:, k % 3, :].rearrange("p (t f) -> p t f", t=T)
                        dve.wait_ge(s_row[k], 32 * T * (i + 1))
                        v.wait()
                        v(nc.vector.tensor_tensor(lin[:, :, :], xl[:, k, :, F:XW], xr[:, k, :, F:XW], ALU.add))
                        v(nc.vector.tensor_copy(mx[:, k % 2, :, 0:1], mx[:, (k + 1) % 2, :, T:T + 1]))
                        dve.wait_ge(s_relu, i * NB + k + 3)
                        v(nc.vector.tensor_tensor(zk, zk, att_b[:, :].unsqueeze(1).broadcast_to([P, T, F]), ALU.mult))
                        v.wait()
                        v(nc.vector.tensor_reduce(logit[:, 0, :, :], zk.rearrange("p t (h c) -> p t h c", h=H), AX.X, ALU.add))
                        v.wait()
                        v(nc.vector.tensor_tensor(lg[:, :, :], logit[:, 0, :, :].rearrange("p t h -> p h t"),
                                                  lin[:, :, :].rearrange("p t h -> p h t"), ALU.add))
                        v.wait()
                        pk = pen[:, bass.ds((i * NB + k) * T, T)]
                        for h in range(H):
                            v(nc.vector.tensor_tensor_scan(mx[:, k % 2, h, 1:T + 1], pk, lg[:, h, :],
                                                           mx[:, k % 2, h, 0:1], ALU.add, ALU.max))
                        v.wait()
                        m0, m1 = mx[:, k % 2, :, 0:T], mx[:, k % 2, :, 1:T + 1]
                        v(nc.vector.tensor_tensor(ex_in[:, k % 2, 0], lg[:, :, :], m1, ALU.subtract))
                        v(nc.vector.tensor_tensor(ex_in[:, k % 2, 1], m0, m1, ALU.subtract))
                        v.wait()
                        nc.vector.tensor_tensor(ex_in[:, k % 2, 1], ex_in[:, k % 2, 1],
                                                pk.unsqueeze(1).broadcast_to([P, H, T]), ALU.add).then_inc(s_d, 1)
                    def sums(k):
                        new, old = state[:, k % 2], state[:, (k + 1) % 2]
                        ea, ec = ex_out[:, k % 2, 0], ex_out[:, k % 2, 1]
                        pr = z[:, k % 3, :].rearrange("p (t h c) -> p t h c", t=T, h=H)
                        dve.wait_ge(s_exp, i * NB + k + 1)
                        nc.vector.tensor_tensor(pr, xl[:, k, :, 0:F].rearrange("p t (h c) -> p t h c", h=H),
                                                ea.rearrange("p h t -> p t h").unsqueeze(3).broadcast_to([P, T, H, C]),
                                                ALU.mult).then_inc(s_free, 1)
                        dve.wait_ge(s_stored[k % 2], 16 * (i * (NB // 2) + k // 2 + 1))
                        for h in range(H):
                            v(nc.vector.tensor_tensor_scan(new[:, :, F + h], ec[:, h, :], ea[:, h, :],
                                                           old[:, T - 1, F + h:F + h + 1], ALU.mult, ALU.add))
                        v(nc.vector.tensor_copy(new[:, :, F + H:SW], mx[:, k % 2, :, 1:T + 1].rearrange("p h t -> p t h")))
                        dve.wait_ge(s_free, i * NB + k + 1 + NB)
                        for t in range(T):
                            prev = old[:, T - 1] if t == 0 else new[:, t - 1]
                            for h in range(H):
                                n = (i * NB + k) * (T * H) + t * H + h
                                if t or k:
                                    dve.wait_ge(s_num, n - 3)
                                hs = slice(h * C, (h + 1) * C)
                                nc.vector.scalar_tensor_tensor(out=new[:, t, hs], in0=prev[:, hs], scalar=ec[:, h, t:t + 1],
                                                               in1=pr[:, t, h, :], op0=ALU.mult, op1=ALU.add).then_inc(s_num, 1)
                        dve.wait_ge(s_num, (i * NB + k + 1) * T * H)
                        v.wait()
                        dve.sem_inc(s_st, 1)
                    for k in range(NB):
                        logits(k)
                        if k >= 1:
                            sums(k - 1)
                    sums(NB - 1)
                    v.leave(TRIPS)
                v.wait()
                v(nc.vector.tensor_copy(last_state[:, :], state[:, 1, T - 1, :]))
                v.wait()
                total["v"] = v.base + v.n

        s_cst = sem("carry_step")
        with ExitStack() as c:
            tri = sb("tri", [P, P], c=c)
            same, cpen = sb("same", [P, P], c=c), sb("cpen", [P, P], c=c)
            mrow, wrow = sb("mrow", [P, H, P], c=c), sb("wrow", [P, H, P], c=c)
            wq = sb("wq", [P, H, P], c=c)
            cmax = sb("cmax", [P, H], c=c)
            crow = sb("crow", [P, SW], c=c)
            mp, tp, op = (ps(n, [P, 512], c) for n in ("mp", "tp", "op"))
            block = c.enter_context(nc.Block())

            @block.gpsimd
            def _(pool):
                nc.gpsimd.affine_select(out=tri[:, :], in_=ones[:, :], compare_op=ALU.is_ge, fill=0.0,
                                        base=0, pattern=[[-1, P]], channel_multiplier=1).then_inc(s_cst, 1)

            @block.tensor
            def _(pe):
                pe.wait_ge(s_cst, 1)
                for h in range(H):
                    m = nc.tensor.matmul(mp[:, h * P:(h + 1) * P], last_state[:, F + H + h:F + H + h + 1].broadcast_to([P, P]),
                                         ident[:, :], start=True, stop=True)
                m.then_inc(s_cst, 1)
                pe.wait_ge(s_cst, 4)
                for h in range(H):
                    m = nc.tensor.transpose(tp[:, h * P:(h + 1) * P], wrow[:, h, :], ident[:, :])
                m.then_inc(s_cst, 1)
                pe.wait_ge(s_cst, 6)
                for h in range(H):
                    nc.tensor.matmul(op[:, h * C:(h + 1) * C], wq[:, h, :], last_state[:, h * C:(h + 1) * C],
                                     start=True, stop=True)
                    m = nc.tensor.matmul(op[:, F + h:F + h + 1], wq[:, h, :], last_state[:, F + h:F + h + 1],
                                         start=True, stop=True)
                m.then_inc(s_cst, 1)

            @block.vector
            def _(dve):
                v = chain(dve, c_v, "v")
                dve.wait_ge(s_cst, 2)
                v(nc.vector.tensor_scalar(same[:, :], dl_row[:, :], dl_col[:, 0:1], None, ALU.is_equal))
                v.wait()
                v(nc.vector.tensor_tensor(same[:, :], same[:, :], tri[:, :], ALU.mult))
                v.wait()
                v(nc.vector.tensor_scalar(cpen[:, :], same[:, :], 1.0, -NEG, ALU.subtract, ALU.mult))
                v.wait()
                v(nc.vector.tensor_tensor(mrow[:, :, :], mp[:, :].rearrange("p (h q) -> p h q", h=H),
                                          cpen[:, :].unsqueeze(1).broadcast_to([P, H, P]), ALU.add))
                v.wait()
                v(nc.vector.tensor_reduce(cmax[:, :], mrow[:, :, :], AX.X, ALU.max))
                v.wait()
                nc.vector.tensor_tensor(mrow[:, :, :], mrow[:, :, :], cmax[:, :].unsqueeze(2).broadcast_to([P, H, P]),
                                        ALU.subtract).then_inc(s_cst, 1)
                dve.wait_ge(s_cst, 5)
                nc.vector.tensor_copy(wq[:, :, :], tp[:, :].rearrange("p (h q) -> p h q", h=H)).then_inc(s_cst, 1)
                dve.wait_ge(s_cst, 7)
                v(nc.vector.tensor_copy(crow[:, 0:F + H], op[:, 0:F + H]))
                nc.vector.tensor_copy(crow[:, F + H:SW], cmax[:, :]).then_inc(s_cst, 1)
                v.wait()
                total["v"] = v.n

            @block.scalar
            def _(act):
                act.wait_ge(s_cst, 3)
                nc.scalar.activation(wrow[:, :, :], mrow[:, :, :], ACT.Exp).then_inc(s_cst, 1)

            @block.sync
            def _(sp):
                sp.wait_ge(s_cst, 8)
                sp.wait_ge(c_v, total["v"])
                store(sp, soft_carry[0:P, :], crow[:, :])
                sp.wait_ge(stored, total["stored"])

        def group_loop(eng, trip):
            with eng.Fori(0, NG // 2) as i:
                trip(i * 2, 0)
                trip(i * 2 + 1, 1)
            assert NG % 2 == 1
            trip(NG - 1, 0)

        own_l = xl_tab.rearrange("(t p) f -> p t f", p=P)
        own_r = xr_tab.rearrange("(t p) f -> p t f", p=P)
        s_own = [sem("own_rows_landed0"), sem("own_rows_landed1")]
        s_seg = [sem("segment_rows_landed0"), sem("segment_rows_landed1")]
        s_sidx, s_mfree = sem("segment_index_ready"), sem("merge_buffer_free")
        s_mexp_in, s_mexp = sem("merge_exponents_ready"), sem("merge_exp_ready")
        with ExitStack() as c:
            ol, orr = sb("ol", [P, 2, TU, XW], c=c), sb("orr", [P, 2, TU, XW], c=c)
            ge, gc = sb("ge", [P, 2, TU, SW], c=c), sb("gc", [P, 2, TU, SW], c=c)
            ie, ic = sb("ie", [P, 2, TU], I32, c=c), sb("ic", [P, 2, TU], I32, c=c)
            bias = sb("gat_bias", [P, F], c=c)
            self_l, mtop, den = (sb(n, [P, TU, H], c=c) for n in ("self_l", "mtop", "den"))
            wexp = sb("wexp", [P, 3, TU, H], c=c)
            block = c.enter_context(nc.Block())

            @block.sync
            def _(sp):
                load(sp, bias[:, :], row(a["L0_gnn_bias"], F))
                def trip(g, b):
                    sp.wait_ge(s_mfree, g + 1)
                    for buf, tab in ((ol, own_l), (orr, own_r)):
                        sp.dma_start(buf[:, b, :, :], tab[:, bass.ds(g * TU, TU), :]).then_inc(s_own[b], 16)
                group_loop(sp, trip)

            @block.gpsimd
            def _(pool):
                def trip(g, b):
                    pool.wait_ge(s_mfree, g + 1)
                    alone(pool)
                    nc.gpsimd.tensor_copy(ie[:, b, :], idx_end[:, bass.ds(g * TU, TU)]).then_inc(s_sidx, 1)
                    nc.gpsimd.tensor_copy(ic[:, b, :], idx_carry[:, bass.ds(g * TU, TU)]).then_inc(s_sidx, 1)
                    pool.wait_ge(s_sidx, 2 * (g + 1))
                    alone(pool)
                    for j in range(TU):
                        for buf, ix, tab in ((ge, ie, soft_tab), (gc, ic, soft_carry)):
                            pool.indirect_dma_start(buf[:, b, j, :], None, tab,
                                                    bass.IndirectOffsetOnAxis(ix[:, b, j:j + 1], 0)).then_inc(s_seg[b], 16)
                group_loop(pool, trip)

            @block.scalar
            def _(act):
                def trip(g, b):
                    act.wait_ge(s_mexp_in, g + 1)
                    nc.scalar.activation(wexp[:, :, :, :], wexp[:, :, :, :], ACT.Exp).then_inc(s_mexp, 1)
                group_loop(act, trip)

            @block.vector
            def _(dve):
                v = chain(dve, c_v, "v")
                dve.wait_ge(loaded, total["loaded"])
                dve.sem_inc(s_mfree, 2)
                K = 22
                before = v.n
                def trip(g, b):
                    v.base, v.n = before + g * K, 0
                    fr, num = slice(0, F), lambda x: x[:, b, :, 0:F].rearrange("p t (h c) -> p t h c", h=H)
                    def step(ins):
                        v(ins)
                        v.wait()
                    dve.wait_ge(s_own[b], 16 * (g - b + 2))
                    v.wait()
                    step(nc.vector.tensor_tensor(orr[:, b], orr[:, b], ol[:, b], ALU.add))
                    step(nc.vector.tensor_scalar(orr[:, b, :, fr], orr[:, b, :, fr], 0.0, 1.0 - SLOPE, ALU.max, ALU.mult))
                    step(nc.vector.tensor_tensor(orr[:, b, :, fr], orr[:, b, :, fr],
                                                 att_b[:, :].unsqueeze(1).broadcast_to([P, TU, F]), ALU.mult))
                    step(nc.vector.tensor_reduce(self_l[:, :, :], num(orr), AX.X, ALU.add))
                    step(nc.vector.tensor_tensor(self_l[:, :, :], self_l[:, :, :], orr[:, b, :, F:XW], ALU.add))
                    dve.wait_ge(s_seg[b], 16 * TU * (g - b + 2))
                    me, mc = ge[:, b, :, F + H:SW], gc[:, b, :, F + H:SW]
                    step(nc.vector.tensor_tensor(mtop[:, :, :], me, mc, ALU.max))
                    step(nc.vector.tensor_tensor(mtop[:, :, :], mtop[:, :, :], self_l[:, :, :], ALU.max))
                    v(nc.vector.tensor_tensor(wexp[:, 0], me, mtop[:, :, :], ALU.subtract))
                    v(nc.vector.tensor_tensor(wexp[:, 1], mc, mtop[:, :, :], ALU.subtract))
                    v.wait()
                    nc.vector.tensor_tensor(wexp[:, 2], self_l[:, :, :], mtop[:, :, :], ALU.subtract).then_inc(s_mexp_in, 1)
                    dve.wait_ge(s_mexp, g + 1)
                    de, dc = ge[:, b, :, F:F + H], gc[:, b, :, F:F + H]
                    v(nc.vector.tensor_tensor(de, de, wexp[:, 0], ALU.mult))
                    step(nc.vector.tensor_tensor(dc, dc, wexp[:, 1], ALU.mult))
                    step(nc.vector.tensor_tensor(den[:, :, :], de, dc, ALU.add))
                    step(nc.vector.tensor_tensor(den[:, :, :], den[:, :, :], wexp[:, 2], ALU.add))
                    step(nc.vector.reciprocal(den[:, :, :], den[:, :, :]))
                    step(nc.vector.tensor_tensor(wexp[:, :, :, :], wexp[:, :, :, :],
                                                 den[:, :, :].unsqueeze(1).broadcast_to([P, 3, TU, H]), ALU.mult))
                    for k, x in enumerate((ge, gc, ol)):
                        v(nc.vector.tensor_tensor(num(x), num(x), wexp[:, k].unsqueeze(3).broadcast_to([P, TU, H, C]), ALU.mult))
                    xg = X[:, bass.ds(g * TU, TU), :]
                    step(nc.vector.tensor_tensor(xg, xg, bias[:, :].unsqueeze(1).broadcast_to([P, TU, F]), ALU.add))
                    step(nc.vector.tensor_tensor(ge[:, b, :, fr], ge[:, b, :, fr], gc[:, b, :, fr], ALU.add))
                    step(nc.vector.tensor_tensor(ge[:, b, :, fr], ge[:, b, :, fr], ol[:, b, :, fr], ALU.add))
                    step(nc.vector.tensor_tensor(xg, xg, ge[:, b, :, fr], ALU.add))
                    dve.sem_inc(s_mfree, 1)
                    assert v.n == K, v.n
                group_loop(dve, trip)
                total["v"] = before + NG * K

        XT = sb("XT", [P, KF, NP])
        gate = sb("gate", [P, NT, 8])

        def top_two(step, pr, eq, sels, vals, r0, kk, rank, ne):
            wide = lambda x: x[:, :].unsqueeze(2).broadcast_to([P, NT, ne])
            rk = rank[:, :].unsqueeze(1).broadcast_to([P, NT, ne])
            step(nc.vector.tensor_reduce(r0[:, :], pr[:, :, :], AX.X, ALU.add))
            step(nc.vector.reciprocal(r0[:, :], r0[:, :]))
            step(nc.vector.tensor_tensor(pr[:, :, :], pr[:, :, :], wide(r0), ALU.mult))
            for val, sel in zip(vals, sels):
                step(nc.vector.tensor_reduce(val[:, :], pr[:, :, :], AX.X, ALU.max))
                step(nc.vector.tensor_tensor(eq[:, :, :], pr[:, :, :], wide(val), ALU.is_equal))
                step(nc.vector.tensor_tensor(eq[:, :, :], eq[:, :, :], rk, ALU.mult))
                step(nc.vector.tensor_reduce(kk[:, :], eq[:, :, :], AX.X, ALU.max))
                step(nc.vector.tensor_tensor(sel[:, :, :], rk, wide(kk), ALU.is_equal))
                step(nc.vector.scalar_tensor_tensor(out=pr[:, :, :], in0=sel[:, :, :], scalar=-2.0, in1=pr[:, :, :],
                                                    op0=ALU.mult, op1=ALU.add))

        def gated(name, ne, w_in, bias_in, keep=None, more=None):
            def build(c, w, bank):
                gb = sb(f"{name}_gb", [P, 8], c=c)
                pool_more, sp_more = more(c) if more else (None, None)

                def loads(sp):
                    load(sp, w[:, :, :], w_in.rearrange("(k p) n -> p k n", p=P))
                    if bias_in is not None:
                        load(sp, gb[:, 0:ne], row(bias_in, ne))
                    if sp_more:
                        sp_more(sp)

                def consume(v, dve, mm, g, j, s_use):
                    t = bass.ds(g * TU + j, 1)
                    m = mm[:, 0:ne].unsqueeze(1)
                    if bias_in is not None:
                        if j == 0:
                            dve.wait_ge(loaded, total["loaded"])
                        nc.vector.tensor_tensor(gate[:, t, 0:ne], m, gb[:, 0:ne].unsqueeze(1), ALU.add).then_inc(s_use, 1)
                    else:
                        nc.vector.tensor_scalar(gate[:, t, 0:ne], m, 1.0, None, ALU.mult).then_inc(s_use, 1)

                def last(v, dve):
                    done(dve, s_gate_of[0], NT)
                ex = {"loads": loads, "consume": consume, "steps": 0, "last": last}
                if pool_more:
                    ex["pool"] = pool_more
                return ex
            s_gate_of = [None]

            def with_use(c, w, bank):
                ex = build(c, w, bank)
                inner = ex["consume"]

                def consume(v, dve, mm, g, j, s_use):
                    s_gate_of[0] = s_use
                    inner(v, dve, mm, g, j, s_use)
                ex["consume"] = consume
                return ex
            norm_phase(name, ne, XT, with_use, keep)

        def route_phase(name, ne, soft_top, out_bias):
            s_ex, s_exd = sem(f"{name}_exponents_ready"), sem(f"{name}_exp_ready")
            s_tp, s_wt, s_bm, s_bu = (sem(f"{name}_{n}") for n in ("weights_transposed", "weightsT_ready", "bias_product", "bias_used"))
            s_z = sem(f"{name}_bias_zeroed")
            nr = ne + 1
            with ExitStack() as c:
                G = lambda n: sb(f"{name}_{n}", [P, NT, ne], c=c)
                pr, eq, s1, s2 = G("pr"), G("eq"), G("s1"), G("s2")
                R = lambda n: sb(f"{name}_{n}", [P, NT], c=c)
                r0, v1, v2, kk = R("r0"), R("v1"), R("v2"), R("kk")
                rank = sb(f"{name}_rank", [P, ne], c=c)
                wx = sb(f"{name}_wx", [P, NT, nr], c=c)
                stage_w = sb(f"{name}_stage", [P, 2, TU * nr], c=c)
                wts = sb(f"{name}_wts", [TU * nr, 2, P], c=c)
                bd = sb(f"{name}_bd", [TU * nr, TU, F], c=c)
                tp = ps(f"{name}_tp", [P, 512], c)
                bp = ps(f"{name}_bp", [P, TU, F], c)
                block = c.enter_context(nc.Block())

                @block.gpsimd
                def _(pool):
                    nc.gpsimd.memset(bd[:, :, :], 0.0).then_inc(s_z, 1)
                    nc.gpsimd.iota(rank[:, :], [[-1, ne]], base=ne, channel_multiplier=0,
                                   allow_small_or_imprecise_dtypes=True).then_inc(s_z, 1)

                @block.sync
                def _(sp):
                    sp.wait_ge(s_z, 2)
                    for j in range(TU):
                        eb, shared = out_bias
                        load(sp, bd[j * nr:j * nr + ne, j, :], eb)
                        load(sp, bd[j * nr + ne:(j + 1) * nr, j, :], shared.rearrange("(a n) -> a n", a=1))

                @block.vector
                def _(dve):
                    v = chain(dve, c_v, "v")
                    def step(ins):
                        v(ins)
                        v.wait()
                    g = gate[:, :, 0:ne]
                    wide = lambda x: x[:, :].unsqueeze(2).broadcast_to([P, NT, ne])
                    step(nc.vector.tensor_reduce(r0[:, :], g, AX.X, ALU.max))
                    nc.vector.tensor_tensor(pr[:, :, :], g, wide(r0), ALU.subtract).then_inc(s_ex, 1)
                    dve.wait_ge(s_exd, 1)
                    dve.wait_ge(s_z, 2)
                    top_two(step, pr, eq, (s1, s2), (v1, v2), r0, kk, rank, ne)
                    if soft_top:
                        nc.vector.tensor_tensor(v2[:, :], v2[:, :], v1[:, :], ALU.subtract).then_inc(s_ex, 1)
                        dve.wait_ge(s_exd, 2)
                        step(nc.vector.memset(v1[:, :], 1.0))
                    step(nc.vector.tensor_tensor(r0[:, :], v1[:, :], v2[:, :], ALU.add))
                    step(nc.vector.reciprocal(r0[:, :], r0[:, :]))
                    step(nc.vector.tensor_tensor(s1[:, :, :], s1[:, :, :], wide(v1), ALU.mult))
                    step(nc.vector.tensor_tensor(s2[:, :, :], s2[:, :, :], wide(v2), ALU.mult))
                    step(nc.vector.tensor_tensor(s1[:, :, :], s1[:, :, :], s2[:, :, :], ALU.add))
                    step(nc.vector.tensor_tensor(g, s1[:, :, :], wide(r0), ALU.mult))
                    step(nc.vector.tensor_copy(wx[:, :, 0:ne], g))
                    step(nc.vector.memset(wx[:, :, ne:nr], 1.0))
                    before, K = v.n, 2
                    prime(dve, s_bu)
                    def trip(k, b):
                        v.base, v.n = before + k * K, 0
                        v(nc.vector.tensor_scalar(stage_w[:, b, :].rearrange("p (t e) -> p t e", t=TU),
                                                  wx[:, bass.ds(k * TU, TU), :], 1.0, None, ALU.mult))
                        dve.wait_ge(s_bm, k + 1)
                        xg = X[:, bass.ds(k * TU, TU), :]
                        v(nc.vector.tensor_tensor(xg, xg, bp[:, :, :], ALU.add))
                        dve.sem_inc(s_bu, 1)
                    group_loop(dve, trip)
                    total["v_before_bias"], total["v"] = before, before + NG * K

                @block.scalar
                def _(act):
                    act.wait_ge(s_ex, 1)
                    nc.scalar.activation(pr[:, :, :], pr[:, :, :], ACT.Exp).then_inc(s_exd, 1)
                    if soft_top:
                        act.wait_ge(s_ex, 2)
                        nc.scalar.activation(v2[:, :], v2[:, :], ACT.Exp).then_inc(s_exd, 1)
                    def trip(k, b):
                        act.wait_ge(s_tp, k + 1)
                        nc.scalar.activation(wts[:, b, :], tp[0:TU * nr, 0:P], ACT.Copy).then_inc(s_wt, 1)
                    group_loop(act, trip)

                @block.tensor
                def _(pe):
                    pe.wait_ge(loaded, total["loaded"])
                    def trip(k, b):
                        pe.wait_ge(c_v, total["v_before_bias"] + k * 2 + 1)
                        alone(pe)
                        nc.tensor.transpose(tp[0:TU * nr, 0:P], stage_w[:, b, :], ident[:, :]).then_inc(s_tp, 1)
                        pe.wait_ge(s_wt, k + 1)
                        done(pe, s_bu, k)
                        for j in range(TU):
                            m = nc.tensor.matmul(bp[:, j, :], wts[:, b, :], bd[:, j, :], start=True, stop=True)
                        m.then_inc(s_bm, 1)
                    group_loop(pe, trip)

        gated("gate0", 4, a["L0_ffn_gW"], a["L0_ffn_gb"])
        route_phase("route0", 4, True, (a["L0_ffn_eb3"], a["L0_ffn_sb3"]))

        s_a, s_ar, s_b, s_br, s_c, s_cu = (sem(n) for n in ("hidden1_product", "hidden1_ready", "hidden2_product",
                                                            "hidden2_ready", "output_product", "output_used"))
        s_bt = sem("ffn0_bias_step")
        with ExitStack() as c:
            NETS = [(2, P)] + [(1, 64)] * 4
            w1 = [sb(f"f0w1_{n}", [P, KF, ch * P], c=c) for n, (ch, _) in enumerate(NETS)]
            w2 = [sb(f"f0w2_{n}", [P, ch, h2], c=c) for n, (ch, h2) in enumerate(NETS)]
            w3 = [sb(f"f0w3_{n}", [h2, F], c=c) for n, (_, h2) in enumerate(NETS)]
            NB1 = 2 + 4 + 1 + 4
            brow, bcol = sb("f0brow", [NB1, P], c=c), sb("f0bcol", [P, NB1], c=c)
            h1 = sb("f0h1", [P, 2, 4, GW], c=c)
            h2 = sb("f0h2", [P, 2, 2 * GW], c=c)
            ap_ = [ps(f"f0a{b}", [P, 512], c) for b in range(2)]
            bp_ = [ps(f"f0b{b}", [P, 512], c) for b in range(2)]
            yp = ps("f0y", [P, TU, F], c)
            block = c.enter_context(nc.Block())
            A = [(n, hf, ch) for n, (chs, _) in enumerate(NETS) for hf in range(2) for ch in range(chs)]
            NA_, NB_, NC_ = len(A), 2 * len(NETS), len(NETS)
            first_a = {n: min(i for i, u in enumerate(A) if u[0] == n) for n in range(NC_)}
            last_a = {n: max(i for i, u in enumerate(A) if u[0] == n) for n in range(NC_)}
            ORDER = ["A0", "A1", "B0", "A2", "B1", "C0", "A3", "B2", "C1", "A4", "B3", "C2", "B4", "C3", "C4"]
            evac = [u for u in ORDER if u[0] in "AB"]

            @block.sync
            def _(sp):
                load(sp, w1[0][:, :, :], a["L0_ffn_sW1"].rearrange("(k p) n -> p k n", p=P))
                load(sp, w2[0][:, :, :], a["L0_ffn_sW2"].rearrange("(k p) n -> p k n", p=P))
                load(sp, w3[0][:, :], a["L0_ffn_sW3"])
                for n in range(4):
                    load(sp, w1[n + 1][:, :, :], a["L0_ffn_eW1"][n].rearrange("(k p) n -> p k n", p=P))
                    load(sp, w2[n + 1][:, 0, :], a["L0_ffn_eW2"][n])
                    load(sp, w3[n + 1][:, :], a["L0_ffn_eW3"][n])
                sp.wait_ge(s_bt, 1)
                load(sp, brow[0:2, :], a["L0_ffn_sb1"].rearrange("(a n) -> a n", a=2))
                load(sp, brow[2:6, :], a["L0_ffn_eb1"])
                load(sp, brow[6:7, :], a["L0_ffn_sb2"].rearrange("(a n) -> a n", a=1))
                load(sp, brow[7:11, 0:64], a["L0_ffn_eb2"])

            @block.gpsimd
            def _(pool):
                nc.gpsimd.memset(brow[:, :], 0.0).then_inc(s_bt, 1)

            @block.tensor
            def _(pe):
                pe.wait_ge(loaded, total["loaded"])
                nc.tensor.transpose(ap_[0][:, 0:NB1], brow[:, :], ident[0:NB1, 0:NB1]).then_inc(s_bt, 1)
                pe.wait_ge(s_bt, 3)
                prime(pe, s_a, s_b, s_c)
                with pe.Fori(0, NG) as g:
                    for u in ORDER:
                        n = int(u[1])
                        chs, wd = NETS[n]
                        if u[0] == "A":
                            for q in range(first_a[n], last_a[n] + 1):
                                _, hf, ch = A[q]
                                done(pe, s_ar, g * NA_ + q - 1 if q else g * NA_)
                                for k in range(KF):
                                    m = nc.tensor.matmul(ap_[q % 2][:, 0:GW], w1[n][:, k, ch * P:(ch + 1) * P],
                                                         XT[:, k, bass.ds(g * (2 * GW) + hf * GW, GW)],
                                                         start=(k == 0), stop=(k == KF - 1))
                                m.then_inc(s_a, 1)
                        elif u[0] == "B":
                            for hf in range(2):
                                q = 2 * n + hf
                                done(pe, s_ar, g * NA_ + first_a[n] + (hf + 1) * chs)
                                done(pe, s_br, g * NB_ + q - 1 if q else g * NB_)
                                for ch in range(chs):
                                    m = nc.tensor.matmul(bp_[hf][0:wd, 0:GW], w2[n][:, ch, :], h1[:, n % 2, hf * chs + ch, :],
                                                         start=(ch == 0), stop=(ch == chs - 1))
                                m.then_inc(s_b, 1)
                        else:
                            done(pe, s_br, g * NB_ + 2 * n + 2)
                            done(pe, s_cu, g * NC_ + n)
                            for j in range(TU):
                                m = nc.tensor.matmul(yp[:, j, :], h2[0:wd, n % 2, j * P:(j + 1) * P], w3[n][:, :],
                                                     start=True, stop=True)
                            m.then_inc(s_c, 1)

            @block.scalar
            def _(act):
                act.wait_ge(s_bt, 2)
                nc.scalar.activation(bcol[:, :], ap_[0][:, 0:NB1], ACT.Copy).then_inc(s_bt, 1)
                act.wait_ge(s_bt, 3)
                prime(act, s_ar, s_br)
                with act.Fori(0, NG) as g:
                    for u in evac:
                        n = int(u[1])
                        chs, wd = NETS[n]
                        if u[0] == "A":
                            for q in range(first_a[n], last_a[n] + 1):
                                _, hf, ch = A[q]
                                done(act, s_a, g * NA_ + q + 1)
                                done(act, s_b, g * NB_ + 2 * (n - 1) if n >= 2 else g * NB_)
                                bi = ch if n == 0 else 1 + n
                                nc.scalar.activation(h1[:, n % 2, hf * chs + ch, :], ap_[q % 2][:, 0:GW], ACT.Relu,
                                                     bias=bcol[:, bi:bi + 1]).then_inc(s_ar, 1)
                        else:
                            for hf in range(2):
                                done(act, s_b, g * NB_ + 2 * n + hf + 1)
                                done(act, s_c, g * NC_ + n - 1 if n >= 2 else g * NC_)
                                bi = 6 + n
                                nc.scalar.activation(h2[0:wd, n % 2, hf * GW:(hf + 1) * GW], bp_[hf][0:wd, 0:GW], ACT.Relu,
                                                     bias=bcol[0:wd, bi:bi + 1]).then_inc(s_br, 1)

            @block.vector
            def _(dve):
                v = chain(dve, c_v, "v")
                prime(dve, s_cu)
                with dve.Fori(0, NG) as g:
                    v.enter(g, NC_ * TU)
                    for n in range(NC_):
                        done(dve, s_c, g * NC_ + n + 1)
                        if n:
                            v.wait()
                        for j in range(TU):
                            xt = X[:, bass.ds(g * TU + j, 1), :]
                            y = yp[:, j:j + 1, :]
                            if n == 0:
                                v(nc.vector.tensor_tensor(xt, xt, y, ALU.add))
                            else:
                                v(nc.vector.scalar_tensor_tensor(out=xt, in0=y,
                                                                 scalar=gate[:, bass.ds(g * TU + j, 1), n - 1:n].rearrange("p a b -> p (a b)"),
                                                                 in1=xt, op0=ALU.mult, op1=ALU.add))
                        v.wait()
                        dve.sem_inc(s_cu, 1)
                    v.leave(NG)
                total["v"] = v.base + v.n

        s_xst = [sem("xp_stored0"), sem("xp_stored1")]
        s_pw = sem("proj_weight_step")

        def xp_phase(c, w, bank):
            wn = sb("wproj_rows", [P, KF, F], c=c)
            bias, rowb = sb("xp_bias", [P, F], c=c), sb("xp_row", [P, 2, F], c=c)

            def loads(sp):
                load(sp, wn[:, :, :], a["L1_gnn_W_proj"].rearrange("(o p) i -> p o i", p=P))
                for b in range(2):
                    sp.dma_start(bias[:, b * P:(b + 1) * P], row(a["L1_gnn_b_proj"][b * P:(b + 1) * P], P)).then_inc(s_xst[b], 16)

            def pe_(pe):
                for k in range(KF):
                    for o in range(KF):
                        m = nc.tensor.transpose(bank[:, (k * KF + o) * P:(k * KF + o + 1) * P],
                                                wn[:, o, k * P:(k + 1) * P], ident[:, :])
                m.then_inc(s_pw, 1)
                pe.wait_ge(s_pw, 2)

            def act_(act):
                act.wait_ge(s_pw, 1)
                nc.scalar.activation(w[:, :, :], bank[:, :].rearrange("p (k n) -> p k n", k=KF), ACT.Copy).then_inc(s_pw, 1)

            def consume(v, dve, mm, g, j, s_use):
                b = j % 2
                dve.wait_ge(s_xst[b], 16 * (g * USES[b] + j // 2 + 1))
                if j == 0:
                    dve.wait_ge(s_xst[1], 16)
                v(nc.vector.tensor_tensor(rowb[:, b, :], mm[:, 0:F], bias[:, :], ALU.add))
                v.wait()
                nc.vector.tensor_scalar(rowb[:, b, :], rowb[:, b, :], 0.0, None, ALU.max).then_inc(s_use, 1)

            def rows(sp, s_use):
                with sp.Fori(0, NG) as g:
                    for j in range(TU):
                        t, b = g * TU + j, j % 2
                        done(sp, s_use, t + 1)
                        sp.dma_start(xp_tab[bass.ds(t * P, P), :], rowb[:, b, :]).then_inc(s_xst[b], 16)
                for b in range(2):
                    sp.wait_ge(s_xst[b], 16 * (NG * USES[b] + 1))
            return {"loads": loads, "consume": consume, "steps": 1, "rows": rows, "pe": pe_, "act": act_}

        norm_phase("xp", F, XT, xp_phase)

        s_mrow = [sem(f"max_rows_landed{b}") for b in range(NB)]
        s_mst = [sem(f"max_stored{b}") for b in range(NB)]
        s_midx, s_mdone, s_mx, s_mz = (sem(n) for n in ("max_index_ready", "max_chunk_ready", "max_step", "max_neutral_ready"))
        max_rows = max_tab[0:P * EP, :].rearrange("(p e) f -> p e f", p=P)
        last_max = sb("last_max", [P, F])
        with ExitStack() as c:
            mb = sb("mb", [P, NB, T, F], c=c)
            si = sb("msi", [P, NB, T], I32, c=c)
            zero = sb("zero_row", [1, NB, F // 2], c=c)
            block = c.enter_context(nc.Block())

            @block.sync
            def _(sp):
                sp.wait_ge(s_mz, 1)
                for b in range(NB):
                    tab, r = ((max_tab, P * EP), (max_carry, P))[b // 2]
                    hb = slice((b % 2) * (F // 2), (b % 2 + 1) * (F // 2))
                    sp.dma_start(tab[r:r + 1, hb], zero[0:1, b, :]).then_inc(s_mst[b], 16)
                with sp.Fori(0, TRIPS) as i:
                    for k in range(NB):
                        sp.wait_ge(s_mdone, i * NB + k + 1)
                        sp.dma_start(max_rows[:, bass.ds((i * NB + k) * T, T), :], mb[:, k, :, :]).then_inc(s_mst[k], 16)
                for b in range(NB):
                    sp.wait_ge(s_mst[b], 16 * (TRIPS + 1))

            @block.gpsimd
            def _(pool):
                nc.gpsimd.memset(zero[:, :, :], 0.0).then_inc(s_mz, 1)
                with pool.Fori(0, TRIPS) as i:
                    for b in range(NB):
                        pool.wait_ge(s_mst[b], 16 * (i + 1))
                        alone(pool)
                        nc.gpsimd.tensor_copy(si[:, b, :], src_i[:, bass.ds((i * NB + b) * T, T)]).then_inc(s_midx, 1)
                        pool.wait_ge(s_midx, i * NB + b + 1)
                        alone(pool)
                        for t in range(T):
                            pool.indirect_dma_start(mb[:, b, t, :], None, xp_tab,
                                                    bass.IndirectOffsetOnAxis(si[:, b, t:t + 1], 0)).then_inc(s_mrow[b], 16)

            @block.vector
            def _(dve):
                v = chain(dve, c_v, "v")
                v(nc.vector.memset(last_max[:, :], 0.0))
                v.wait()
                with dve.Fori(0, TRIPS) as i:
                    for k in range(NB):
                        dve.wait_ge(s_mrow[k], 16 * T * (i + 1))
                        for t in range(T):
                            n = (i * NB + k) * T + t
                            prev = mb[:, k, t - 1, :] if t else last_max[:, :]
                            if t or k:
                                dve.wait_ge(s_mx, n)
                            e = n
                            nc.vector.scalar_tensor_tensor(out=mb[:, k, t, :], in0=prev, scalar=keep[:, bass.ds(e, 1)],
                                                           in1=mb[:, k, t, :], op0=ALU.mult, op1=ALU.max).then_inc(s_mx, 1)
                        dve.wait_ge(s_mx, (i * NB + k + 1) * T)
                        nc.vector.tensor_copy(last_max[:, :], mb[:, k, T - 1, :]).then_inc(s_mdone, 1)
                        dve.wait_ge(s_mdone, i * NB + k + 1)
                v.wait()
                total["v"] = v.n

        s_mc = sem("max_carry_step")
        with ExitStack() as c:
            kc = sb("kc", [P, P], c=c)
            cm = sb("cm", [P, KF, P], c=c)
            crow = sb("mcrow", [P, F], c=c)
            ft = ps("ft", [P, 512], c)
            bk = ps("bk", [P, 512], c)
            block = c.enter_context(nc.Block())

            @block.tensor
            def _(pe):
                for k in range(KF):
                    m = nc.tensor.transpose(ft[:, k * P:(k + 1) * P], last_max[:, k * P:(k + 1) * P], ident[:, :])
                m.then_inc(s_mc, 1)
                pe.wait_ge(s_mc, 3)
                for k in range(KF):
                    m = nc.tensor.transpose(bk[:, k * P:(k + 1) * P], cm[:, k, :], ident[:, :])
                m.then_inc(s_mc, 1)

            @block.vector
            def _(dve):
                v = chain(dve, c_v, "v")
                v(nc.vector.memset(kc[:, 0:1], 0.0))
                v(nc.vector.tensor_tensor(kc[:, 1:P], dl_row[:, 1:P], dl_row[:, 0:P - 1], ALU.is_equal))
                v.wait()
                dve.wait_ge(s_mc, 1)
                for k in range(KF):
                    nc.vector.tensor_tensor_scan(cm[:, k, :], kc[:, :], ft[:, k * P:(k + 1) * P], 0.0,
                                                 ALU.mult, ALU.max).then_inc(s_mc, 1)
                dve.wait_ge(s_mc, 4)
                nc.vector.tensor_copy(crow[:, :], bk[:, 0:F]).then_inc(s_mc, 1)
                v.wait()
                total["v"] = v.n

            @block.sync
            def _(sp):
                sp.wait_ge(s_mc, 5)
                store(sp, max_carry[0:P, :], crow[:, :])
                sp.wait_ge(stored, total["stored"])

        own_x = xp_tab.rearrange("(t p) f -> p t f", p=P)
        s_ow = [sem("own_xp_landed0"), sem("own_xp_landed1")]
        s_sg = [sem("max_segment_landed0"), sem("max_segment_landed1")]
        (s_ix, s_fr, s_ag, s_at, s_as, s_lp, s_lo, s_w2, s_gfree) = (sem(n) for n in (
            "max_segment_index_ready", "aggregate_buffer_free", "aggregate_ready", "aggregate_transposed",
            "aggregateT_ready", "layer_product", "layer_out_ready", "layer_weight_step", "aggregate_transposed_group"))
        with ExitStack() as c:
            ox = sb("ox", [P, 2, TU, F], c=c)
            ge, gc = sb("mge", [P, 2, TU, F], c=c), sb("mgc", [P, 2, TU, F], c=c)
            ie, ic = sb("mie", [P, 2, TU], I32, c=c), sb("mic", [P, 2, TU], I32, c=c)
            wn = sb("wlr_rows", [P, 2, KF, F], c=c)
            wt = sb("wlr_t", [P, 2, KF, F], c=c)
            bl = sb("bl", [P, KF], c=c)
            ags = sb("ags", [P, 2, KF, P], c=c)
            tb = [ps(f"ltb{b}", [P, 512], c) for b in range(2)]
            ob = [ps(f"lob{b}", [P, 512], c) for b in range(2)]
            block = c.enter_context(nc.Block())

            @block.sync
            def _(sp):
                load(sp, wn[:, 0], a["L1_gnn_W_l"].rearrange("(o p) i -> p o i", p=P))
                load(sp, wn[:, 1], a["L1_gnn_W_r"].rearrange("(o p) i -> p o i", p=P))
                with nc.allow_non_contiguous_dma(reason="256 values"):
                    load(sp, bl[:, :], a["L1_gnn_b_l"].rearrange("(k p) -> p k", p=P))
                def trip(g, b):
                    sp.wait_ge(s_fr, g + 1)
                    sp.dma_start(ox[:, b, :, :], own_x[:, bass.ds(g * TU, TU), :]).then_inc(s_ow[b], 16)
                group_loop(sp, trip)

            @block.gpsimd
            def _(pool):
                def trip(g, b):
                    pool.wait_ge(s_fr, g + 1)
                    alone(pool)
                    nc.gpsimd.tensor_copy(ie[:, b, :], idx_end[:, bass.ds(g * TU, TU)]).then_inc(s_ix, 1)
                    nc.gpsimd.tensor_copy(ic[:, b, :], idx_carry[:, bass.ds(g * TU, TU)]).then_inc(s_ix, 1)
                    pool.wait_ge(s_ix, 2 * (g + 1))
                    alone(pool)
                    for j in range(TU):
                        for buf, ix, tab in ((ge, ie, max_tab), (gc, ic, max_carry)):
                            pool.indirect_dma_start(buf[:, b, j, :], None, tab,
                                                    bass.IndirectOffsetOnAxis(ix[:, b, j:j + 1], 0)).then_inc(s_sg[b], 16)
                group_loop(pool, trip)

            @block.vector
            def _(dve):
                v = chain(dve, c_v, "v")
                before, K = v.n, 1
                def trip(g, b):
                    v.base, v.n = before + g * K, 0
                    dve.wait_ge(s_ow[b], 8 * (g - b + 2))
                    dve.wait_ge(s_sg[b], 16 * TU * (g - b + 2))
                    v(nc.vector.tensor_tensor(ge[:, b], ge[:, b], gc[:, b], ALU.max))
                    v.wait()
                    nc.vector.tensor_tensor(ge[:, b], ge[:, b], ox[:, b], ALU.max).then_inc(s_ag, 1)
                group_loop(dve, trip)
                total["v"] = before + NG * K

            @block.tensor
            def _(pe):
                pe.wait_ge(loaded, total["loaded"])
                for s in range(2):
                    for k in range(KF):
                        for o in range(KF):
                            m = nc.tensor.transpose(tb[s][:, (k * KF + o) * P:(k * KF + o + 1) * P],
                                                    wn[:, s, o, k * P:(k + 1) * P], ident[:, :])
                m.then_inc(s_w2, 1)
                pe.wait_ge(s_w2, 3)
                pe.sem_inc(s_fr, 2)
                prime(pe, s_at, s_lp)
                def trip(g, b):
                    pe.wait_ge(s_ag, g + 1)
                    def turn(j):
                        q = j % 2
                        done(pe, s_as, g * TU + j - 1 if j >= 2 else g * TU)
                        for k in range(KF):
                            m = nc.tensor.transpose(tb[q][:, k * P:(k + 1) * P], ge[:, b, j, k * P:(k + 1) * P], ident[:, :])
                        m.then_inc(s_at, 1)
                    turn(0)
                    for j in range(TU):
                        t, q = g * TU + j, j % 2
                        if j + 1 < TU:
                            turn(j + 1)
                        done(pe, s_as, t + 1)
                        done(pe, s_lo, t - 1 if j >= 2 else g * TU)
                        for o in range(KF):
                            for k in range(KF):
                                nc.tensor.matmul(ob[q][:, o * P:(o + 1) * P], wt[:, 0, k, o * P:(o + 1) * P], ags[:, q, k, :],
                                                 start=(k == 0), stop=False)
                            for k in range(KF):
                                m = nc.tensor.matmul(ob[q][:, o * P:(o + 1) * P], wt[:, 1, k, o * P:(o + 1) * P],
                                                     XT[:, k, bass.ds(t * P, P)], start=False, stop=(k == KF - 1))
                        m.then_inc(s_lp, 1)
                    pe.wait_ge(s_as, g * TU + TU + 1)
                    pe.sem_inc(s_fr, 1)
                group_loop(pe, trip)

            @block.scalar
            def _(act):
                act.wait_ge(s_w2, 1)
                for s in range(2):
                    nc.scalar.activation(wt[:, s, :, :], tb[s][:, :].rearrange("p (k n) -> p k n", k=KF), ACT.Copy).then_inc(s_w2, 1)
                act.wait_ge(loaded, total["loaded"])
                prime(act, s_as, s_lo)
                def trip(g, b):
                    def take(j):
                        done(act, s_at, g * TU + j + 1)
                        done(act, s_lp, g * TU + j - 1 if j >= 2 else g * TU)
                        nc.scalar.activation(ags[:, j % 2, :, :], tb[j % 2][:, 0:F].rearrange("p (k n) -> p k n", k=KF),
                                             ACT.Copy).then_inc(s_as, 1)
                    take(0)
                    for j in range(TU):
                        t, q = g * TU + j, j % 2
                        if j + 1 < TU:
                            take(j + 1)
                        done(act, s_lp, t + 1)
                        alone(act)
                        for o in range(KF):
                            m = nc.scalar.activation(XT[:, o, bass.ds(t * P, P)], ob[q][:, o * P:(o + 1) * P], ACT.Relu,
                                                     bias=bl[:, o:o + 1])
                        m.then_inc(s_lo, 1)
                group_loop(act, trip)

        SC = 250
        assert N % SC == 0
        s_bst, s_bp, s_bq, s_nx, s_nt, s_nu = (sem(n) for n in ("bn_stats_step", "bn_var_ready", "bn_std_ready", "bn_scaled",
                                                               "bn_transposed", "bn_added"))
        with ExitStack() as c:
            st6 = sb("bn6", [P, KF, N // SC, 6], c=c)
            mv = sb("bnmv", [P, KF, 2], c=c)
            gm, bt = sb("gm", [P, KF], c=c), sb("bt", [P, KF], c=c)
            scl, shf = sb("scl", [P, KF], c=c), sb("shf", [P, KF], c=c)
            nx = sb("nx", [P, 2, KF, P], c=c)
            nb_ = [ps(f"bnb{b}", [P, 512], c) for b in range(2)]
            block = c.enter_context(nc.Block())

            @block.sync
            def _(sp):
                with nc.allow_non_contiguous_dma(reason="256 values each"):
                    load(sp, gm[:, :], a["L1_gnn_gamma"].rearrange("(k p) -> p k", p=P))
                    load(sp, bt[:, :], a["L1_gnn_beta"].rearrange("(k p) -> p k", p=P))

            @block.scalar
            def _(act):
                prime(act, s_nx)
                act.wait_ge(s_bp, 1)
                nc.scalar.activation(scl[:, :], mv[:, :, 1], ACT.Sqrt).then_inc(s_bq, 1)
                act.wait_ge(s_bp, 2)
                with act.Fori(0, NG) as g:
                    for j in range(TU):
                        t, q = g * TU + j, j % 2
                        done(act, s_nt, t - 1 if j >= 2 else g * TU)
                        alone(act)
                        for k in range(KF):
                            m = nc.scalar.activation(nx[:, q, k, :], XT[:, k, bass.ds(t * P, P)], ACT.Identity,
                                                     scale=scl[:, k:k + 1], bias=shf[:, k:k + 1])
                        m.then_inc(s_nx, 1)

            @block.tensor
            def _(pe):
                prime(pe, s_nt)
                with pe.Fori(0, NG) as g:
                    for j in range(TU):
                        t, q = g * TU + j, j % 2
                        done(pe, s_nx, t + 1)
                        done(pe, s_nu, t - 1 if j >= 2 else g * TU)
                        for k in range(KF):
                            m = nc.tensor.transpose(nb_[q][:, k * P:(k + 1) * P], nx[:, q, k, :], ident[:, :])
                        m.then_inc(s_nt, 1)

            @block.vector
            def _(dve):
                v = chain(dve, c_v, "v")
                prime(dve, s_nu)
                for k in range(KF):
                    for n in range(N // SC):
                        v(nc.vector.bn_stats(st6[:, k, n, :], XT[:, k, n * SC:(n + 1) * SC]))
                v.wait()
                for k in range(KF):
                    v(nc.vector.bn_aggr(mv[:, k, :], st6[:, k, :, :]))
                v.wait()
                nc.vector.tensor_scalar(mv[:, :, 1], mv[:, :, 1], 1e-5, None, ALU.add).then_inc(s_bp, 1)
                dve.wait_ge(s_bq, 1)
                dve.wait_ge(loaded, total["loaded"])
                for ins in (lambda: nc.vector.reciprocal(scl[:, :], scl[:, :]),
                            lambda: nc.vector.tensor_tensor(scl[:, :], scl[:, :], gm[:, :], ALU.mult),
                            lambda: nc.vector.tensor_tensor(shf[:, :], scl[:, :], mv[:, :, 0], ALU.mult)):
                    v(ins())
                    v.wait()
                nc.vector.tensor_tensor(shf[:, :], bt[:, :], shf[:, :], ALU.subtract).then_inc(s_bp, 1)
                with dve.Fori(0, NG) as g:
                    for j in range(TU):
                        t, q = g * TU + j, j % 2
                        done(dve, s_nt, t + 1)
                        xt = X[:, bass.ds(t, 1), :]
                        nc.vector.tensor_tensor(xt, xt, nb_[q][:, 0:F].unsqueeze(1), ALU.add).then_inc(s_nu, 1)
                done(dve, s_nu, NT)
                total["v"] = v.n


        NE, FH = 8, 1024
        NF = FH // P
        ST = 2 * P
        MT = -(-(2 * NP + NE * (ST - 1)) // ST)
        ET = -(-NP // ST)
        assert MT % 2 == 1 and NP < 2 ** 24
        slot_x, slot_y = dram("slot_x", (MT * ST, F)), dram("slot_y", (MT * ST, F))
        bias_tab = dram("bias_tab", (NE, P, NF))
        pos = [sb(f"slot{k}", [P, NT], I32) for k in range(2)]
        wsel = [sb(f"weight{k}", [P, NT]) for k in range(2)]
        tile_e = sb("tile_e", [P, MT], I32)
        sbcol = sb("sbcol", [P, NF])
        mean1, rstd1 = sb("mean1", [P, NT]), sb("rstd1", [P, NT])
        s_zr, s_zf = sem("slot_zeros_ready"), sem("slots_zeroed")

        def zero_slots(c):
            zt = sb("slot_zeros", [P, 6, F], c=c)
            def pool_(pool):
                nc.gpsimd.memset(zt[:, :, :], 0.0).then_inc(s_zr, 1)
            def sp_(sp):
                sp.wait_ge(s_zr, 1)
                view = slot_x.rearrange("(p q) f -> p q f", p=P)
                for q in range(0, MT * ST // P, 6):
                    sp.dma_start(view[:, q:q + 6, :], zt[:, :, :]).then_inc(s_zf, 16)
            assert MT * ST // P % 6 == 0
            return pool_, sp_
        gated("gate1", 8, a["L1_ffn_Wr"], None, keep=(mean1, rstd1), more=zero_slots)

        s_sh, s_shr, s_sh2, s_sy, s_syu = (sem(n) for n in ("shared_hidden_product", "shared_hidden_ready", "shared_hidden_used",
                                                            "shared_out_ready", "shared_out_used"))

        class Shared:
            def __init__(self, c, tag):
                self.w1 = sb("shw1" + tag, [P, KF, FH], c=c)
                self.w2 = sb("shw2" + tag, [P, NF, F], c=c)
                self.ht = sb("shht" + tag, [P, 2, 2 * GW], c=c)
                self.hp = [ps(f"shh{b}" + tag, [P, 2, 512], c) for b in range(1)]
                self.yp = ps("shy" + tag, [P, TU, F], c)
                self.h_at = lambda f, hf: self.hp[0][:, hf, 0:GW]

            def loads(self, sp):
                load(sp, self.w1[:, :, :], a["L1_ffn_W1s"].rearrange("(k p) n -> p k n", p=P))
                load(sp, self.w2[:, :, :], a["L1_ffn_W2s"].rearrange("(k p) n -> p k n", p=P))

            def pe(self, pe, g0, g1):
                with pe.Fori(g0, g1) as g:
                    for f in range(NF + 1):
                        if f < NF:
                            for hf in range(2):
                                done(pe, s_shr, (g * NF + f) * 2 + hf - 1 if f or hf else g * NF * 2)
                                for k in range(KF):
                                    m = nc.tensor.matmul(self.h_at(f, hf), self.w1[:, k, f * P:(f + 1) * P],
                                                         XT[:, k, bass.ds(g * (2 * GW) + hf * GW, GW)],
                                                         start=(k == 0), stop=(k == KF - 1))
                                m.then_inc(s_sh, 1)
                        if f >= 1:
                            q = f - 1
                            done(pe, s_shr, (g * NF + q + 1) * 2)
                            if q == 0:
                                done(pe, s_syu, g)
                            for j in range(TU):
                                m = nc.tensor.matmul(self.yp[:, j, :], self.ht[:, q % 2, j * P:(j + 1) * P], self.w2[:, q, :],
                                                     start=(q == 0 and j % 2 == 0),
                                                     stop=(q == NF - 1 and (j % 2 == 1 or j == TU - 1)))
                            m.then_inc(s_sh2 if q < NF - 1 else s_sy, 1)

            def act(self, act, g0, g1):
                with act.Fori(g0, g1) as g:
                    for f in range(NF):
                        for hf in range(2):
                            done(act, s_sh, (g * NF + f) * 2 + hf + 1)
                            if f >= 2:
                                done(act, s_sh2, g * (NF - 1) + f - 1)
                            elif f == 0:
                                done(act, s_sh2, g * (NF - 1))
                            else:
                                done(act, s_sy, g)
                            nc.scalar.activation(self.ht[:, f % 2, hf * GW:(hf + 1) * GW], self.h_at(f, hf),
                                                 ACT.Gelu, bias=sbcol[:, f:f + 1]).then_inc(s_shr, 1)

            def dve(self, dve, v, g):
                done(dve, s_sy, g + 1)
                xg = X[:, g * TU:(g + 1) * TU, :]
                v.wait()
                nc.vector.tensor_tensor(xg, xg, self.yp[:, :, :], ALU.add).then_inc(s_syu, 1)
                done(dve, s_syu, g + 1)

        G0 = 4
        s_rt, s_rte = sem("routing_step"), sem("gates_exp_ready")
        s_nr, s_pi, s_sc = sem("normalized_rows_ready"), sem("slot_index_ready"), [sem("rows_scattered0"), sem("rows_scattered1")]
        with ExitStack() as c:
            sh = Shared(c, "a")
            brow, bcol = sb("f1brow", [(NE + 1) * NF, P], c=c), sb("f1bcol", [P, (NE + 1) * NF], c=c)
            b2s = sb("f1b2s", [P, F], c=c)
            low = sb("low", [P, P], c=c)
            G = lambda n: sb(f"r1_{n}", [P, NT, NE], c=c)
            pr, eq, s1, s2, sel, tot, rk_ = G("pr"), G("eq"), G("s1"), G("s2"), G("sel"), G("tot"), G("rk")
            incl = sb("r1_incl", [P, NE, NT], c=c)
            R = lambda n: sb(f"r1_{n}", [P, NT], c=c)
            r0, v1, v2, kk, onest = R("r0"), R("v1"), R("v2"), R("kk"), R("ones")
            rank = sb("r1_rank", [P, NE], c=c)
            thr, cmp_ = sb("r1_thr", [P, ET], c=c), sb("r1_cmp", [P, NE, ET], c=c)
            ntl, tend, base = (sb(f"r1_{n}", [P, NE], c=c) for n in ("ntl", "tend", "base"))
            tno, tcm, tex = sb("r1_tno", [P, MT], c=c), sb("r1_tcm", [P, MT, NE], c=c), sb("r1_tex", [P, MT], c=c)
            xrow = sb("r1_xrow", [P, 2, TU, F], c=c)
            pi = sb("r1_pi", [P, 2, 2, TU], I32, c=c)
            rp = ps("r1_rp", [P, 2, 512], c)
            block = c.enter_context(nc.Block())

            @block.sync
            def _(sp):
                sh.loads(sp)
                load(sp, brow[0:NF, :], a["L1_ffn_b1s"].rearrange("(c p) -> c p", p=P))
                load(sp, brow[NF:, :], a["L1_ffn_b1p"].rearrange("e (c p) -> (e c) p", p=P))
                load(sp, b2s[:, :], row(a["L1_ffn_b2s"], F))
                sp.wait_ge(s_rt, 7)
                store(sp, bias_tab.rearrange("e p c -> p e c"), bcol[:, NF:].rearrange("p (e c) -> p e c", e=NE))
                sp.wait_ge(stored, total["stored"])

            @block.gpsimd
            def _(pool):
                for out_, pat, b_ in ((rank[:, :], [[-1, NE]], NE), (thr[:, :], [[ST, ET]], 0), (tno[:, :], [[1, MT]], 0)):
                    nc.gpsimd.iota(out_, pat, base=b_, channel_multiplier=0, allow_small_or_imprecise_dtypes=True).then_inc(s_rt, 1)
                nc.gpsimd.affine_select(out=low[:, :], in_=ones[:, :], compare_op=ALU.is_gt, fill=0.0,
                                        base=0, pattern=[[1, P]], channel_multiplier=-1).then_inc(s_rt, 1)
                nc.gpsimd.memset(onest[:, :], 1.0).then_inc(s_rt, 1)
                pool.wait_ge(s_zf, 16 * (MT * ST // P // 6))
                pool.wait_ge(s_rt, 11)
                def trip(g, b):
                    pool.wait_ge(s_nr, g + 1)
                    alone(pool)
                    for k in range(2):
                        nc.gpsimd.tensor_copy(pi[:, b, k, :], pos[k][:, bass.ds(g * TU, TU)]).then_inc(s_pi, 1)
                    pool.wait_ge(s_pi, 2 * (g + 1))
                    alone(pool)
                    for j in range(TU):
                        for k in range(2):
                            pool.indirect_dma_start(slot_x, bass.IndirectOffsetOnAxis(pi[:, b, k, j:j + 1], 0),
                                                    xrow[:, b, j, :], None).then_inc(s_sc[b], 16)
                group_loop(pool, trip)
                for b in range(2):
                    pool.wait_ge(s_sc[b], 32 * TU * ((NG + 1 - b) // 2))

            @block.tensor
            def _(pe):
                pe.wait_ge(loaded, total["loaded"])
                nb1 = (NE + 1) * NF
                pe.wait_ge(s_rt, 5)
                nc.tensor.transpose(rp[:, 0, 0:nb1], brow[:, :], ident[0:nb1, 0:nb1]).then_inc(s_rt, 1)
                prime(pe, s_sh, s_sh2, s_sy)
                pe.wait_ge(s_rt, 7)
                sh.pe(pe, 0, 1)
                pe.wait_ge(s_rt, 9)
                nc.tensor.matmul(rp[:, 0, 0:NT * NE], low[:, :], sel[:, :, :].rearrange("p t e -> p (t e)"), start=True, stop=True)
                nc.tensor.matmul(rp[:, 1, 0:NT * NE], ones[:, :], sel[:, :, :].rearrange("p t e -> p (t e)"),
                                 start=True, stop=True).then_inc(s_rt, 1)
                sh.pe(pe, 1, G0)

            @block.scalar
            def _(act):
                act.wait_ge(s_rt, 6)
                nc.scalar.activation(sbcol[:, :], rp[:, 0, 0:NF], ACT.Copy).then_inc(s_rte, 1)
                nc.scalar.activation(bcol[:, :], rp[:, 0, 0:(NE + 1) * NF], ACT.Copy).then_inc(s_rt, 1)
                prime(act, s_shr)
                act.wait_ge(s_rt, 8)
                nc.scalar.activation(pr[:, :, :], pr[:, :, :], ACT.Exp).then_inc(s_rte, 1)
                sh.act(act, 0, G0)

            @block.vector
            def _(dve):
                v = chain(dve, c_v, "v")
                def step(ins):
                    v(ins)
                    v.wait()
                prime(dve, s_syu)
                g = gate[:, :, 0:NE]
                wide = lambda x: x[:, :].unsqueeze(2).broadcast_to([P, NT, NE])
                step(nc.vector.tensor_reduce(r0[:, :], g, AX.X, ALU.max))
                dve.wait_ge(s_rt, 7)
                nc.vector.tensor_tensor(pr[:, :, :], g, wide(r0), ALU.subtract).then_inc(s_rt, 1)
                dve.wait_ge(s_rte, 2)
                top_two(step, pr, eq, (s1, s2), (v1, v2), r0, kk, rank, NE)
                step(nc.vector.tensor_tensor(r0[:, :], v1[:, :], v2[:, :], ALU.add))
                step(nc.vector.reciprocal(r0[:, :], r0[:, :]))
                step(nc.vector.tensor_tensor(wsel[0][:, :], v1[:, :], r0[:, :], ALU.mult))
                step(nc.vector.tensor_tensor(wsel[1][:, :], v2[:, :], r0[:, :], ALU.mult))
                nc.vector.tensor_tensor(sel[:, :, :], s1[:, :, :], s2[:, :, :], ALU.add).then_inc(s_rt, 1)
                dve.wait_ge(s_rt, 10)
                pe_view = lambda k: rp[:, k, 0:NT * NE].rearrange("p (t e) -> p t e", e=NE)
                step(nc.vector.tensor_copy(tot[:, :, :], pe_view(1)))
                for e in range(NE):
                    v(nc.vector.tensor_tensor_scan(incl[:, e, :], onest[:, :], tot[:, :, e], 0.0, ALU.mult, ALU.add))
                v.wait()
                step(nc.vector.tensor_tensor(cmp_[:, :, :], incl[:, :, NT - 1:NT].broadcast_to([P, NE, ET]),
                                             thr[:, :].unsqueeze(1).broadcast_to([P, NE, ET]), ALU.is_gt))
                step(nc.vector.tensor_reduce(ntl[:, :], cmp_[:, :, :], AX.X, ALU.add))
                step(nc.vector.tensor_tensor_scan(tend[:, :], onest[:, 0:NE], ntl[:, :], 0.0, ALU.mult, ALU.add))
                step(nc.vector.tensor_tensor(base[:, :], tend[:, :], ntl[:, :], ALU.subtract))
                step(nc.vector.tensor_scalar(base[:, :], base[:, :], float(ST), None, ALU.mult))
                step(nc.vector.tensor_tensor(rk_[:, :, :], pe_view(0), tot[:, :, :], ALU.subtract))
                step(nc.vector.tensor_tensor(rk_[:, :, :], rk_[:, :, :], incl[:, :, :].rearrange("p e t -> p t e"), ALU.add))
                step(nc.vector.tensor_tensor(rk_[:, :, :], rk_[:, :, :], base[:, :].unsqueeze(1).broadcast_to([P, NT, NE]), ALU.add))
                for k, s in enumerate((s1, s2)):
                    step(nc.vector.tensor_tensor(s[:, :, :], s[:, :, :], rk_[:, :, :], ALU.mult))
                    step(nc.vector.tensor_reduce(r0[:, :], s[:, :, :], AX.X, ALU.add))
                    step(nc.vector.tensor_copy(pos[k][:, :], r0[:, :]))
                step(nc.vector.tensor_tensor(tcm[:, :, :], tend[:, :].unsqueeze(1).broadcast_to([P, MT, NE]),
                                             tno[:, :].unsqueeze(2).broadcast_to([P, MT, NE]), ALU.is_le))
                step(nc.vector.tensor_reduce(tex[:, :], tcm[:, :, :], AX.X, ALU.add))
                step(nc.vector.tensor_scalar(tex[:, :], tex[:, :], float(NE - 1), None, ALU.min))
                step(nc.vector.tensor_copy(tile_e[:, :], tex[:, :]))
                dve.sem_inc(s_rt, 1)
                def rows(g):
                    b = g % 2
                    if g >= 2:
                        dve.wait_ge(s_sc[b], 32 * TU * (g // 2))
                    xg = X[:, g * TU:(g + 1) * TU, :]
                    cols = slice(g * TU, (g + 1) * TU)
                    for j in range(TU):
                        t = g * TU + j
                        v(nc.vector.tensor_scalar(xrow[:, b, j, :], X[:, t, :], mean1[:, t:t + 1], rstd1[:, t:t + 1],
                                                  ALU.subtract, ALU.mult))
                    v.wait()
                    dve.sem_inc(s_nr, 1)
                    step(nc.vector.tensor_tensor(xg, xg, b2s[:, :].unsqueeze(1).broadcast_to([P, TU, F]), ALU.add))
                dve.wait_ge(loaded, total["loaded"])
                for g in range(NG):
                    rows(g)
                    if g % 2 == 1 or g == NG - 1:
                        sh.dve(dve, v, g // 2 if g < NG - 1 else G0 - 1)
                total["v"] = v.n


        s_wl = [sem("expert_weights_landed0"), sem("expert_weights_landed1")]
        s_xl = [sem("slot_rows_landed0"), sem("slot_rows_landed1")]
        s_ys = [sem("expert_rows_stored0"), sem("expert_rows_stored1")]
        s_xtp, s_xts, s_h, s_hr, s_h2, s_y, s_yr = (sem(n) for n in (
            "slot_x_transposed", "slot_xT_ready", "hidden_product", "hidden_ready", "hidden_used", "expert_out_ready", "expert_rows_ready"))
        with ExitStack() as c:
            w1, w2 = sb("ew1", [P, 2, KF, FH], c=c), sb("ew2", [P, 2, NF, F], c=c)
            b1, b2 = sb("eb1", [P, 2, NF], c=c), sb("eb2", [P, 2, F], c=c)
            xs, xt = sb("xs", [P, 2, 2, F], c=c), sb("xt", [P, 2, KF, ST], c=c)
            ht = sb("eht", [P, 2, ST], c=c)
            yr = sb("yr", [P, 2, 2, F], c=c)
            hp = [ps(f"eh{b}", [P, 512], c) for b in range(2)]
            yp = [ps(f"ey{b}", [P, 2, F], c) for b in range(2)]
            tp = [ps(f"etp{b}", [P, KF, ST], c) for b in range(2)]
            slots = slot_x.rearrange("(n q p) f -> n p q f", p=P, q=2)
            slots_y = slot_y.rearrange("(n q p) f -> n p q f", p=P, q=2)
            block = c.enter_context(nc.Block())
            PER = 16 * 4

            def tiles(eng, one):
                with eng.Fori(0, MT // 2) as i:
                    one(i * 2, 0)
                    one(i * 2 + 1, 1)
                one(MT - 1, 0)

            @block.sync
            def _(sp):
                def one(n, b):
                    sp.wait_ge(s_yr, n + 1)
                    e = sp.value_load(tile_e[0:1, bass.ds(n, 1)], min_val=0, max_val=NE - 1)
                    sp.dma_start(xs[:, b], slots[bass.ds(n, 1)].rearrange("n p q f -> (n p) q f")).then_inc(s_xl[b], 16)
                    for dst, src in ((w1[:, b], a["L1_ffn_W1p"][bass.ds(e, 1)].rearrange("e (k p) n -> p (e k) n", p=P)),
                                     (w2[:, b], a["L1_ffn_W2p"][bass.ds(e, 1)].rearrange("e (k p) n -> p (e k) n", p=P)),
                                     (b1[:, b], bias_tab[bass.ds(e, 1)].rearrange("e p c -> (e p) c")),
                                     (b2[:, b], a["L1_ffn_b2p"][bass.ds(e, 1)].broadcast_to([P, F]))):
                        sp.dma_start(dst, src).then_inc(s_wl[b], 16)
                tiles(sp, one)

            @block.tensor
            def _(pe):
                prime(pe, s_y, s_h, s_h2, s_xtp)
                def turn(n, b):
                    pe.wait_ge(s_xl[b], 8 * (n - b + 2))
                    for q in range(2):
                        for k in range(KF):
                            m = nc.tensor.transpose(tp[b][:, k, q * P:(q + 1) * P], xs[:, b, q, k * P:(k + 1) * P], ident[:, :])
                    m.then_inc(s_xtp, 1)
                turn(0, 0)
                def one(n, b):
                    pe.wait_ge(s_wl[b], (PER // 2) * (n - b + 2))
                    done(pe, s_xts, n + 1)
                    for f in range(NF + 1):
                        if f == NF // 2 and not isinstance(n, int):
                            turn(n + 1, 1 - b)
                        if f < NF:
                            done(pe, s_hr, n * NF + f - 1 if f else n * NF)
                            for k in range(KF):
                                m = nc.tensor.matmul(hp[f % 2][:, 0:ST], w1[:, b, k, f * P:(f + 1) * P], xt[:, b, k, :],
                                                     start=(k == 0), stop=(k == KF - 1))
                            m.then_inc(s_h, 1)
                        if f >= 1:
                            q = f - 1
                            done(pe, s_hr, n * NF + q + 1)
                            if q == 0:
                                pe.wait_ge(s_yr, n + 1)
                            for j in range(2):
                                m = nc.tensor.matmul(yp[b][:, j, :], ht[:, q % 2, j * P:(j + 1) * P], w2[:, b, q, :],
                                                     start=(q == 0 and j == 0), stop=(q == NF - 1 and j == 1))
                            m.then_inc(s_h2 if q < NF - 1 else s_y, 1)
                tiles(pe, one)

            @block.scalar
            def _(act):
                prime(act, s_hr)
                def one(n, b):
                    act.wait_ge(s_wl[b], (PER // 2) * (n - b + 2))
                    for f in range(NF):
                        done(act, s_h, n * NF + f + 1)
                        if f >= 2:
                            done(act, s_h2, n * (NF - 1) + f - 1)
                        elif f == 0:
                            done(act, s_h2, n * (NF - 1))
                        else:
                            done(act, s_y, n)
                        nc.scalar.activation(ht[:, f % 2, :], hp[f % 2][:, 0:ST], ACT.Gelu,
                                             bias=b1[:, b, f:f + 1]).then_inc(s_hr, 1)
                tiles(act, one)

            @block.vector
            def _(dve):
                prime(dve, s_xts)
                dve.sem_inc(s_yr, 2)
                def take(n, b):
                    done(dve, s_xtp, n + 1)
                    nc.vector.tensor_copy(xt[:, b], tp[b][:, :, :]).then_inc(s_xts, 1)
                take(0, 0)
                def one(n, b):
                    if not isinstance(n, int):
                        take(n + 1, 1 - b)
                    done(dve, s_y, n + 1)
                    dve.wait_ge(s_ys[b], 8 * (n - b + 2))
                    nc.vector.tensor_tensor(yr[:, b], yp[b][:, :, :], b2[:, b].unsqueeze(1).broadcast_to([P, 2, F]),
                                            ALU.add).then_inc(s_yr, 1)
                tiles(dve, one)

            @block.gpsimd
            def _(pool):
                for b in range(2):
                    pool.dma_start(yr[:, b], slots[0]).then_inc(s_ys[b], 16)
                def one(n, b):
                    pool.wait_ge(s_yr, n + 3)
                    alone(pool)
                    pool.dma_start(slots_y[bass.ds(n, 1)].rearrange("n p q f -> (n p) q f"), yr[:, b]).then_inc(s_ys[b], 16)
                tiles(pool, one)
                for b in range(2):
                    pool.wait_ge(s_ys[b], 16 * ((MT + 1 - b) // 2 + 1))

        s_gi, s_gr, s_gf = sem("sum_index_ready"), [sem("sum_rows_landed0"), sem("sum_rows_landed1")], sem("sum_buffer_free")
        with ExitStack() as c:
            sh = Shared(c, "b")
            rows_ = [sb(f"sum_rows{k}", [P, 2, TU, F], c=c) for k in range(2)]
            pi = sb("sum_pi", [P, 2, 2, TU], I32, c=c)
            block = c.enter_context(nc.Block())

            @block.sync
            def _(sp):
                sh.loads(sp)

            @block.gpsimd
            def _(pool):
                def trip(g, b):
                    pool.wait_ge(s_gf, g + 1)
                    alone(pool)
                    for k in range(2):
                        nc.gpsimd.tensor_copy(pi[:, b, k, :], pos[k][:, bass.ds(g * TU, TU)]).then_inc(s_gi, 1)
                    pool.wait_ge(s_gi, 2 * (g + 1))
                    alone(pool)
                    for j in range(TU):
                        for k in range(2):
                            pool.indirect_dma_start(rows_[k][:, b, j, :], None, slot_y,
                                                    bass.IndirectOffsetOnAxis(pi[:, b, k, j:j + 1], 0)).then_inc(s_gr[b], 16)
                group_loop(pool, trip)

            @block.tensor
            def _(pe):
                pe.wait_ge(loaded, total["loaded"])
                sh.pe(pe, G0, NG)

            @block.scalar
            def _(act):
                sh.act(act, G0, NG)

            @block.vector
            def _(dve):
                v = chain(dve, c_v, "v")
                dve.sem_inc(s_gf, 2)
                for g in range(NG):
                    b = g % 2
                    dve.wait_ge(s_gr[b], 32 * TU * (g // 2 + 1))
                    for k in range(2):
                        v.wait()
                        for j in range(TU):
                            t = g * TU + j
                            v(nc.vector.scalar_tensor_tensor(out=X[:, t, :], in0=rows_[k][:, b, j, :], scalar=wsel[k][:, t:t + 1],
                                                             in1=X[:, t, :], op0=ALU.mult, op1=ALU.add))
                    v.wait()
                    dve.sem_inc(s_gf, 1)
                    if g % 2 == 1:
                        sh.dve(dve, v, G0 + g // 2)
                total["v"] = v.n

        if stage == 1:
            pass
        s_out = sem("out_stored")
        with nc.Block() as block:
            @block.sync
            def _(sp):
                sp.dma_start(out[0:(NT - 1) * P, :].rearrange("(t p) f -> p t f", p=P), X[:, 0:NT - 1, :]).then_inc(s_out, 16)
                sp.dma_start(out[(NT - 1) * P:N, :], X[0:TAIL, NT - 1, :]).then_inc(s_out, 16)
                sp.wait_ge(s_out, 32)


_INS = ["x", "src", "dst",
        "L0_gnn_W_l", "L0_gnn_b_l", "L0_gnn_W_r", "L0_gnn_b_r", "L0_gnn_att", "L0_gnn_bias",
        "L0_ffn_sW1", "L0_ffn_sb1", "L0_ffn_sW2", "L0_ffn_sb2", "L0_ffn_sW3", "L0_ffn_sb3",
        "L0_ffn_eW1", "L0_ffn_eb1", "L0_ffn_eW2", "L0_ffn_eb2", "L0_ffn_eW3", "L0_ffn_eb3", "L0_ffn_gW", "L0_ffn_gb",
        "L1_gnn_W_proj", "L1_gnn_b_proj", "L1_gnn_W_l", "L1_gnn_b_l", "L1_gnn_W_r", "L1_gnn_gamma", "L1_gnn_beta",
        "L1_ffn_Wr", "L1_ffn_W1s", "L1_ffn_b1s", "L1_ffn_W2s", "L1_ffn_b2s", "L1_ffn_W1p", "L1_ffn_b1p",
        "L1_ffn_W2p", "L1_ffn_b2p"]


def kernel(**inputs):
    import numpy as _np
    import concourse.bacc as _bacc
    from concourse import mybir as _mybir
    from concourse.bass_utils import run_bass_kernel_spmd as _run

    nc = _bacc.Bacc("TRN2", target_bir_lowering=False, num_devices=1)
    arrays, aps = {}, {}
    for name in _INS:
        v = _np.ascontiguousarray(inputs[name])
        arrays[f"in_{name}"] = v
        aps[name] = nc.dram_tensor(f"in_{name}", v.shape, _mybir.dt.from_np(v.dtype), kind="ExternalInput").ap()
    out = nc.dram_tensor("out", (N, F), _mybir.dt.float32, kind="ExternalOutput").ap()
    graph_block_kernel(nc, aps, out)
    r = _run(nc, [arrays], core_ids=[0])
    return r.results[0]["out"]
```

```python
from contextlib import ExitStack

import numpy as np
import concourse.bass as bass
from concourse import mybir

F32, I32, F32R = mybir.dt.float32, mybir.dt.int32, mybir.dt.float32r
ALU = mybir.AluOpType
ACT = mybir.ActivationFunctionType
AX = mybir.AxisListType

P = 128
N, E, F = 6250, 100000, 256
KF = F // P
H, C = 4, 64
NT = -(-N // P)
NP = NT * P
TAIL = N - (NT - 1) * P
T = 7
NB = 4
EP = 784
CH = EP // T
ELAST = E - (P - 1) * EP
XW = F + H
SW = F + 2 * H
BIG = 1.0e6
NEG = -1.0e30
SLOPE = 0.2
LN_EPS = 1e-5
TU = 7
NG = NT // TU
GW = TU * P // 2
assert CH * T == EP and CH % NB == 0 and NG * TU == NT and 0 < ELAST < EP


class Chain:

    def __init__(self, eng, sem):
        self.eng, self.sem, self.n, self.base = eng, sem, 0, 0

    def __call__(self, ins):
        ins.then_inc(self.sem, 1)
        self.n += 1

    def wait(self):
        if isinstance(self.base, int) and self.base + self.n == 0:
            return
        self.eng.wait_ge(self.sem, self.base + self.n)

    def enter(self, i, per_trip):
        self.before, self.per_trip = self.base + self.n, per_trip
        self.base, self.n = self.before + i * per_trip, 0

    def leave(self, trips):
        assert self.n == self.per_trip, (self.n, self.per_trip)
        self.base, self.n = self.before + trips * self.per_trip, 0


def graph_block_kernel(nc, a, out):
    ctx = ExitStack()
    with ctx:
        def dram(name, shape, dt=F32):
            return nc.dram_tensor(name, shape, dt, kind="Internal").ap()

        def sem(name):
            return ctx.enter_context(nc.semaphore(name))

        def sb(name, shape, dt=F32, c=ctx):
            return c.enter_context(nc.sbuf_tensor(name, shape, dt))

        def ps(name, shape, c):
            return c.enter_context(nc.psum_tensor(name, shape, F32))

        xl_tab, xr_tab = dram("xl_tab", (NP, XW)), dram("xr_tab", (NP, XW))
        xp_tab = dram("xp_tab", (NP, F))
        dst_rows = dram("dst_rows", (P, EP))
        soft_tab = dram("soft_tab", (P * EP + 1, SW))
        soft_carry = dram("soft_carry", (P + 1, SW))
        max_tab = dram("max_tab", (P * EP + 1, F))
        max_carry = dram("max_carry", (P + 1, F))

        X = sb("X", [P, NT, F])
        ident = sb("ident", [P, P])
        ones = sb("ones", [P, P])
        node = sb("node", [P, NT])
        idx_end = sb("idx_end", [P, NT], I32)
        idx_carry = sb("idx_carry", [P, NT], I32)
        dl_col = sb("dl_col", [P, 1])
        dl_row = sb("dl_row", [P, P])
        ends = sb("ends", [P, 2, EP + NB * T], I32)
        src_i, dst_i = ends[:, 0, :], ends[:, 1, :]
        keep, pen = sb("keep", [P, EP]), sb("pen", [P, EP])

        c_v, c_a, c_t, c_p = sem("dve_step"), sem("act_step"), sem("pe_step"), sem("pool_step")
        settle = sem("wait_stood_alone")
        loaded, stored = sem("loaded"), sem("stored")
        total = {"loaded": 0, "stored": 0, "v": 0, "a": 0, "t": 0, "p": 0}

        def load(eng, dst, src):
            eng.dma_start(dst, src).then_inc(loaded, 16)
            total["loaded"] += 16

        def store(eng, dst, src):
            eng.dma_start(dst, src).then_inc(stored, 16)
            total["stored"] += 16

        def chain(eng, s, key):
            c = Chain(eng, s)
            c.n = total[key]
            return c

        def alone(eng):
            eng.sem_inc(settle, 1)

        def prime(eng, *sems):
            for s in sems:
                eng.sem_inc(s, 1)

        def done(eng, s, n):
            eng.wait_ge(s, n + 1)

        def row(vec, n):
            return vec.rearrange("(a n) -> a n", a=1).broadcast_to([P, n])

        s_id, s_dst = sem("ident_ready"), sem("dst_ready")
        att_b = sb("att_b", [P, F])
        upto, below = sb("upto", [P, NT]), sb("below", [P, NT])
        rowi = sb("rowi", [P, NT], I32)
        limits = sb("limits", [P, 3, NT])
        with ExitStack() as c:
            node_b = sb("node_b", [P, NT, P], c=c)
            dst_f = sb("dst_f", [P, EP], c=c)
            scr = sb("scr", [P, EP], c=c)
            dlb = ps("dlb", [P, P], c)
            block = c.enter_context(nc.Block())

            @block.sync
            def _(sp):
                sp.wait_ge(s_id, 6)
                load(sp, X[:, 0:NT - 1, :], a["x"][0:(NT - 1) * P, :].rearrange("(t p) f -> p t f", p=P))
                load(sp, X[0:TAIL, NT - 1, :], a["x"][(NT - 1) * P:N, :])
                for t, v in ((src_i, a["src"]), (dst_i, a["dst"])):
                    load(sp, t[0:P - 1, 0:EP], v[0:(P - 1) * EP].rearrange("(p e) -> p e", p=P - 1))
                    load(sp, t[P - 1:P, 0:ELAST], v[(P - 1) * EP:E].rearrange("(p e) -> p e", p=1))
                sp.wait_ge(s_dst, 1)
                store(sp, dst_rows, dst_f[:, :])
                sp.wait_ge(stored, total["stored"])

            @block.gpsimd
            def _(pool):
                p = chain(pool, c_p, "p")
                nc.gpsimd.memset(X[:, NT - 1, :], 0.0).then_inc(s_id, 1)
                nc.gpsimd.memset(src_i[:, ELAST:], 0).then_inc(s_id, 1)
                nc.gpsimd.memset(dst_i[:, ELAST:], int(BIG)).then_inc(s_id, 1)
                nc.gpsimd.memset(ones[:, :], 1.0).then_inc(s_id, 1)
                p(nc.gpsimd.memset(ident[:, :], 0.0))
                p.wait()
                nc.gpsimd.affine_select(out=ident[:, :], in_=ident[:, :], compare_op=ALU.not_equal, fill=1.0,
                                        base=0, pattern=[[-1, P]], channel_multiplier=1).then_inc(s_id, 1)
                nc.gpsimd.iota(node[:, :], [[P, NT]], base=0, channel_multiplier=1,
                               allow_small_or_imprecise_dtypes=True).then_inc(s_id, 1)
                total["p"] = p.n

            @block.tensor
            def _(pe):
                pe.wait_ge(s_id, 6)
                pe.wait_ge(s_dst, 2)
                nc.tensor.matmul(dlb[:, :], dl_col[:, 0:1].broadcast_to([P, P]), ident[:, :],
                                 start=True, stop=True).then_inc(c_t, 1)
                total["t"] = 1

            @block.vector
            def _(dve):
                v = chain(dve, c_v, "v")
                dve.wait_ge(loaded, total["loaded"])
                nc.vector.tensor_copy(dst_f[:, :], dst_i[:, 0:EP]).then_inc(s_dst, 1)
                dve.wait_ge(s_dst, 1)
                nc.vector.tensor_copy(dl_col[:, :], dst_f[:, EP - 1:EP]).then_inc(s_dst, 1)
                v(nc.vector.memset(keep[:, 0:1], 0.0))
                v(nc.vector.tensor_tensor(keep[:, 1:EP], dst_f[:, 1:EP], dst_f[:, 0:EP - 1], ALU.is_equal))
                v.wait()
                v(nc.vector.tensor_scalar(pen[:, :], keep[:, :], 1.0, -NEG, ALU.subtract, ALU.mult))
                dve.wait_ge(s_dst, 2)
                v(nc.vector.tensor_scalar(scr[:, :], dst_f[:, :], float(N - 1), None, ALU.min))
                v.wait()
                v(nc.vector.tensor_copy(dst_i[:, 0:EP], scr[:, :]))
                dve.wait_ge(c_t, 1)
                v(nc.vector.tensor_copy(dl_row[:, :], dlb[:, :]))
                v.wait()
                dve.wait_ge(s_id, 6)
                dlv = dl_row[:, :].unsqueeze(1).broadcast_to([P, NT, P])
                nov = node[:, :].unsqueeze(2).broadcast_to([P, NT, P])
                for op, dst in ((ALU.is_lt, below), (ALU.is_le, upto)):
                    v(nc.vector.tensor_tensor(node_b[:, :, :], dlv, nov, op))
                    v.wait()
                    v(nc.vector.tensor_reduce(dst[:, :], node_b[:, :, :], AX.X, ALU.add))
                    v.wait()
                v(nc.vector.tensor_copy(rowi[:, :], upto[:, :]))
                for k in range(3):
                    v(nc.vector.tensor_scalar(limits[:, k, :], node[:, :], 1.0 - k, None, ALU.add))
                v.wait()
                total["v"] = v.n

        def norm_phase(name, width, tokens, ph, keep=None):
            s_stat = sem(f"{name}_statistics_step")
            s_xn, s_tp, s_ev = sem(f"{name}_xn_ready"), sem(f"{name}_transposed"), sem(f"{name}_xT_ready")
            s_mm, s_use = sem(f"{name}_product"), sem(f"{name}_product_used")
            s_xt = sem(f"{name}_xT_kept") if tokens is not None else None
            with ExitStack() as c:
                st6 = sb("st6" + name, [P, NT, 6], c=c)
                mean, rstd = keep or (sb(n + name, [P, NT], c=c) for n in ("mean", "rstd"))
                tmp = sb("tmp" + name, [P, NT], c=c)
                xn = sb("xn" + name, [P, TU, F], c=c)
                xts = sb("xts" + name, [P, 3, KF, P], c=c)
                w = sb("w" + name, [P, KF, width], c=c)
                xt_ps = [ps(f"xt_ps{b}" + name, [P, 512], c) for b in range(2)]
                mm_ps = [ps(f"mm_ps{b}" + name, [P, 512], c) for b in range(2)]
                xt_ps0 = xt_ps[0]
                ex = ph(c, w, xt_ps0)
                block = c.enter_context(nc.Block())

                def xt_view(b):
                    return xt_ps[b][:, 0:F].rearrange("p (k n) -> p k n", k=KF)

                @block.sync
                def _(sp):
                    ex["loads"](sp)
                    if "rows" in ex:
                        ex["rows"](sp, s_use)

                @block.vector
                def _(dve):
                    v = chain(dve, c_v, "v")
                    prime(dve, s_use, s_xn)
                    with dve.Fori(0, NG) as g:
                        v.enter(g, TU)
                        for j in range(TU):
                            v(nc.vector.bn_stats(st6[:, bass.ds(g * TU + j, 1), :], X[:, bass.ds(g * TU + j, 1), :]))
                        v.leave(NG)
                    v.wait()
                    v(nc.vector.tensor_tensor(mean[:, :], st6[:, :, 1], st6[:, :, 4], ALU.add))
                    v(nc.vector.tensor_tensor(tmp[:, :], st6[:, :, 1], st6[:, :, 4], ALU.subtract))
                    v.wait()
                    v(nc.vector.tensor_tensor(tmp[:, :], tmp[:, :], tmp[:, :], ALU.mult))
                    v(nc.vector.tensor_tensor(rstd[:, :], st6[:, :, 2], st6[:, :, 5], ALU.add))
                    v.wait()
                    v(nc.vector.tensor_scalar(rstd[:, :], rstd[:, :], 1.0 / F, LN_EPS, ALU.mult, ALU.add))
                    v(nc.vector.tensor_scalar(mean[:, :], mean[:, :], 0.5, None, ALU.mult))
                    v.wait()
                    nc.vector.scalar_tensor_tensor(out=rstd[:, :], in0=tmp[:, :], scalar=0.25, in1=rstd[:, :],
                                                   op0=ALU.mult, op1=ALU.add).then_inc(s_stat, 1)
                    dve.wait_ge(s_stat, 2)
                    nc.vector.reciprocal(rstd[:, :], tmp[:, :]).then_inc(s_stat, 1)
                    dve.wait_ge(s_stat, 3)
                    def normalize(g, j):
                        t = g * TU + j
                        nc.vector.tensor_scalar(xn[:, j:j + 1, :], X[:, bass.ds(t, 1), :], mean[:, bass.ds(t, 1)],
                                                rstd[:, bass.ds(t, 1)], ALU.subtract, ALU.mult).then_inc(s_xn, 1)
                    def trip(g, last):
                        for j in range(TU):
                            if j + 2 < TU:
                                normalize(g, j + 2)
                            elif not last:
                                normalize(g + 1, j + 2 - TU)
                            done(dve, s_mm, g * TU + j + 1)
                            ex["consume"](v, dve, mm_ps[j % 2], g, j, s_use)
                    normalize(0, 0)
                    normalize(0, 1)
                    with dve.Fori(0, NG - 1) as g:
                        v.enter(g, TU * ex["steps"])
                        trip(g, False)
                        v.leave(NG - 1)
                    trip(NG - 1, True)
                    v.wait()
                    if "last" in ex:
                        ex["last"](v, dve, s_use)
                    total["v"] = v.base + v.n

                @block.scalar
                def _(act):
                    prime(act, s_ev, *([s_xt] if tokens is not None else []))
                    act.wait_ge(s_stat, 1)
                    nc.scalar.activation(tmp[:, :], rstd[:, :], ACT.Sqrt).then_inc(s_stat, 1)
                    if "act" in ex:
                        ex["act"](act)
                    with act.Fori(0, NG) as g:
                        for j in range(TU):
                            t, b = g * TU + j, j % 3
                            done(act, s_tp, t + 1)
                            done(act, s_mm, t - 2 if j >= 3 else g * TU)
                            nc.scalar.activation(xts[:, b, :, :], xt_view(j % 2), ACT.Copy).then_inc(s_ev, 1)
                            if tokens is not None:
                                nc.scalar.activation(tokens[:, :, bass.ds(t * P, P)], xt_view(j % 2), ACT.Copy).then_inc(s_xt, 1)
                            if "act_tile" in ex:
                                ex["act_tile"](act, g, j)

                @block.gpsimd
                def _(pool):
                    if "pool" in ex:
                        ex["pool"](pool)

                @block.tensor
                def _(pe):
                    prime(pe, s_tp, s_mm)
                    pe.wait_ge(loaded, total["loaded"])
                    if "pe" in ex:
                        ex["pe"](pe)
                    def turn(g, j):
                        t = g * TU + j
                        done(pe, s_xn, t + 1)
                        done(pe, s_ev if tokens is None else s_xt, t - 1 if j >= 2 else g * TU)
                        for k in range(KF):
                            m = nc.tensor.transpose(xt_ps[j % 2][:, k * P:(k + 1) * P], xn[:, j, k * P:(k + 1) * P],
                                                    ident[:, :])
                        m.then_inc(s_tp, 1)
                    def trip(g, last):
                        for j in range(TU):
                            t, b = g * TU + j, j % 2
                            if j + 1 < TU:
                                turn(g, j + 1)
                            elif not last:
                                turn(g + 1, 0)
                            done(pe, s_ev, t + 1)
                            done(pe, s_use, t - 1 if j >= 2 else g * TU)
                            for k in range(KF):
                                m = nc.tensor.matmul(mm_ps[b][:, 0:width], xts[:, j % 3, k, :], w[:, k, :],
                                                     start=(k == 0), stop=(k == KF - 1))
                            m.then_inc(s_mm, 1)
                    turn(0, 0)
                    with pe.Fori(0, NG - 1) as g:
                        trip(g, False)
                    trip(NG - 1, True)

        USES = [(TU + 1) // 2, TU // 2]

        s_rows = [sem(f"dst_row_landed{b}") for b in range(3)]
        s_ridx, s_counted = sem("row_index_ready"), sem("dst_row_counted")
        s_pst = [sem("proj_stored0"), sem("proj_stored1")]

        def proj(c, w, bank):
            bias = sb("proj_bias", [P, 2 * F], c=c)
            rows = sb("rows", [P, 3, EP], c=c)
            scr = sb("relu_scratch", [P, 3, EP], c=c)
            ri = sb("ri", [P, TU], I32, c=c)
            rsum = sb("rsum", [P, 3, NT], c=c)
            fa, fb = sb("fa", [P, NT], c=c), sb("fb", [P, NT], c=c)
            cnt_lt, cnt_le = sb("cnt_lt", [P, NT], c=c), sb("cnt_le", [P, NT], c=c)
            rowb, am = sb("proj_row", [P, 2, 2, XW], c=c), sb("proj_att", [P, 2, 2, F], c=c)

            def loads(sp):
                load(sp, w[:, :, 0:F], a["L0_gnn_W_l"].rearrange("(k p) n -> p k n", p=P))
                load(sp, w[:, :, F:2 * F], a["L0_gnn_W_r"].rearrange("(k p) n -> p k n", p=P))
                for b, n in enumerate(("L0_gnn_b_l", "L0_gnn_b_r")):
                    sp.dma_start(bias[:, b * F:(b + 1) * F], row(a[n], F)).then_inc(s_pst[b], 32)
                load(sp, att_b[:, :], row(a["L0_gnn_att"].rearrange("h c -> (h c)"), F))

            def consume(v, dve, mm, g, j, s_use):
                b = j % 2
                r, m = rowb[:, b, :, :], am[:, b, :, :]
                dve.wait_ge(s_pst[b], 32 * (g * USES[b] + j // 2 + 1))
                if j == 0:
                    dve.wait_ge(s_pst[1], 32)
                    dve.wait_ge(loaded, total["loaded"])
                v(nc.vector.tensor_tensor(r[:, :, 0:F], mm[:, 0:2 * F].rearrange("p (s f) -> p s f", s=2),
                                          bias[:, :].rearrange("p (s f) -> p s f", s=2), ALU.add))
                v.wait()
                for k in range(2):
                    v(nc.vector.scalar_tensor_tensor(out=m[:, k, :], in0=r[:, k, 0:F], scalar=SLOPE, in1=att_b[:, :],
                                                     op0=ALU.mult, op1=ALU.mult))
                v.wait()
                nc.vector.tensor_reduce(r[:, :, F:XW], m.rearrange("p s (h c) -> p s h c", h=H), AX.X,
                                        ALU.add).then_inc(s_use, 1)

            def store_rows(sp, s_use):
                with sp.Fori(0, NG) as g:
                    for j in range(TU):
                        t, b = g * TU + j, j % 2
                        done(sp, s_use, t + 1)
                        for k, tab in enumerate((xl_tab, xr_tab)):
                            sp.dma_start(tab[bass.ds(t * P, P), :], rowb[:, b, k, :]).then_inc(s_pst[b], 16)
                for b in range(2):
                    sp.wait_ge(s_pst[b], 32 * (NG * USES[b] + 1))

            def gather_rows(pool):
                pool.sem_inc(s_counted, 9)
                with pool.Fori(0, NG) as g:
                    pool.wait_ge(s_counted, (g * TU + 3) * 3)
                    alone(pool)
                    nc.gpsimd.tensor_copy(ri[:, :], rowi[:, bass.ds(g * TU, TU)]).then_inc(s_ridx, 1)
                    pool.wait_ge(s_ridx, g + 1)
                    alone(pool)
                    for j in range(TU):
                        pool.wait_ge(s_counted, (g * TU + j + 1) * 3 if j else (g * TU + 3) * 3)
                        alone(pool)
                        pool.indirect_dma_start(rows[:, j % 3, :], None, dst_rows,
                                                bass.IndirectOffsetOnAxis(ri[:, j:j + 1], 0)).then_inc(s_rows[j % 3], 16)

            def count(act, g, j):
                b = j % 3
                act.wait_ge(s_rows[b], 16 * (g * (3 if b == 0 else 2) + j // 3 + 1))
                alone(act)
                for k in range(3):
                    act.wait_ge(s_counted, (g * TU + j + 2) * 3 + k + 1)
                    alone(act)
                    nc.scalar.activation(scr[:, k, :], rows[:, b, :], ACT.Relu, bias=limits[:, k, bass.ds(g * TU + j, 1)],
                                         scale=-1.0, accum_out=rsum[:, k, bass.ds(g * TU + j, 1)]).then_inc(s_counted, 1)

            def index(v, dve, s_use):
                dve.wait_ge(s_counted, 3 * (NT + 3))
                v(nc.vector.tensor_tensor(cnt_le[:, :], rsum[:, 0, :], rsum[:, 1, :], ALU.subtract))
                v(nc.vector.tensor_tensor(cnt_lt[:, :], rsum[:, 1, :], rsum[:, 2, :], ALU.subtract))
                def step(ins):
                    v(ins)
                    v.wait()
                v.wait()
                step(nc.vector.tensor_tensor(fa[:, :], cnt_le[:, :], cnt_lt[:, :], ALU.is_gt))
                step(nc.vector.tensor_scalar(fb[:, :], upto[:, :], float(EP), -1.0 - P * EP, ALU.mult, ALU.add))
                step(nc.vector.tensor_tensor(fb[:, :], fb[:, :], cnt_le[:, :], ALU.add))
                step(nc.vector.tensor_tensor(fb[:, :], fb[:, :], fa[:, :], ALU.mult))
                step(nc.vector.tensor_scalar(fb[:, :], fb[:, :], float(P * EP), None, ALU.add))
                step(nc.vector.tensor_copy(idx_end[:, :], fb[:, :]))
                step(nc.vector.tensor_tensor(fa[:, :], upto[:, :], below[:, :], ALU.is_gt))
                step(nc.vector.tensor_scalar(fb[:, :], upto[:, :], -1.0 - P, None, ALU.add))
                step(nc.vector.tensor_tensor(fb[:, :], fb[:, :], fa[:, :], ALU.mult))
                step(nc.vector.tensor_scalar(fb[:, :], fb[:, :], float(P), None, ALU.add))
                step(nc.vector.tensor_copy(idx_carry[:, :], fb[:, :]))
            return {"loads": loads, "consume": consume, "steps": 3, "rows": store_rows, "pool": gather_rows,
                    "act_tile": count, "last": index}

        norm_phase("proj", 2 * F, None, proj)

        s_row = [sem(f"rows_landed{b}") for b in range(NB)]
        s_free, s_idx = sem("rows_free"), sem("gather_index_ready")
        s_z, s_relu, s_d, s_exp = sem("z_ready"), sem("relu_ready"), sem("exponents_ready"), sem("exp_ready")
        s_st, s_stored = sem("state_ready"), [sem("state_stored0"), sem("state_stored1")]
        s_neutral, s_num = sem("neutral_ready"), sem("numerator_step")
        TRIPS = CH // NB
        soft_rows = soft_tab[0:P * EP, :].rearrange("(p e) f -> p e f", p=P)
        last_state = sb("last_state", [P, SW])
        neutral = sb("neutral", [1, SW])
        with ExitStack() as c:
            xl = sb("xl", [P, NB, T, XW], c=c)
            xr = sb("xr", [P, NB, T, XW], c=c)
            z = sb("z", [P, 3, T * F], c=c)
            lin, logit = sb("lin", [P, T, H], c=c), sb("logit", [P, T, H], c=c)
            lg = sb("lg", [P, H, T], c=c)
            mx = sb("mx", [P, 2, H, T + 1], c=c)
            ex_in, ex_out = sb("ex_in", [P, 2, 2, H, T], c=c), sb("ex_out", [P, 2, 2, H, T], c=c)
            state = sb("state", [P, 2, T, SW], c=c)
            ix = sb("gather_index", [P, NB, 2, T], I32, c=c)
            zp = [ps(f"zp{b}", [P, T, F], c) for b in range(2)]
            block = c.enter_context(nc.Block())

            @block.tensor
            def _(pe):
                pe.sem_inc(s_z, 1)
                with pe.Fori(0, TRIPS) as i:
                    for k in range(NB):
                        pe.wait_ge(s_row[k], 32 * T * (i + 1))
                        pe.wait_ge(s_relu, i * NB + k + 1)
                        for t in range(0, T, 2):
                            w = slice(t, min(t + 2, T))
                            nc.tensor.matmul(zp[k % 2][:, w, :], ident[:, :], xl[:, k, w, 0:F], start=True, stop=False)
                            m = nc.tensor.matmul(zp[k % 2][:, w, :], ident[:, :], xr[:, k, w, 0:F], start=False, stop=True)
                        m.then_inc(s_z, 1)

            @block.gpsimd
            def _(pool):
                nc.gpsimd.memset(neutral[0:1, 0:F + H], 0.0).then_inc(s_neutral, 1)
                nc.gpsimd.memset(neutral[0:1, F + H:SW], NEG).then_inc(s_neutral, 1)
                with pool.Fori(0, TRIPS) as i:
                    for b in range(NB):
                        pool.wait_ge(s_idx, i * NB + b + 1)
                        pool.wait_ge(s_free, i * NB + b + 1)
                        alone(pool)
                        for t in range(T):
                            for k, (buf, tab) in enumerate(((xl, xl_tab), (xr, xr_tab))):
                                pool.indirect_dma_start(buf[:, b, t, :], None, tab,
                                                        bass.IndirectOffsetOnAxis(ix[:, b, k, t:t + 1], 0)).then_inc(s_row[b], 16)

            @block.scalar
            def _(act):
                act.sem_inc(s_relu, 2)
                with act.Fori(0, TRIPS) as i:
                    def relu(k):
                        done(act, s_z, i * NB + k + 1)
                        act.wait_ge(s_st, i * NB + k + 1 if k != 0 else i * NB + 3)
                        nc.scalar.activation(z[:, k % 3, :], zp[k % 2][:, :, :].rearrange("p t f -> p (t f)"), ACT.Relu,
                                             scale=1.0 - SLOPE).then_inc(s_relu, 1)
                    relu(0)
                    for k in range(NB):
                        if k + 1 < NB:
                            relu(k + 1)
                        act.wait_ge(s_d, i * NB + k + 1)
                        nc.scalar.activation(ex_out[:, k % 2], ex_in[:, k % 2], ACT.Exp).then_inc(s_exp, 1)

            @block.sync
            def _(sp):
                sp.wait_ge(s_neutral, 2)
                sp.dma_start(soft_tab[P * EP:P * EP + 1, :], neutral[0:1, :]).then_inc(s_stored[0], 16)
                sp.dma_start(soft_carry[P:P + 1, :], neutral[0:1, :]).then_inc(s_stored[1], 16)
                with sp.Fori(0, TRIPS) as i:
                    for k in range(NB):
                        sp.wait_ge(s_st, i * NB + k + 4)
                        sp.dma_start(soft_rows[:, bass.ds((i * NB + k) * T, T), :], state[:, k % 2, :, :]).then_inc(s_stored[k % 2], 16)
                for b in range(2):
                    sp.wait_ge(s_stored[b], 16 * (CH // 2 + 1))

            @block.vector
            def _(dve):
                v = chain(dve, c_v, "v")
                v(nc.vector.memset(state[:, 1, T - 1, 0:F + H], 0.0))
                v(nc.vector.memset(state[:, 1, T - 1, F + H:SW], NEG))
                v(nc.vector.memset(mx[:, 1, :, T:T + 1], NEG))
                v.wait()
                for b in range(NB):
                    nc.vector.tensor_copy(ix[:, b, :, :], ends[:, :, b * T:(b + 1) * T]).then_inc(s_idx, 1)
                dve.sem_inc(s_free, NB)
                dve.sem_inc(s_st, 3)
                with dve.Fori(0, TRIPS) as i:
                    v.enter(i, NB * 16)
                    def logits(k):
                        zk = z[:, k % 3, :].rearrange("p (t f) -> p t f", t=T)
                        dve.wait_ge(s_row[k], 32 * T * (i + 1))
                        nc.vector.tensor_copy(ix[:, k, :, :], ends[:, :, bass.ds(((i + 1) * NB + k) * T, T)]).then_inc(s_idx, 1)
                        v.wait()
                        v(nc.vector.tensor_tensor(lin[:, :, :], xl[:, k, :, F:XW], xr[:, k, :, F:XW], ALU.add))
                        v(nc.vector.tensor_copy(mx[:, k % 2, :, 0:1], mx[:, (k + 1) % 2, :, T:T + 1]))
                        dve.wait_ge(s_relu, i * NB + k + 3)
                        v(nc.vector.tensor_tensor(zk, zk, att_b[:, :].unsqueeze(1).broadcast_to([P, T, F]), ALU.mult))
                        v.wait()
                        v(nc.vector.tensor_reduce(logit[:, :, :], zk.rearrange("p t (h c) -> p t h c", h=H), AX.X, ALU.add))
                        v.wait()
                        v(nc.vector.tensor_tensor(lg[:, :, :], logit[:, :, :].rearrange("p t h -> p h t"),
                                                  lin[:, :, :].rearrange("p t h -> p h t"), ALU.add))
                        v.wait()
                        pk = pen[:, bass.ds((i * NB + k) * T, T)]
                        for h in range(H):
                            v(nc.vector.tensor_tensor_scan(mx[:, k % 2, h, 1:T + 1], pk, lg[:, h, :],
                                                           mx[:, k % 2, h, 0:1], ALU.add, ALU.max))
                        v.wait()
                        m0, m1 = mx[:, k % 2, :, 0:T], mx[:, k % 2, :, 1:T + 1]
                        v(nc.vector.tensor_tensor(ex_in[:, k % 2, 0], lg[:, :, :], m1, ALU.subtract))
                        v(nc.vector.tensor_tensor(ex_in[:, k % 2, 1], m0, m1, ALU.subtract))
                        v.wait()
                        nc.vector.tensor_tensor(ex_in[:, k % 2, 1], ex_in[:, k % 2, 1],
                                                pk.unsqueeze(1).broadcast_to([P, H, T]), ALU.add).then_inc(s_d, 1)
                    def sums(k):
                        new, old = state[:, k % 2], state[:, (k + 1) % 2]
                        ea, ec = ex_out[:, k % 2, 0], ex_out[:, k % 2, 1]
                        pr = z[:, k % 3, :].rearrange("p (t h c) -> p t h c", t=T, h=H)
                        dve.wait_ge(s_exp, i * NB + k + 1)
                        nc.vector.tensor_tensor(pr, xl[:, k, :, 0:F].rearrange("p t (h c) -> p t h c", h=H),
                                                ea.rearrange("p h t -> p t h").unsqueeze(3).broadcast_to([P, T, H, C]),
                                                ALU.mult).then_inc(s_free, 1)
                        dve.wait_ge(s_stored[k % 2], 16 * (i * (NB // 2) + k // 2 + 1))
                        for h in range(H):
                            v(nc.vector.tensor_tensor_scan(new[:, :, F + h], ec[:, h, :], ea[:, h, :],
                                                           old[:, T - 1, F + h:F + h + 1], ALU.mult, ALU.add))
                        v(nc.vector.tensor_copy(new[:, :, F + H:SW], mx[:, k % 2, :, 1:T + 1].rearrange("p h t -> p t h")))
                        dve.wait_ge(s_free, i * NB + k + 1 + NB)
                        for t in range(T):
                            prev = old[:, T - 1] if t == 0 else new[:, t - 1]
                            for h in range(H):
                                n = (i * NB + k) * (T * H) + t * H + h
                                if t or k:
                                    dve.wait_ge(s_num, n - 3)
                                hs = slice(h * C, (h + 1) * C)
                                nc.vector.scalar_tensor_tensor(out=new[:, t, hs], in0=prev[:, hs], scalar=ec[:, h, t:t + 1],
                                                               in1=pr[:, t, h, :], op0=ALU.mult, op1=ALU.add).then_inc(s_num, 1)
                        dve.wait_ge(s_num, (i * NB + k + 1) * T * H)
                        v.wait()
                        dve.sem_inc(s_st, 1)
                    for k in range(NB):
                        logits(k)
                        if k >= 1:
                            sums(k - 1)
                    sums(NB - 1)
                    v.leave(TRIPS)
                v.wait()
                v(nc.vector.tensor_copy(last_state[:, :], state[:, 1, T - 1, :]))
                v.wait()
                total["v"] = v.base + v.n

        s_cst = sem("carry_step")
        with ExitStack() as c:
            tri = sb("tri", [P, P], c=c)
            same, cpen = sb("same", [P, P], c=c), sb("cpen", [P, P], c=c)
            mrow, wrow = sb("mrow", [P, H, P], c=c), sb("wrow", [P, H, P], c=c)
            wq = sb("wq", [P, H, P], c=c)
            cmax = sb("cmax", [P, H], c=c)
            crow = sb("crow", [P, SW], c=c)
            mp, tp, op = (ps(n, [P, 512], c) for n in ("mp", "tp", "op"))
            block = c.enter_context(nc.Block())

            @block.gpsimd
            def _(pool):
                nc.gpsimd.affine_select(out=tri[:, :], in_=ones[:, :], compare_op=ALU.is_ge, fill=0.0,
                                        base=0, pattern=[[-1, P]], channel_multiplier=1).then_inc(s_cst, 1)

            @block.tensor
            def _(pe):
                pe.wait_ge(s_cst, 1)
                for h in range(H):
                    m = nc.tensor.matmul(mp[:, h * P:(h + 1) * P], last_state[:, F + H + h:F + H + h + 1].broadcast_to([P, P]),
                                         ident[:, :], start=True, stop=True)
                m.then_inc(s_cst, 1)
                pe.wait_ge(s_cst, 4)
                for h in range(H):
                    m = nc.tensor.transpose(tp[:, h * P:(h + 1) * P], wrow[:, h, :], ident[:, :])
                m.then_inc(s_cst, 1)
                pe.wait_ge(s_cst, 6)
                for h in range(H):
                    nc.tensor.matmul(op[:, h * C:(h + 1) * C], wq[:, h, :], last_state[:, h * C:(h + 1) * C],
                                     start=True, stop=True)
                    m = nc.tensor.matmul(op[:, F + h:F + h + 1], wq[:, h, :], last_state[:, F + h:F + h + 1],
                                         start=True, stop=True)
                m.then_inc(s_cst, 1)

            @block.vector
            def _(dve):
                v = chain(dve, c_v, "v")
                dve.wait_ge(s_cst, 2)
                v(nc.vector.tensor_scalar(same[:, :], dl_row[:, :], dl_col[:, 0:1], None, ALU.is_equal))
                v.wait()
                v(nc.vector.tensor_tensor(same[:, :], same[:, :], tri[:, :], ALU.mult))
                v.wait()
                v(nc.vector.tensor_scalar(cpen[:, :], same[:, :], 1.0, -NEG, ALU.subtract, ALU.mult))
                v.wait()
                v(nc.vector.tensor_tensor(mrow[:, :, :], mp[:, :].rearrange("p (h q) -> p h q", h=H),
                                          cpen[:, :].unsqueeze(1).broadcast_to([P, H, P]), ALU.add))
                v.wait()
                v(nc.vector.tensor_reduce(cmax[:, :], mrow[:, :, :], AX.X, ALU.max))
                v.wait()
                nc.vector.tensor_tensor(mrow[:, :, :], mrow[:, :, :], cmax[:, :].unsqueeze(2).broadcast_to([P, H, P]),
                                        ALU.subtract).then_inc(s_cst, 1)
                dve.wait_ge(s_cst, 5)
                nc.vector.tensor_copy(wq[:, :, :], tp[:, :].rearrange("p (h q) -> p h q", h=H)).then_inc(s_cst, 1)
                dve.wait_ge(s_cst, 7)
                v(nc.vector.tensor_copy(crow[:, 0:F + H], op[:, 0:F + H]))
                nc.vector.tensor_copy(crow[:, F + H:SW], cmax[:, :]).then_inc(s_cst, 1)
                v.wait()
                total["v"] = v.n

            @block.scalar
            def _(act):
                act.wait_ge(s_cst, 3)
                nc.scalar.activation(wrow[:, :, :], mrow[:, :, :], ACT.Exp).then_inc(s_cst, 1)

            @block.sync
            def _(sp):
                sp.wait_ge(s_cst, 8)
                sp.wait_ge(c_v, total["v"])
                store(sp, soft_carry[0:P, :], crow[:, :])
                sp.wait_ge(stored, total["stored"])

        def group_loop(eng, trip):
            with eng.Fori(0, NG // 2) as i:
                trip(i * 2, 0)
                trip(i * 2 + 1, 1)
            assert NG % 2 == 1
            trip(NG - 1, 0)

        own_l = xl_tab.rearrange("(t p) f -> p t f", p=P)
        own_r = xr_tab.rearrange("(t p) f -> p t f", p=P)
        s_own = [sem("own_rows_landed0"), sem("own_rows_landed1")]
        s_seg = [sem("segment_rows_landed0"), sem("segment_rows_landed1")]
        s_sidx, s_mfree = sem("segment_index_ready"), sem("merge_buffer_free")
        s_mexp_in, s_mexp = sem("merge_exponents_ready"), sem("merge_exp_ready")
        s_mzz, s_mrelu = sem("self_z_ready"), sem("self_relu_ready")
        s_mw, s_msum = sem("merge_part_weighted"), sem("merge_sum_ready")
        with ExitStack() as c:
            ol, orr = sb("ol", [P, 2, TU, XW], c=c), sb("orr", [P, 2, TU, XW], c=c)
            ge, gc = sb("ge", [P, 2, TU, SW], c=c), sb("gc", [P, 2, TU, SW], c=c)
            ie, ic = sb("ie", [P, 2, TU], I32, c=c), sb("ic", [P, 2, TU], I32, c=c)
            bias = sb("gat_bias", [P, F], c=c)
            self_l, mtop, den = (sb(n, [P, TU, H], c=c) for n in ("self_l", "mtop", "den"))
            wexp = sb("wexp", [P, 3, TU, H], c=c)
            sump = ps("merge_sum", [P, TU, F], c)
            pairs = [slice(t, min(t + 2, TU)) for t in range(0, TU, 2)]
            block = c.enter_context(nc.Block())

            @block.sync
            def _(sp):
                load(sp, bias[:, :], row(a["L0_gnn_bias"], F))
                def trip(g, b):
                    sp.wait_ge(s_mfree, g + 1)
                    for buf, tab in ((ol, own_l), (orr, own_r)):
                        sp.dma_start(buf[:, b, :, :], tab[:, bass.ds(g * TU, TU), :]).then_inc(s_own[b], 16)
                group_loop(sp, trip)

            @block.gpsimd
            def _(pool):
                def trip(g, b):
                    pool.wait_ge(s_mfree, g + 1)
                    alone(pool)
                    nc.gpsimd.tensor_copy(ie[:, b, :], idx_end[:, bass.ds(g * TU, TU)]).then_inc(s_sidx, 1)
                    nc.gpsimd.tensor_copy(ic[:, b, :], idx_carry[:, bass.ds(g * TU, TU)]).then_inc(s_sidx, 1)
                    pool.wait_ge(s_sidx, 2 * (g + 1))
                    alone(pool)
                    for j in range(TU):
                        for buf, ix, tab in ((ge, ie, soft_tab), (gc, ic, soft_carry)):
                            pool.indirect_dma_start(buf[:, b, j, :], None, tab,
                                                    bass.IndirectOffsetOnAxis(ix[:, b, j:j + 1], 0)).then_inc(s_seg[b], 16)
                group_loop(pool, trip)

            @block.tensor
            def _(pe):
                def trip(g, b):
                    pe.wait_ge(s_mfree, g + 2)
                    for k, x in enumerate((ge, gc, ol)):
                        done(pe, s_mw, g * 3 + k + 1)
                        for w in pairs:
                            m = nc.tensor.matmul(sump[:, w, :], ident[:, :], x[:, b, w, 0:F], start=(k == 0), stop=(k == 2))
                    m.then_inc(s_msum, 1)
                group_loop(pe, trip)

            @block.scalar
            def _(act):
                prime(act, s_mrelu)
                def relu(g, b):
                    done(act, s_mzz, g + 1)
                    nc.scalar.activation(orr[:, b, :, 0:F], orr[:, b, :, 0:F], ACT.Relu, scale=1.0 - SLOPE).then_inc(s_mrelu, 1)
                relu(0, 0)
                def trip(g, b):
                    act.wait_ge(s_mexp_in, g + 1)
                    nc.scalar.activation(wexp[:, :, :, :], wexp[:, :, :, :], ACT.Exp).then_inc(s_mexp, 1)
                    if not isinstance(g, int):
                        relu(g + 1, 1 - b)
                group_loop(act, trip)

            @block.vector
            def _(dve):
                v = chain(dve, c_v, "v")
                dve.wait_ge(loaded, total["loaded"])
                dve.sem_inc(s_mfree, 2)
                prime(dve, s_mw, s_mzz)
                def self_z(g, b):
                    dve.wait_ge(s_own[b], 16 * (g - b + 2))
                    nc.vector.tensor_tensor(orr[:, b], orr[:, b], ol[:, b], ALU.add).then_inc(s_mzz, 1)
                self_z(0, 0)
                K = 15
                before = v.n
                def trip(g, b):
                    v.base, v.n = before + g * K, 0
                    fr, num = slice(0, F), lambda x: x[:, b, :, 0:F].rearrange("p t (h c) -> p t h c", h=H)
                    def step(ins):
                        v(ins)
                        v.wait()
                    if not (isinstance(g, int) and g == 0):
                        v.wait()
                    done(dve, s_mrelu, g + 1)
                    step(nc.vector.tensor_tensor(orr[:, b, :, fr], orr[:, b, :, fr],
                                                 att_b[:, :].unsqueeze(1).broadcast_to([P, TU, F]), ALU.mult))
                    step(nc.vector.tensor_reduce(self_l[:, :, :], num(orr), AX.X, ALU.add))
                    step(nc.vector.tensor_tensor(self_l[:, :, :], self_l[:, :, :], orr[:, b, :, F:XW], ALU.add))
                    dve.wait_ge(s_seg[b], 16 * TU * (g - b + 2))
                    me, mc = ge[:, b, :, F + H:SW], gc[:, b, :, F + H:SW]
                    step(nc.vector.tensor_tensor(mtop[:, :, :], me, mc, ALU.max))
                    step(nc.vector.tensor_tensor(mtop[:, :, :], mtop[:, :, :], self_l[:, :, :], ALU.max))
                    v(nc.vector.tensor_tensor(wexp[:, 0], me, mtop[:, :, :], ALU.subtract))
                    v(nc.vector.tensor_tensor(wexp[:, 1], mc, mtop[:, :, :], ALU.subtract))
                    v.wait()
                    nc.vector.tensor_tensor(wexp[:, 2], self_l[:, :, :], mtop[:, :, :], ALU.subtract).then_inc(s_mexp_in, 1)
                    dve.wait_ge(s_mexp, g + 1)
                    de, dc = ge[:, b, :, F:F + H], gc[:, b, :, F:F + H]
                    v(nc.vector.tensor_tensor(de, de, wexp[:, 0], ALU.mult))
                    step(nc.vector.tensor_tensor(dc, dc, wexp[:, 1], ALU.mult))
                    step(nc.vector.tensor_tensor(den[:, :, :], de, dc, ALU.add))
                    step(nc.vector.tensor_tensor(den[:, :, :], den[:, :, :], wexp[:, 2], ALU.add))
                    step(nc.vector.reciprocal(den[:, :, :], den[:, :, :]))
                    step(nc.vector.tensor_tensor(wexp[:, :, :, :], wexp[:, :, :, :],
                                                 den[:, :, :].unsqueeze(1).broadcast_to([P, 3, TU, H]), ALU.mult))
                    for k, x in enumerate((ge, gc, ol)):
                        nc.vector.tensor_tensor(num(x), num(x), wexp[:, k].unsqueeze(3).broadcast_to([P, TU, H, C]),
                                                ALU.mult).then_inc(s_mw, 1)
                    xg = X[:, bass.ds(g * TU, TU), :]
                    step(nc.vector.tensor_tensor(xg, xg, bias[:, :].unsqueeze(1).broadcast_to([P, TU, F]), ALU.add))
                    if not isinstance(g, int):
                        self_z(g + 1, 1 - b)
                    dve.wait_ge(s_msum, g + 1)
                    step(nc.vector.tensor_tensor(xg, xg, sump[:, :, :], ALU.add))
                    dve.sem_inc(s_mfree, 1)
                    assert v.n == K, v.n
                group_loop(dve, trip)
                total["v"] = before + NG * K

        XT = sb("XT", [P, KF, NP])
        gate = sb("gate", [P, NT, 8])

        def top_two(step, pr, eq, sels, vals, r0, kk, rank, ne):
            wide = lambda x: x[:, :].unsqueeze(2).broadcast_to([P, NT, ne])
            rk = rank[:, :].unsqueeze(1).broadcast_to([P, NT, ne])
            step(nc.vector.tensor_reduce(r0[:, :], pr[:, :, :], AX.X, ALU.add))
            step(nc.vector.reciprocal(r0[:, :], r0[:, :]))
            step(nc.vector.tensor_tensor(pr[:, :, :], pr[:, :, :], wide(r0), ALU.mult))
            for val, sel in zip(vals, sels):
                step(nc.vector.tensor_reduce(val[:, :], pr[:, :, :], AX.X, ALU.max))
                step(nc.vector.tensor_tensor(eq[:, :, :], pr[:, :, :], wide(val), ALU.is_equal))
                step(nc.vector.tensor_tensor(eq[:, :, :], eq[:, :, :], rk, ALU.mult))
                step(nc.vector.tensor_reduce(kk[:, :], eq[:, :, :], AX.X, ALU.max))
                step(nc.vector.tensor_tensor(sel[:, :, :], rk, wide(kk), ALU.is_equal))
                step(nc.vector.scalar_tensor_tensor(out=pr[:, :, :], in0=sel[:, :, :], scalar=-2.0, in1=pr[:, :, :],
                                                    op0=ALU.mult, op1=ALU.add))

        def gated(name, ne, w_in, bias_in, keep=None, more=None):
            def build(c, w, bank):
                gb = sb(f"{name}_gb", [P, 8], c=c)
                pool_more, sp_more = more(c) if more else (None, None)

                def loads(sp):
                    load(sp, w[:, :, :], w_in.rearrange("(k p) n -> p k n", p=P))
                    if bias_in is not None:
                        load(sp, gb[:, 0:ne], row(bias_in, ne))
                    if sp_more:
                        sp_more(sp)

                def consume(v, dve, mm, g, j, s_use):
                    t = bass.ds(g * TU + j, 1)
                    m = mm[:, 0:ne].unsqueeze(1)
                    if bias_in is not None:
                        if j == 0:
                            dve.wait_ge(loaded, total["loaded"])
                        nc.vector.tensor_tensor(gate[:, t, 0:ne], m, gb[:, 0:ne].unsqueeze(1), ALU.add).then_inc(s_use, 1)
                    else:
                        nc.vector.tensor_scalar(gate[:, t, 0:ne], m, 1.0, None, ALU.mult).then_inc(s_use, 1)

                def last(v, dve, s_use):
                    done(dve, s_use, NT)
                ex = {"loads": loads, "consume": consume, "steps": 0, "last": last}
                if pool_more:
                    ex["pool"] = pool_more
                return ex
            norm_phase(name, ne, XT, build, keep)

        s_bt = sem("ffn0_bias_step")
        held = ExitStack()
        NETS = [(2, P)] + [(1, 64)] * 4
        ones_row = [0] + [1] * 4
        w1 = [sb(f"f0w1_{n}", [P, KF, ch * P], c=held) for n, (ch, _) in enumerate(NETS)]
        w2 = [sb(f"f0w2_{n}", [P, ch, h2], c=held) for n, (ch, h2) in enumerate(NETS)]
        w3 = [sb(f"f0w3_{n}", [h2 + ones_row[n], F], c=held) for n, (_, h2) in enumerate(NETS)]
        sb3 = sb("f0sb3", [P, F], c=held)
        NB1 = 2 + 4 + 1 + 4
        brow = sb("f0brow", [NB1, P], c=held)

        def ffn0_weights(c):
            def pool_(pool):
                nc.gpsimd.memset(brow[:, :], 0.0).then_inc(s_bt, 1)
            def sp_(sp):
                load(sp, w1[0][:, :, :], a["L0_ffn_sW1"].rearrange("(k p) n -> p k n", p=P))
                load(sp, w2[0][:, :, :], a["L0_ffn_sW2"].rearrange("(k p) n -> p k n", p=P))
                load(sp, w3[0][:, :], a["L0_ffn_sW3"])
                load(sp, sb3[:, :], row(a["L0_ffn_sb3"], F))
                for n in range(4):
                    load(sp, w1[n + 1][:, :, :], a["L0_ffn_eW1"][n].rearrange("(k p) n -> p k n", p=P))
                    load(sp, w2[n + 1][:, 0, :], a["L0_ffn_eW2"][n])
                    load(sp, w3[n + 1][0:64, :], a["L0_ffn_eW3"][n])
                    load(sp, w3[n + 1][64:65, :], a["L0_ffn_eb3"][n:n + 1])
                sp.wait_ge(s_bt, 1)
                load(sp, brow[0:2, :], a["L0_ffn_sb1"].rearrange("(a n) -> a n", a=2))
                load(sp, brow[2:6, :], a["L0_ffn_eb1"])
                load(sp, brow[6:7, :], a["L0_ffn_sb2"].rearrange("(a n) -> a n", a=1))
                load(sp, brow[7:11, 0:64], a["L0_ffn_eb2"])
            return pool_, sp_

        gated("gate0", 4, a["L0_ffn_gW"], a["L0_ffn_gb"], more=ffn0_weights)

        s_a, s_ar, s_b, s_br, s_c, s_cu = (sem(n) for n in ("hidden1_product", "hidden1_ready", "hidden2_product",
                                                            "hidden2_ready", "output_product", "output_used"))
        s_ex, s_exd, s_z = sem("route0_exponents_ready"), sem("route0_exp_ready"), sem("ffn0_constants_ready")
        with ExitStack() as c:
            ne = 4
            pr, eq, s1, s2 = (sb(f"route0_{n}", [P, NT, ne], c=c) for n in ("pr", "eq", "s1", "s2"))
            r0, v1, v2, kk = (sb(f"route0_{n}", [P, NT], c=c) for n in ("r0", "v1", "v2", "kk"))
            rank = sb("route0_rank", [P, ne], c=c)
            bcol = sb("f0bcol", [P, NB1], c=c)
            h1 = sb("f0h1", [P, 2, 4, GW], c=c)
            h2 = sb("f0h2", [P, 3, 2 * GW], c=c)
            slot = lambda n: n % 2 if n else 2
            ap_ = [ps(f"f0a{b}", [P, 512], c) for b in range(2)]
            bp_ = [ps(f"f0b{b}", [P, 512], c) for b in range(2)]
            yp = ps("f0y", [P, TU, F], c)
            block = c.enter_context(nc.Block())
            A = [(n, hf, ch) for n, (chs, _) in enumerate(NETS) for hf in range(2) for ch in range(chs)]
            NA_, NB_, NC_ = len(A), 2 * len(NETS), len(NETS)
            first_a = {n: min(i for i, u in enumerate(A) if u[0] == n) for n in range(NC_)}
            last_a = {n: max(i for i, u in enumerate(A) if u[0] == n) for n in range(NC_)}
            ORDER = ["A0", "A1", "B0", "A2", "B1", "C0", "A3", "B2", "C1", "A4", "B3", "C2", "B4", "C3", "C4"]
            evac = [u for u in ORDER if u[0] in "AB"]

            @block.gpsimd
            def _(pool):
                nc.gpsimd.iota(rank[:, :], [[-1, ne]], base=ne, channel_multiplier=0,
                               allow_small_or_imprecise_dtypes=True).then_inc(s_z, 1)
                pool.wait_ge(s_z, 1)
                nc.gpsimd.memset(h2[64:65, 0:2, :], 1.0).then_inc(s_z, 1)

            @block.tensor
            def _(pe):
                pe.wait_ge(loaded, total["loaded"])
                nc.tensor.transpose(ap_[0][:, 0:NB1], brow[:, :], ident[0:NB1, 0:NB1]).then_inc(s_bt, 1)
                pe.wait_ge(s_bt, 3)
                pe.wait_ge(s_z, 2)
                prime(pe, s_a, s_b, s_c)
                with pe.Fori(0, NG) as g:
                    for u in ORDER:
                        n = int(u[1])
                        chs, wd = NETS[n]
                        if u[0] == "A":
                            for q in range(first_a[n], last_a[n] + 1):
                                _, hf, ch = A[q]
                                done(pe, s_ar, g * NA_ + q - 1 if q else g * NA_)
                                for k in range(KF):
                                    m = nc.tensor.matmul(ap_[q % 2][:, 0:GW], w1[n][:, k, ch * P:(ch + 1) * P],
                                                         XT[:, k, bass.ds(g * (2 * GW) + hf * GW, GW)],
                                                         start=(k == 0), stop=(k == KF - 1))
                                m.then_inc(s_a, 1)
                        elif u[0] == "B":
                            for hf in range(2):
                                q = 2 * n + hf
                                done(pe, s_ar, g * NA_ + first_a[n] + (hf + 1) * chs)
                                done(pe, s_br, g * NB_ + q - 1 if q else g * NB_)
                                for ch in range(chs):
                                    m = nc.tensor.matmul(bp_[hf][0:wd, 0:GW], w2[n][:, ch, :], h1[:, n % 2, hf * chs + ch, :],
                                                         start=(ch == 0), stop=(ch == chs - 1))
                                m.then_inc(s_b, 1)
                        else:
                            done(pe, s_br, g * NB_ + 2 * n + 2)
                            done(pe, s_cu, g * NC_ + n)
                            for j in range(TU):
                                m = nc.tensor.matmul(yp[:, j, :], h2[0:wd + ones_row[n], slot(n), j * P:(j + 1) * P], w3[n][:, :],
                                                     start=True, stop=True)
                            m.then_inc(s_c, 1)

            @block.scalar
            def _(act):
                act.wait_ge(s_bt, 2)
                nc.scalar.activation(bcol[:, :], ap_[0][:, 0:NB1], ACT.Copy).then_inc(s_bt, 1)
                act.wait_ge(s_bt, 3)
                act.wait_ge(s_ex, 1)
                nc.scalar.activation(pr[:, :, :], pr[:, :, :], ACT.Exp).then_inc(s_exd, 1)
                act.wait_ge(s_ex, 2)
                nc.scalar.activation(v2[:, :], v2[:, :], ACT.Exp).then_inc(s_exd, 1)
                prime(act, s_ar, s_br)
                with act.Fori(0, NG) as g:
                    for u in evac:
                        n = int(u[1])
                        chs, wd = NETS[n]
                        if u[0] == "A":
                            for q in range(first_a[n], last_a[n] + 1):
                                _, hf, ch = A[q]
                                done(act, s_a, g * NA_ + q + 1)
                                done(act, s_b, g * NB_ + 2 * (n - 1) if n >= 2 else g * NB_)
                                bi = ch if n == 0 else 1 + n
                                nc.scalar.activation(h1[:, n % 2, hf * chs + ch, :], ap_[q % 2][:, 0:GW], ACT.Relu,
                                                     bias=bcol[:, bi:bi + 1]).then_inc(s_ar, 1)
                        else:
                            for hf in range(2):
                                done(act, s_b, g * NB_ + 2 * n + hf + 1)
                                done(act, s_c, g * NC_ + n - 1 if n >= 2 else g * NC_)
                                bi = 6 + n
                                nc.scalar.activation(h2[0:wd, slot(n), hf * GW:(hf + 1) * GW], bp_[hf][0:wd, 0:GW], ACT.Relu,
                                                     bias=bcol[0:wd, bi:bi + 1]).then_inc(s_br, 1)

            @block.vector
            def _(dve):
                v = chain(dve, c_v, "v")
                def step(ins):
                    v(ins)
                    v.wait()
                g = gate[:, :, 0:ne]
                wide = lambda x: x[:, :].unsqueeze(2).broadcast_to([P, NT, ne])
                step(nc.vector.tensor_reduce(r0[:, :], g, AX.X, ALU.max))
                nc.vector.tensor_tensor(pr[:, :, :], g, wide(r0), ALU.subtract).then_inc(s_ex, 1)
                dve.wait_ge(s_exd, 1)
                dve.wait_ge(s_z, 2)
                top_two(step, pr, eq, (s1, s2), (v1, v2), r0, kk, rank, ne)
                nc.vector.tensor_tensor(v2[:, :], v2[:, :], v1[:, :], ALU.subtract).then_inc(s_ex, 1)
                dve.wait_ge(s_exd, 2)
                step(nc.vector.tensor_scalar(r0[:, :], v2[:, :], 1.0, None, ALU.add))
                step(nc.vector.reciprocal(r0[:, :], r0[:, :]))
                step(nc.vector.tensor_tensor(s2[:, :, :], s2[:, :, :], wide(v2), ALU.mult))
                step(nc.vector.tensor_tensor(s1[:, :, :], s1[:, :, :], s2[:, :, :], ALU.add))
                step(nc.vector.tensor_tensor(g, s1[:, :, :], wide(r0), ALU.mult))
                dve.wait_ge(loaded, total["loaded"])
                prime(dve, s_cu)
                with dve.Fori(0, NG) as g:
                    v.enter(g, NC_ * TU + 1)
                    xg = X[:, bass.ds(g * TU, TU), :]
                    v(nc.vector.tensor_tensor(xg, xg, sb3[:, :].unsqueeze(1).broadcast_to([P, TU, F]), ALU.add))
                    for n in range(NC_):
                        done(dve, s_c, g * NC_ + n + 1)
                        v.wait()
                        for j in range(TU):
                            xt = X[:, bass.ds(g * TU + j, 1), :]
                            y = yp[:, j:j + 1, :]
                            if n == 0:
                                v(nc.vector.tensor_tensor(xt, xt, y, ALU.add))
                            else:
                                v(nc.vector.scalar_tensor_tensor(out=xt, in0=y,
                                                                 scalar=gate[:, bass.ds(g * TU + j, 1), n - 1:n].rearrange("p a b -> p (a b)"),
                                                                 in1=xt, op0=ALU.mult, op1=ALU.add))
                        v.wait()
                        dve.sem_inc(s_cu, 1)
                    v.leave(NG)
                total["v"] = v.base + v.n

        held.close()

        s_xst = [sem("xp_stored0"), sem("xp_stored1")]
        s_pw = sem("proj_weight_step")

        def xp_phase(c, w, bank):
            wn = sb("wproj_rows", [P, KF, F], c=c)
            bias, rowb = sb("xp_bias", [P, F], c=c), sb("xp_row", [P, 2, F], c=c)

            def loads(sp):
                load(sp, wn[:, :, :], a["L1_gnn_W_proj"].rearrange("(o p) i -> p o i", p=P))
                for b in range(2):
                    sp.dma_start(bias[:, b * P:(b + 1) * P], row(a["L1_gnn_b_proj"][b * P:(b + 1) * P], P)).then_inc(s_xst[b], 16)

            def pe_(pe):
                for k in range(KF):
                    for o in range(KF):
                        m = nc.tensor.transpose(bank[:, (k * KF + o) * P:(k * KF + o + 1) * P],
                                                wn[:, o, k * P:(k + 1) * P], ident[:, :])
                m.then_inc(s_pw, 1)
                pe.wait_ge(s_pw, 2)

            def act_(act):
                act.wait_ge(s_pw, 1)
                nc.scalar.activation(w[:, :, :], bank[:, :].rearrange("p (k n) -> p k n", k=KF), ACT.Copy).then_inc(s_pw, 1)

            def consume(v, dve, mm, g, j, s_use):
                b = j % 2
                dve.wait_ge(s_xst[b], 16 * (g * USES[b] + j // 2 + 1))
                if j == 0:
                    dve.wait_ge(s_xst[1], 16)
                v(nc.vector.tensor_tensor(rowb[:, b, :], mm[:, 0:F], bias[:, :], ALU.add))
                v.wait()
                nc.vector.tensor_scalar(rowb[:, b, :], rowb[:, b, :], 0.0, None, ALU.max).then_inc(s_use, 1)

            def rows(sp, s_use):
                with sp.Fori(0, NG) as g:
                    for j in range(TU):
                        t, b = g * TU + j, j % 2
                        done(sp, s_use, t + 1)
                        sp.dma_start(xp_tab[bass.ds(t * P, P), :], rowb[:, b, :]).then_inc(s_xst[b], 16)
                for b in range(2):
                    sp.wait_ge(s_xst[b], 16 * (NG * USES[b] + 1))
            return {"loads": loads, "consume": consume, "steps": 1, "rows": rows, "pe": pe_, "act": act_}

        norm_phase("xp", F, XT, xp_phase)

        s_mrow = [sem(f"max_rows_landed{b}") for b in range(NB)]
        s_mst = [sem(f"max_stored{b}") for b in range(NB)]
        s_midx, s_mdone, s_mx, s_mz = (sem(n) for n in ("max_index_ready", "max_chunk_ready", "max_step", "max_neutral_ready"))
        max_rows = max_tab[0:P * EP, :].rearrange("(p e) f -> p e f", p=P)
        last_max = sb("last_max", [P, F])
        with ExitStack() as c:
            mb = sb("mb", [P, NB, T, F], c=c)
            ix = sb("max_gather_index", [P, NB, T], I32, c=c)
            zero = sb("zero_row", [1, NB, F // 2], c=c)
            block = c.enter_context(nc.Block())

            @block.sync
            def _(sp):
                sp.wait_ge(s_mz, 1)
                for b in range(NB):
                    tab, r = ((max_tab, P * EP), (max_carry, P))[b // 2]
                    hb = slice((b % 2) * (F // 2), (b % 2 + 1) * (F // 2))
                    sp.dma_start(tab[r:r + 1, hb], zero[0:1, b, :]).then_inc(s_mst[b], 16)
                with sp.Fori(0, TRIPS) as i:
                    for k in range(NB):
                        sp.wait_ge(s_mdone, i * NB + k + 1)
                        sp.dma_start(max_rows[:, bass.ds((i * NB + k) * T, T), :], mb[:, k, :, :]).then_inc(s_mst[k], 16)
                for b in range(NB):
                    sp.wait_ge(s_mst[b], 16 * (TRIPS + 1))

            @block.gpsimd
            def _(pool):
                nc.gpsimd.memset(zero[:, :, :], 0.0).then_inc(s_mz, 1)
                with pool.Fori(0, TRIPS) as i:
                    for b in range(NB):
                        pool.wait_ge(s_mst[b], 16 * (i + 1))
                        pool.wait_ge(s_midx, i * NB + b + 1)
                        alone(pool)
                        for t in range(T):
                            pool.indirect_dma_start(mb[:, b, t, :], None, xp_tab,
                                                    bass.IndirectOffsetOnAxis(ix[:, b, t:t + 1], 0)).then_inc(s_mrow[b], 16)

            @block.vector
            def _(dve):
                v = chain(dve, c_v, "v")
                v(nc.vector.memset(last_max[:, :], 0.0))
                for b in range(NB):
                    nc.vector.tensor_copy(ix[:, b, :], src_i[:, b * T:(b + 1) * T]).then_inc(s_midx, 1)
                v.wait()
                with dve.Fori(0, TRIPS) as i:
                    for k in range(NB):
                        dve.wait_ge(s_mrow[k], 16 * T * (i + 1))
                        nc.vector.tensor_copy(ix[:, k, :], src_i[:, bass.ds(((i + 1) * NB + k) * T, T)]).then_inc(s_midx, 1)
                        for t in range(T):
                            n = (i * NB + k) * T + t
                            prev = mb[:, k, t - 1, :] if t else last_max[:, :]
                            if t or k:
                                dve.wait_ge(s_mx, n)
                            e = n
                            nc.vector.scalar_tensor_tensor(out=mb[:, k, t, :], in0=prev, scalar=keep[:, bass.ds(e, 1)],
                                                           in1=mb[:, k, t, :], op0=ALU.mult, op1=ALU.max).then_inc(s_mx, 1)
                        dve.wait_ge(s_mx, (i * NB + k + 1) * T)
                        nc.vector.tensor_copy(last_max[:, :], mb[:, k, T - 1, :]).then_inc(s_mdone, 1)
                        dve.wait_ge(s_mdone, i * NB + k + 1)
                v.wait()
                total["v"] = v.n

        s_mc = sem("max_carry_step")
        with ExitStack() as c:
            kc = sb("kc", [P, P], c=c)
            cm = sb("cm", [P, KF, P], c=c)
            crow = sb("mcrow", [P, F], c=c)
            ft = ps("ft", [P, 512], c)
            bk = ps("bk", [P, 512], c)
            block = c.enter_context(nc.Block())

            @block.tensor
            def _(pe):
                for k in range(KF):
                    m = nc.tensor.transpose(ft[:, k * P:(k + 1) * P], last_max[:, k * P:(k + 1) * P], ident[:, :])
                m.then_inc(s_mc, 1)
                pe.wait_ge(s_mc, 3)
                for k in range(KF):
                    m = nc.tensor.transpose(bk[:, k * P:(k + 1) * P], cm[:, k, :], ident[:, :])
                m.then_inc(s_mc, 1)

            @block.vector
            def _(dve):
                v = chain(dve, c_v, "v")
                v(nc.vector.memset(kc[:, 0:1], 0.0))
                v(nc.vector.tensor_tensor(kc[:, 1:P], dl_row[:, 1:P], dl_row[:, 0:P - 1], ALU.is_equal))
                v.wait()
                dve.wait_ge(s_mc, 1)
                for k in range(KF):
                    nc.vector.tensor_tensor_scan(cm[:, k, :], kc[:, :], ft[:, k * P:(k + 1) * P], 0.0,
                                                 ALU.mult, ALU.max).then_inc(s_mc, 1)
                dve.wait_ge(s_mc, 4)
                nc.vector.tensor_copy(crow[:, :], bk[:, 0:F]).then_inc(s_mc, 1)
                v.wait()
                total["v"] = v.n

            @block.sync
            def _(sp):
                sp.wait_ge(s_mc, 5)
                store(sp, max_carry[0:P, :], crow[:, :])
                sp.wait_ge(stored, total["stored"])

        own_x = xp_tab.rearrange("(t p) f -> p t f", p=P)
        s_ow = [sem("own_xp_landed0"), sem("own_xp_landed1")]
        s_sg = [sem("max_segment_landed0"), sem("max_segment_landed1")]
        (s_ix, s_fr, s_ag, s_at, s_as, s_lp, s_lo, s_w2, s_gfree) = (sem(n) for n in (
            "max_segment_index_ready", "aggregate_buffer_free", "aggregate_ready", "aggregate_transposed",
            "aggregateT_ready", "layer_product", "layer_out_ready", "layer_weight_step", "aggregate_transposed_group"))
        with ExitStack() as c:
            ox = sb("ox", [P, 2, TU, F], c=c)
            ge, gc = sb("mge", [P, 2, TU, F], c=c), sb("mgc", [P, 2, TU, F], c=c)
            ie, ic = sb("mie", [P, 2, TU], I32, c=c), sb("mic", [P, 2, TU], I32, c=c)
            wn = sb("wlr_rows", [P, 2, KF, F], c=c)
            wt = sb("wlr_t", [P, 2, KF, F], c=c)
            bl = sb("bl", [P, KF], c=c)
            ags = sb("ags", [P, 2, KF, P], c=c)
            tb = [ps(f"ltb{b}", [P, 512], c) for b in range(2)]
            ob = [ps(f"lob{b}", [P, 512], c) for b in range(2)]
            block = c.enter_context(nc.Block())

            @block.sync
            def _(sp):
                load(sp, wn[:, 0], a["L1_gnn_W_l"].rearrange("(o p) i -> p o i", p=P))
                load(sp, wn[:, 1], a["L1_gnn_W_r"].rearrange("(o p) i -> p o i", p=P))
                with nc.allow_non_contiguous_dma(reason="256 values"):
                    load(sp, bl[:, :], a["L1_gnn_b_l"].rearrange("(k p) -> p k", p=P))
                def trip(g, b):
                    sp.wait_ge(s_fr, g + 1)
                    sp.dma_start(ox[:, b, :, :], own_x[:, bass.ds(g * TU, TU), :]).then_inc(s_ow[b], 16)
                group_loop(sp, trip)

            @block.gpsimd
            def _(pool):
                def trip(g, b):
                    pool.wait_ge(s_fr, g + 1)
                    alone(pool)
                    nc.gpsimd.tensor_copy(ie[:, b, :], idx_end[:, bass.ds(g * TU, TU)]).then_inc(s_ix, 1)
                    nc.gpsimd.tensor_copy(ic[:, b, :], idx_carry[:, bass.ds(g * TU, TU)]).then_inc(s_ix, 1)
                    pool.wait_ge(s_ix, 2 * (g + 1))
                    alone(pool)
                    for j in range(TU):
                        for buf, ix, tab in ((ge, ie, max_tab), (gc, ic, max_carry)):
                            pool.indirect_dma_start(buf[:, b, j, :], None, tab,
                                                    bass.IndirectOffsetOnAxis(ix[:, b, j:j + 1], 0)).then_inc(s_sg[b], 16)
                group_loop(pool, trip)

            @block.vector
            def _(dve):
                v = chain(dve, c_v, "v")
                before, K = v.n, 1
                def trip(g, b):
                    v.base, v.n = before + g * K, 0
                    dve.wait_ge(s_ow[b], 8 * (g - b + 2))
                    dve.wait_ge(s_sg[b], 16 * TU * (g - b + 2))
                    v(nc.vector.tensor_tensor(ge[:, b], ge[:, b], gc[:, b], ALU.max))
                    v.wait()
                    nc.vector.tensor_tensor(ge[:, b], ge[:, b], ox[:, b], ALU.max).then_inc(s_ag, 1)
                group_loop(dve, trip)
                total["v"] = before + NG * K

            @block.tensor
            def _(pe):
                pe.wait_ge(loaded, total["loaded"])
                for s in range(2):
                    for k in range(KF):
                        for o in range(KF):
                            m = nc.tensor.transpose(tb[s][:, (k * KF + o) * P:(k * KF + o + 1) * P],
                                                    wn[:, s, o, k * P:(k + 1) * P], ident[:, :])
                m.then_inc(s_w2, 1)
                pe.wait_ge(s_w2, 3)
                pe.sem_inc(s_fr, 2)
                prime(pe, s_at, s_lp)
                def trip(g, b):
                    pe.wait_ge(s_ag, g + 1)
                    def turn(j):
                        q = j % 2
                        done(pe, s_as, g * TU + j - 1 if j >= 2 else g * TU)
                        for k in range(KF):
                            m = nc.tensor.transpose(tb[q][:, k * P:(k + 1) * P], ge[:, b, j, k * P:(k + 1) * P], ident[:, :])
                        m.then_inc(s_at, 1)
                    turn(0)
                    for j in range(TU):
                        t, q = g * TU + j, j % 2
                        if j + 1 < TU:
                            turn(j + 1)
                        done(pe, s_as, t + 1)
                        done(pe, s_lo, t - 1 if j >= 2 else g * TU)
                        for o in range(KF):
                            for k in range(KF):
                                nc.tensor.matmul(ob[q][:, o * P:(o + 1) * P], wt[:, 0, k, o * P:(o + 1) * P], ags[:, q, k, :],
                                                 start=(k == 0), stop=False)
                            for k in range(KF):
                                m = nc.tensor.matmul(ob[q][:, o * P:(o + 1) * P], wt[:, 1, k, o * P:(o + 1) * P],
                                                     XT[:, k, bass.ds(t * P, P)], start=False, stop=(k == KF - 1))
                        m.then_inc(s_lp, 1)
                    pe.wait_ge(s_as, g * TU + TU + 1)
                    pe.sem_inc(s_fr, 1)
                group_loop(pe, trip)

            @block.scalar
            def _(act):
                act.wait_ge(s_w2, 1)
                for s in range(2):
                    nc.scalar.activation(wt[:, s, :, :], tb[s][:, :].rearrange("p (k n) -> p k n", k=KF), ACT.Copy).then_inc(s_w2, 1)
                act.wait_ge(loaded, total["loaded"])
                prime(act, s_as, s_lo)
                def trip(g, b):
                    def take(j):
                        done(act, s_at, g * TU + j + 1)
                        done(act, s_lp, g * TU + j - 1 if j >= 2 else g * TU)
                        nc.scalar.activation(ags[:, j % 2, :, :], tb[j % 2][:, 0:F].rearrange("p (k n) -> p k n", k=KF),
                                             ACT.Copy).then_inc(s_as, 1)
                    take(0)
                    for j in range(TU):
                        t, q = g * TU + j, j % 2
                        if j + 1 < TU:
                            take(j + 1)
                        done(act, s_lp, t + 1)
                        alone(act)
                        for o in range(KF):
                            m = nc.scalar.activation(XT[:, o, bass.ds(t * P, P)], ob[q][:, o * P:(o + 1) * P], ACT.Relu,
                                                     bias=bl[:, o:o + 1])
                        m.then_inc(s_lo, 1)
                group_loop(act, trip)

        SC = 250
        assert N % SC == 0
        s_bst, s_bp, s_bq, s_nx, s_nt, s_nu = (sem(n) for n in ("bn_stats_step", "bn_var_ready", "bn_std_ready", "bn_scaled",
                                                               "bn_transposed", "bn_added"))
        with ExitStack() as c:
            st6 = sb("bn6", [P, KF, N // SC, 6], c=c)
            mv = sb("bnmv", [P, KF, 2], c=c)
            gm, bt = sb("gm", [P, KF], c=c), sb("bt", [P, KF], c=c)
            scl, shf = sb("scl", [P, KF], c=c), sb("shf", [P, KF], c=c)
            nx = sb("nx", [P, 2, KF, P], c=c)
            nb_ = [ps(f"bnb{b}", [P, 512], c) for b in range(2)]
            block = c.enter_context(nc.Block())

            @block.sync
            def _(sp):
                with nc.allow_non_contiguous_dma(reason="256 values each"):
                    load(sp, gm[:, :], a["L1_gnn_gamma"].rearrange("(k p) -> p k", p=P))
                    load(sp, bt[:, :], a["L1_gnn_beta"].rearrange("(k p) -> p k", p=P))

            @block.scalar
            def _(act):
                prime(act, s_nx)
                act.wait_ge(s_bp, 1)
                nc.scalar.activation(scl[:, :], mv[:, :, 1], ACT.Sqrt).then_inc(s_bq, 1)
                act.wait_ge(s_bp, 2)
                with act.Fori(0, NG) as g:
                    for j in range(TU):
                        t, q = g * TU + j, j % 2
                        done(act, s_nt, t - 1 if j >= 2 else g * TU)
                        alone(act)
                        for k in range(KF):
                            m = nc.scalar.activation(nx[:, q, k, :], XT[:, k, bass.ds(t * P, P)], ACT.Identity,
                                                     scale=scl[:, k:k + 1], bias=shf[:, k:k + 1])
                        m.then_inc(s_nx, 1)

            @block.tensor
            def _(pe):
                prime(pe, s_nt)
                with pe.Fori(0, NG) as g:
                    for j in range(TU):
                        t, q = g * TU + j, j % 2
                        done(pe, s_nx, t + 1)
                        done(pe, s_nu, t - 1 if j >= 2 else g * TU)
                        for k in range(KF):
                            m = nc.tensor.transpose(nb_[q][:, k * P:(k + 1) * P], nx[:, q, k, :], ident[:, :])
                        m.then_inc(s_nt, 1)

            @block.vector
            def _(dve):
                v = chain(dve, c_v, "v")
                prime(dve, s_nu)
                for k in range(KF):
                    for n in range(N // SC):
                        v(nc.vector.bn_stats(st6[:, k, n, :], XT[:, k, n * SC:(n + 1) * SC]))
                v.wait()
                for k in range(KF):
                    v(nc.vector.bn_aggr(mv[:, k, :], st6[:, k, :, :]))
                v.wait()
                nc.vector.tensor_scalar(mv[:, :, 1], mv[:, :, 1], 1e-5, None, ALU.add).then_inc(s_bp, 1)
                dve.wait_ge(s_bq, 1)
                dve.wait_ge(loaded, total["loaded"])
                for ins in (lambda: nc.vector.reciprocal(scl[:, :], scl[:, :]),
                            lambda: nc.vector.tensor_tensor(scl[:, :], scl[:, :], gm[:, :], ALU.mult),
                            lambda: nc.vector.tensor_tensor(shf[:, :], scl[:, :], mv[:, :, 0], ALU.mult)):
                    v(ins())
                    v.wait()
                nc.vector.tensor_tensor(shf[:, :], bt[:, :], shf[:, :], ALU.subtract).then_inc(s_bp, 1)
                with dve.Fori(0, NG) as g:
                    for j in range(TU):
                        t, q = g * TU + j, j % 2
                        done(dve, s_nt, t + 1)
                        xt = X[:, bass.ds(t, 1), :]
                        nc.vector.tensor_tensor(xt, xt, nb_[q][:, 0:F].unsqueeze(1), ALU.add).then_inc(s_nu, 1)
                done(dve, s_nu, NT)
                total["v"] = v.n


        NE, FH = 8, 1024
        NF = FH // P
        ST = 2 * P
        MT = -(-(2 * NP + NE * (ST - 1)) // ST)
        ET = -(-NP // ST)
        assert MT % 2 == 1 and NP < 2 ** 24
        slot_x, slot_y = dram("slot_x", (MT * ST, F)), dram("slot_y", (MT * ST, F))
        bias_tab = dram("bias_tab", (NE, P, NF))
        pos = [sb(f"slot{k}", [P, NT], I32) for k in range(2)]
        wsel = [sb(f"weight{k}", [P, NT]) for k in range(2)]
        tile_e = sb("tile_e", [P, MT], I32)
        sbcol = sb("sbcol", [P, NF])
        mean1, rstd1 = sb("mean1", [P, NT]), sb("rstd1", [P, NT])
        s_zr, s_zf = sem("slot_zeros_ready"), sem("slots_zeroed")

        s_sh, s_shr, s_sh2, s_sy, s_syu = (sem(n) for n in ("shared_hidden_product", "shared_hidden_ready", "shared_hidden_used",
                                                            "shared_out_ready", "shared_out_used"))

        class Shared:
            def __init__(self, c, tag):
                self.tag = tag
                self.w1 = sb("shw1" + tag, [P, KF, FH], c=c)
                self.w2 = sb("shw2" + tag, [P, NF, F], c=c)

            def open(self, c):
                tag = self.tag
                self.ht = sb("shht" + tag, [P, 2, 2 * GW], c=c)
                self.hp = [ps(f"shh{b}" + tag, [P, 2, 512], c) for b in range(1)]
                self.yp = ps("shy" + tag, [P, TU, F], c)
                self.h_at = lambda f, hf: self.hp[0][:, hf, 0:GW]

            def loads(self, sp):
                load(sp, self.w1[:, :, :], a["L1_ffn_W1s"].rearrange("(k p) n -> p k n", p=P))
                load(sp, self.w2[:, :, :], a["L1_ffn_W2s"].rearrange("(k p) n -> p k n", p=P))

            def pe(self, pe, g0, g1):
                with pe.Fori(g0, g1) as g:
                    for f in range(NF + 1):
                        if f < NF:
                            for hf in range(2):
                                done(pe, s_shr, (g * NF + f) * 2 + hf - 1 if f or hf else g * NF * 2)
                                for k in range(KF):
                                    m = nc.tensor.matmul(self.h_at(f, hf), self.w1[:, k, f * P:(f + 1) * P],
                                                         XT[:, k, bass.ds(g * (2 * GW) + hf * GW, GW)],
                                                         start=(k == 0), stop=(k == KF - 1))
                                m.then_inc(s_sh, 1)
                        if f >= 1:
                            q = f - 1
                            done(pe, s_shr, (g * NF + q + 1) * 2)
                            if q == 0:
                                done(pe, s_syu, g)
                            for j in range(TU):
                                m = nc.tensor.matmul(self.yp[:, j, :], self.ht[:, q % 2, j * P:(j + 1) * P], self.w2[:, q, :],
                                                     start=(q == 0 and j % 2 == 0),
                                                     stop=(q == NF - 1 and (j % 2 == 1 or j == TU - 1)))
                            m.then_inc(s_sh2 if q < NF - 1 else s_sy, 1)

            def act(self, act, g0, g1):
                with act.Fori(g0, g1) as g:
                    for f in range(NF):
                        for hf in range(2):
                            done(act, s_sh, (g * NF + f) * 2 + hf + 1)
                            if f >= 2:
                                done(act, s_sh2, g * (NF - 1) + f - 1)
                            elif f == 0:
                                done(act, s_sh2, g * (NF - 1))
                            else:
                                done(act, s_sy, g)
                            nc.scalar.activation(self.ht[:, f % 2, hf * GW:(hf + 1) * GW], self.h_at(f, hf),
                                                 ACT.Gelu, bias=sbcol[:, f:f + 1]).then_inc(s_shr, 1)

            def dve(self, dve, v, g):
                done(dve, s_sy, g + 1)
                xg = X[:, g * TU:(g + 1) * TU, :]
                v.wait()
                nc.vector.tensor_tensor(xg, xg, self.yp[:, :, :], ALU.add).then_inc(s_syu, 1)
                done(dve, s_syu, g + 1)

        held = ExitStack()
        early = Shared(held, "a")
        brow, b2s = sb("f1brow", [(NE + 1) * NF, P], c=held), sb("f1b2s", [P, F], c=held)

        zt = sb("slot_zeros", [P, 6, F], c=held)

        def zero_slots(c):
            def pool_(pool):
                nc.gpsimd.memset(zt[:, :, :], 0.0).then_inc(s_zr, 1)
            def sp_(sp):
                early.loads(sp)
                load(sp, brow[0:NF, :], a["L1_ffn_b1s"].rearrange("(c p) -> c p", p=P))
                load(sp, brow[NF:, :], a["L1_ffn_b1p"].rearrange("e (c p) -> (e c) p", p=P))
                load(sp, b2s[:, :], row(a["L1_ffn_b2s"], F))
                sp.wait_ge(s_zr, 1)
                view = slot_x.rearrange("(p q) f -> p q f", p=P)
                for q in range(0, MT * ST // P, 6):
                    sp.dma_start(view[:, q:q + 6, :], zt[:, :, :]).then_inc(s_zf, 16)
            assert MT * ST // P % 6 == 0
            return pool_, sp_
        gated("gate1", 8, a["L1_ffn_Wr"], None, keep=(mean1, rstd1), more=zero_slots)

        G0 = 4
        s_rt, s_rte = sem("routing_step"), sem("gates_exp_ready")
        s_nr, s_pi, s_sc = sem("normalized_rows_ready"), sem("slot_index_ready"), [sem("rows_scattered0"), sem("rows_scattered1")]
        with ExitStack() as c:
            sh = early
            sh.open(c)
            bcol = sb("f1bcol", [P, (NE + 1) * NF], c=c)
            low = sb("low", [P, P], c=c)
            G = lambda n: sb(f"r1_{n}", [P, NT, NE], c=c)
            pr, eq, s1, s2, sel, tot, rk_ = G("pr"), G("eq"), G("s1"), G("s2"), G("sel"), G("tot"), G("rk")
            incl = sb("r1_incl", [P, NE, NT], c=c)
            R = lambda n: sb(f"r1_{n}", [P, NT], c=c)
            r0, v1, v2, kk, onest = R("r0"), R("v1"), R("v2"), R("kk"), R("ones")
            rank = sb("r1_rank", [P, NE], c=c)
            thr, cmp_ = sb("r1_thr", [P, ET], c=c), sb("r1_cmp", [P, NE, ET], c=c)
            ntl, tend, base = (sb(f"r1_{n}", [P, NE], c=c) for n in ("ntl", "tend", "base"))
            tno, tcm, tex = sb("r1_tno", [P, MT], c=c), sb("r1_tcm", [P, MT, NE], c=c), sb("r1_tex", [P, MT], c=c)
            xrow = sb("r1_xrow", [P, 2, TU, F], c=c)
            pi = sb("r1_pi", [P, 2, 2, TU], I32, c=c)
            rp = ps("r1_rp", [P, 2, 512], c)
            block = c.enter_context(nc.Block())

            @block.sync
            def _(sp):
                sp.wait_ge(s_rt, 7)
                store(sp, bias_tab.rearrange("e p c -> p e c"), bcol[:, NF:].rearrange("p (e c) -> p e c", e=NE))
                sp.wait_ge(stored, total["stored"])

            @block.gpsimd
            def _(pool):
                for out_, pat, b_ in ((rank[:, :], [[-1, NE]], NE), (thr[:, :], [[ST, ET]], 0), (tno[:, :], [[1, MT]], 0)):
                    nc.gpsimd.iota(out_, pat, base=b_, channel_multiplier=0, allow_small_or_imprecise_dtypes=True).then_inc(s_rt, 1)
                nc.gpsimd.affine_select(out=low[:, :], in_=ones[:, :], compare_op=ALU.is_gt, fill=0.0,
                                        base=0, pattern=[[1, P]], channel_multiplier=-1).then_inc(s_rt, 1)
                nc.gpsimd.memset(onest[:, :], 1.0).then_inc(s_rt, 1)
                pool.wait_ge(s_zf, 16 * (MT * ST // P // 6))
                pool.wait_ge(s_rt, 11)
                def trip(g, b):
                    pool.wait_ge(s_nr, g + 1)
                    alone(pool)
                    for k in range(2):
                        nc.gpsimd.tensor_copy(pi[:, b, k, :], pos[k][:, bass.ds(g * TU, TU)]).then_inc(s_pi, 1)
                    pool.wait_ge(s_pi, 2 * (g + 1))
                    alone(pool)
                    for j in range(TU):
                        for k in range(2):
                            pool.indirect_dma_start(slot_x, bass.IndirectOffsetOnAxis(pi[:, b, k, j:j + 1], 0),
                                                    xrow[:, b, j, :], None).then_inc(s_sc[b], 16)
                group_loop(pool, trip)
                for b in range(2):
                    pool.wait_ge(s_sc[b], 32 * TU * ((NG + 1 - b) // 2))

            @block.tensor
            def _(pe):
                pe.wait_ge(loaded, total["loaded"])
                nb1 = (NE + 1) * NF
                pe.wait_ge(s_rt, 5)
                nc.tensor.transpose(rp[:, 0, 0:nb1], brow[:, :], ident[0:nb1, 0:nb1]).then_inc(s_rt, 1)
                prime(pe, s_sh, s_sh2, s_sy)
                pe.wait_ge(s_rt, 7)
                sh.pe(pe, 0, 1)
                pe.wait_ge(s_rt, 9)
                nc.tensor.matmul(rp[:, 0, 0:NT * NE], low[:, :], sel[:, :, :].rearrange("p t e -> p (t e)"), start=True, stop=True)
                nc.tensor.matmul(rp[:, 1, 0:NT * NE], ones[:, :], sel[:, :, :].rearrange("p t e -> p (t e)"),
                                 start=True, stop=True).then_inc(s_rt, 1)
                sh.pe(pe, 1, G0)

            @block.scalar
            def _(act):
                act.wait_ge(s_rt, 6)
                nc.scalar.activation(sbcol[:, :], rp[:, 0, 0:NF], ACT.Copy).then_inc(s_rte, 1)
                nc.scalar.activation(bcol[:, :], rp[:, 0, 0:(NE + 1) * NF], ACT.Copy).then_inc(s_rt, 1)
                prime(act, s_shr)
                act.wait_ge(s_rt, 8)
                nc.scalar.activation(pr[:, :, :], pr[:, :, :], ACT.Exp).then_inc(s_rte, 1)
                sh.act(act, 0, G0)

            @block.vector
            def _(dve):
                v = chain(dve, c_v, "v")
                def step(ins):
                    v(ins)
                    v.wait()
                prime(dve, s_syu)
                g = gate[:, :, 0:NE]
                wide = lambda x: x[:, :].unsqueeze(2).broadcast_to([P, NT, NE])
                step(nc.vector.tensor_reduce(r0[:, :], g, AX.X, ALU.max))
                dve.wait_ge(s_rt, 7)
                nc.vector.tensor_tensor(pr[:, :, :], g, wide(r0), ALU.subtract).then_inc(s_rt, 1)
                dve.wait_ge(s_rte, 2)
                top_two(step, pr, eq, (s1, s2), (v1, v2), r0, kk, rank, NE)
                step(nc.vector.tensor_tensor(r0[:, :], v1[:, :], v2[:, :], ALU.add))
                step(nc.vector.reciprocal(r0[:, :], r0[:, :]))
                step(nc.vector.tensor_tensor(wsel[0][:, :], v1[:, :], r0[:, :], ALU.mult))
                step(nc.vector.tensor_tensor(wsel[1][:, :], v2[:, :], r0[:, :], ALU.mult))
                nc.vector.tensor_tensor(sel[:, :, :], s1[:, :, :], s2[:, :, :], ALU.add).then_inc(s_rt, 1)
                dve.wait_ge(s_rt, 10)
                pe_view = lambda k: rp[:, k, 0:NT * NE].rearrange("p (t e) -> p t e", e=NE)
                step(nc.vector.tensor_copy(tot[:, :, :], pe_view(1)))
                for e in range(NE):
                    v(nc.vector.tensor_tensor_scan(incl[:, e, :], onest[:, :], tot[:, :, e], 0.0, ALU.mult, ALU.add))
                v.wait()
                step(nc.vector.tensor_tensor(cmp_[:, :, :], incl[:, :, NT - 1:NT].broadcast_to([P, NE, ET]),
                                             thr[:, :].unsqueeze(1).broadcast_to([P, NE, ET]), ALU.is_gt))
                step(nc.vector.tensor_reduce(ntl[:, :], cmp_[:, :, :], AX.X, ALU.add))
                step(nc.vector.tensor_tensor_scan(tend[:, :], onest[:, 0:NE], ntl[:, :], 0.0, ALU.mult, ALU.add))
                step(nc.vector.tensor_tensor(base[:, :], tend[:, :], ntl[:, :], ALU.subtract))
                step(nc.vector.tensor_scalar(base[:, :], base[:, :], float(ST), None, ALU.mult))
                step(nc.vector.tensor_tensor(rk_[:, :, :], pe_view(0), tot[:, :, :], ALU.subtract))
                step(nc.vector.tensor_tensor(rk_[:, :, :], rk_[:, :, :], incl[:, :, :].rearrange("p e t -> p t e"), ALU.add))
                step(nc.vector.tensor_tensor(rk_[:, :, :], rk_[:, :, :], base[:, :].unsqueeze(1).broadcast_to([P, NT, NE]), ALU.add))
                for k, s in enumerate((s1, s2)):
                    step(nc.vector.tensor_tensor(s[:, :, :], s[:, :, :], rk_[:, :, :], ALU.mult))
                    step(nc.vector.tensor_reduce(r0[:, :], s[:, :, :], AX.X, ALU.add))
                    step(nc.vector.tensor_copy(pos[k][:, :], r0[:, :]))
                step(nc.vector.tensor_tensor(tcm[:, :, :], tend[:, :].unsqueeze(1).broadcast_to([P, MT, NE]),
                                             tno[:, :].unsqueeze(2).broadcast_to([P, MT, NE]), ALU.is_le))
                step(nc.vector.tensor_reduce(tex[:, :], tcm[:, :, :], AX.X, ALU.add))
                step(nc.vector.tensor_scalar(tex[:, :], tex[:, :], float(NE - 1), None, ALU.min))
                step(nc.vector.tensor_copy(tile_e[:, :], tex[:, :]))
                dve.sem_inc(s_rt, 1)
                def rows(g):
                    b = g % 2
                    if g >= 2:
                        dve.wait_ge(s_sc[b], 32 * TU * (g // 2))
                    xg = X[:, g * TU:(g + 1) * TU, :]
                    cols = slice(g * TU, (g + 1) * TU)
                    for j in range(TU):
                        t = g * TU + j
                        v(nc.vector.tensor_scalar(xrow[:, b, j, :], X[:, t, :], mean1[:, t:t + 1], rstd1[:, t:t + 1],
                                                  ALU.subtract, ALU.mult))
                    v.wait()
                    dve.sem_inc(s_nr, 1)
                    step(nc.vector.tensor_tensor(xg, xg, b2s[:, :].unsqueeze(1).broadcast_to([P, TU, F]), ALU.add))
                dve.wait_ge(loaded, total["loaded"])
                for g in range(NG):
                    rows(g)
                    if g % 2 == 1 or g == NG - 1:
                        sh.dve(dve, v, g // 2 if g < NG - 1 else G0 - 1)
                total["v"] = v.n


        held.close()

        RW, LAG, AHEAD = 4, 2, 3
        HI, LO = 0, 1
        s_wa = [sem("weights_0_3_landed0"), sem("weights_0_3_landed1")]
        s_wb = [sem("weights_4_7_landed0"), sem("weights_4_7_landed1")]
        s_b1, s_b2 = ([sem(f"expert_{n}_landed{b}") for b in range(2)] for n in ("hidden_bias", "output_bias"))
        s_xl = [sem("slot_rows_landed0"), sem("slot_rows_landed1")]
        s_ys = [sem("expert_rows_stored0"), sem("expert_rows_stored1")]
        s_whi, s_w2hi, s_wlo = sem("w1_high_ready"), sem("w2_high_ready"), sem("weights_low_ready")
        s_xtp, s_xhi, s_xlo = sem("slot_x_transposed"), sem("slot_xT_high_ready"), sem("slot_xT_low_ready")
        s_h, s_hr, s_hhi, s_hlo = (sem(n) for n in ("hidden_product", "hidden_ready", "hidden_high_ready", "hidden_low_ready"))
        s_l2, s_yr = sem("hidden_used"), sem("expert_rows_ready")
        W0, H0, U0 = 2 * NF, 2 * NF, RW + LAG
        with ExitStack() as c:
            wr = sb("ew_raw", [P, 2, NF, 2 * F], c=c)
            ws = sb("ew_split", [P, RW, 2, 2 * F], F32R, c=c)
            b1, b2 = sb("eb1", [P, 2, NF], c=c), sb("eb2", [P, 2, F], c=c)
            xs, xt = sb("xs", [P, 2, 2, F], c=c), sb("xt", [P, 2, 2, KF, ST], F32R, c=c)
            hf = sb("eh_full", [P, 2, ST], c=c)
            hs = sb("eh_split", [P, RW, 2, ST], F32R, c=c)
            yr = sb("yr", [P, 2, 2, F], c=c)
            hp = [ps(f"eh{b}", [P, 512], c) for b in range(2)]
            yp = [ps(f"ey{b}", [P, 2, F], c) for b in range(2)]
            tp = [ps(f"etp{b}", [P, KF, ST], c) for b in range(2)]
            slots = slot_x.rearrange("(n q p) f -> n p q f", p=P, q=2)
            slots_y = slot_y.rearrange("(n q p) f -> n p q f", p=P, q=2)
            block = c.enter_context(nc.Block())
            SPLIT = ((HI, HI), (HI, LO), (LO, HI))

            def tiles(eng, one):
                one(0, 0)
                with eng.Fori(0, (MT - 3) // 2) as i:
                    one(i * 2 + 1, 1)
                    one(i * 2 + 2, 0)
                one(MT - 2, 1)
                one(MT - 1, 0)

            def is_first(n):
                return isinstance(n, int) and n == 0

            def is_last(n):
                return isinstance(n, int) and n == MT - 1

            @block.sync
            def _(sp):
                def one(n, b):
                    e = sp.value_load(tile_e[0:1, bass.ds(n, 1)], min_val=0, max_val=NE - 1)
                    w1e = a["L1_ffn_W1p"][bass.ds(e, 1)].rearrange("e (k p) (f c) -> p (e k) f c", p=P, c=P)
                    w2e = a["L1_ffn_W2p"][bass.ds(e, 1)].rearrange("e (q p) c -> p (e q) c", p=P)
                    def rows1(f0, f1, s):
                        for k in range(KF):
                            sp.dma_start(wr[:, b, f0:f1, k * P:(k + 1) * P], w1e[:, k, f0:f1, :]).then_inc(s, 16)
                    sp.wait_ge(s_xtp, n + 1)
                    sp.dma_start(xs[:, b], slots[bass.ds(n, 1)].rearrange("n p q f -> (n p) q f")).then_inc(s_xl[b], 16)
                    sp.wait_ge(s_wlo, n * NF + 4)
                    rows1(0, 4, s_wa[b])
                    sp.dma_start(wr[:, b, 2:4, F:2 * F], w2e[:, 0:2, :]).then_inc(s_wa[b], 16)
                    sp.wait_ge(s_wlo, n * NF + 8)
                    rows1(4, NF, s_wb[b])
                    sp.dma_start(wr[:, b, 4:NF, F:2 * F], w2e[:, 2:NF - 2, :]).then_inc(s_wb[b], 16)
                    sp.wait_ge(s_hr, n * NF + 8)
                    sp.dma_start(b1[:, b], bias_tab[bass.ds(e, 1)].rearrange("e p c -> (e p) c")).then_inc(s_b1[b], 16)
                    sp.wait_ge(s_wlo, n * NF + 10)
                    sp.dma_start(wr[:, 1 - b, 0:2, F:2 * F], w2e[:, NF - 2:NF, :]).then_inc(s_wb[b], 16)
                    sp.wait_ge(s_yr, n + 1)
                    sp.dma_start(b2[:, b], a["L1_ffn_b2p"][bass.ds(e, 1)].broadcast_to([P, F])).then_inc(s_b2[b], 16)
                tiles(sp, one)

            def landed(n, b, per):
                return per // 2 * (n - b + 2)

            @block.tensor
            def _(pe):
                pe.sem_inc(s_xtp, 2)
                pe.sem_inc(s_h, 1)
                pe.sem_inc(s_l2, U0)
                def turn(n, b):
                    pe.wait_ge(s_xl[b], landed(n, b, 16))
                    for q in range(2):
                        for k in range(KF):
                            m = nc.tensor.transpose(tp[b][:, k, q * P:(q + 1) * P], xs[:, b, q, k * P:(k + 1) * P], ident[:, :])
                    m.then_inc(s_xtp, 1)
                def out_step(n, b, q, slot):
                    pe.wait_ge(s_hlo, n * NF + q + 3)
                    if q == 0:
                        pe.wait_ge(s_yr, n + 1)
                    for j in range(2):
                        for i, (h_, w_) in enumerate(SPLIT):
                            m = nc.tensor.matmul(yp[b][:, j, :], hs[:, q % RW, h_, j * P:(j + 1) * P], ws[:, slot, w_, F:2 * F],
                                                 start=(q == 0 and j == 0 and i == 0), stop=(q == NF - 1 and j == 1 and i == 2))
                    m.then_inc(s_l2, 1)
                turn(0, 0)
                def one(n, b):
                    for f in range(NF):
                        if f == 2 and not is_last(n):
                            turn(n + 1, 1 - b)
                        if f == 0:
                            done(pe, s_xlo, n + 1)
                        pe.wait_ge(s_wlo, n * NF + f + 1 + W0)
                        pe.wait_ge(s_hr, n * NF + f - 1 + H0)
                        for k in range(KF):
                            for i, (w_, x_) in enumerate(SPLIT):
                                m = nc.tensor.matmul(hp[f % 2][:, 0:ST], ws[:, f % RW, w_, k * P:(k + 1) * P], xt[:, b, x_, k, :],
                                                     start=(k == 0 and i == 0), stop=(k == KF - 1 and i == 2))
                        m.then_inc(s_h, 1)
                        if f >= LAG:
                            out_step(n, b, f - LAG, f % RW)
                        elif not is_first(n):
                            out_step(n - 1, 1 - b, NF + f - LAG, f % RW)
                tiles(pe, one)
                for f in range(LAG):
                    pe.wait_ge(s_wlo, MT * NF + f + 1 + W0)
                    out_step(MT - 1, 0, NF + f - LAG, f % RW)

            def step_of(n, b, f):
                return (n, b, f + AHEAD) if f + AHEAD < NF else (n + 1, 1 - b, f + AHEAD - NF)

            def needless(n, f):
                return isinstance(n, int) and n == MT and f >= LAG

            def weights_there(eng, n, b, f):
                if not (isinstance(n, int) and n == MT):
                    if f == 0:
                        eng.wait_ge(s_wa[b], landed(n, b, 48))
                    if f == 4:
                        eng.wait_ge(s_wb[b], landed(n, b, 64))
                eng.wait_ge(s_l2, n * NF + f + 1)

            @block.scalar
            def _(act):
                prime(act, s_whi, s_xhi, s_hhi)
                act.sem_inc(s_hr, H0)
                def high(n, b, f):
                    if needless(n, f):
                        return
                    weights_there(act, n, b, f)
                    nc.scalar.activation(ws[:, f % RW, HI, 0:F], wr[:, b, f, 0:F], ACT.Copy).then_inc(s_whi, 1)
                def turned(n, b):
                    act.wait_ge(s_xtp, n + 3)
                    nc.scalar.activation(xt[:, b, HI], tp[b][:, :, :], ACT.Copy).then_inc(s_xhi, 1)
                for f in range(AHEAD):
                    high(0, 0, f)
                turned(0, 0)
                def one(n, b):
                    act.wait_ge(s_b1[b], landed(n, b, 16))
                    for f in range(NF):
                        done(act, s_h, n * NF + f + 1)
                        act.wait_ge(s_hlo, n * NF + f + 1)
                        nc.scalar.activation(hf[:, f % 2, :], hp[f % 2][:, 0:ST], ACT.Gelu,
                                             bias=b1[:, b, f:f + 1]).then_inc(s_hr, 1)
                        act.wait_ge(s_hr, n * NF + f + 1 + H0)
                        act.wait_ge(s_l2, n * NF + f + 3)
                        nc.scalar.activation(hs[:, f % RW, HI, :], hf[:, f % 2, :], ACT.Copy).then_inc(s_hhi, 1)
                        high(*step_of(n, b, f))
                        if f == 3 and not is_last(n):
                            turned(n + 1, 1 - b)
                tiles(act, one)

            @block.vector
            def _(dve):
                prime(dve, s_xlo)
                dve.sem_inc(s_wlo, W0)
                dve.sem_inc(s_hlo, 2)
                dve.sem_inc(s_yr, 2)
                def low_(n, b, f):
                    if needless(n, f):
                        return
                    done(dve, s_whi, n * NF + f + 1)
                    done(dve, s_w2hi, n * NF + f + 1)
                    nc.vector.tensor_tensor(ws[:, f % RW, LO, :], wr[:, b, f, :], ws[:, f % RW, HI, :].bitcast(F32),
                                            ALU.subtract).then_inc(s_wlo, 1)
                def turned(n, b):
                    done(dve, s_xhi, n + 1)
                    nc.vector.tensor_tensor(xt[:, b, LO], tp[b][:, :, :], xt[:, b, HI].bitcast(F32), ALU.subtract).then_inc(s_xlo, 1)
                def rows(n, b):
                    dve.wait_ge(s_b2[b], landed(n, b, 16))
                    dve.wait_ge(s_l2, (n + 1) * NF + U0)
                    dve.wait_ge(s_ys[b], landed(n, b, 16))
                    nc.vector.tensor_tensor(yr[:, b], yp[b][:, :, :], b2[:, b].unsqueeze(1).broadcast_to([P, 2, F]),
                                            ALU.add).then_inc(s_yr, 1)
                for f in range(AHEAD):
                    low_(0, 0, f)
                turned(0, 0)
                def one(n, b):
                    for f in range(NF):
                        done(dve, s_hhi, n * NF + f + 1)
                        nc.vector.tensor_tensor(hs[:, f % RW, LO, :], hf[:, f % 2, :], hs[:, f % RW, HI, :].bitcast(F32),
                                                ALU.subtract).then_inc(s_hlo, 1)
                        low_(*step_of(n, b, f))
                        if f == 2 and not is_first(n):
                            rows(n - 1, 1 - b)
                        if f == 3 and not is_last(n):
                            turned(n + 1, 1 - b)
                tiles(dve, one)
                rows(MT - 1, 0)

            @block.gpsimd
            def _(pool):
                nc.gpsimd.memset(wr[:, 0, 0:2, F:2 * F], 0.0).then_inc(s_w2hi, 1)
                for b in range(2):
                    pool.dma_start(yr[:, b], slots[0]).then_inc(s_ys[b], 16)
                def high2(n, b, f):
                    if needless(n, f):
                        return
                    weights_there(pool, n, b, f)
                    pool.wait_ge(s_wlo, n * NF + f - RW + 1 + W0)
                    alone(pool)
                    nc.gpsimd.tensor_copy(ws[:, f % RW, HI, F:2 * F], wr[:, b, f, F:2 * F]).then_inc(s_w2hi, 1)
                pool.wait_ge(s_w2hi, 1)
                for f in range(AHEAD):
                    high2(0, 0, f)
                def put(n, b):
                    pool.wait_ge(s_yr, n + 3)
                    alone(pool)
                    pool.dma_start(slots_y[bass.ds(n, 1)].rearrange("n p q f -> (n p) q f"), yr[:, b]).then_inc(s_ys[b], 16)
                def one(n, b):
                    for f in range(NF):
                        high2(*step_of(n, b, f))
                        if f == 4 and not is_first(n):
                            put(n - 1, 1 - b)
                tiles(pool, one)
                put(MT - 1, 0)
                for b in range(2):
                    pool.wait_ge(s_ys[b], 16 * ((MT + 1 - b) // 2 + 1))

        s_gi, s_gr, s_gf = sem("sum_index_ready"), [sem("sum_rows_landed0"), sem("sum_rows_landed1")], sem("sum_buffer_free")
        with ExitStack() as c:
            sh = Shared(c, "b")
            sh.open(c)
            rows_ = [sb(f"sum_rows{k}", [P, 2, TU, F], c=c) for k in range(2)]
            pi = sb("sum_pi", [P, 2, 2, TU], I32, c=c)
            block = c.enter_context(nc.Block())

            @block.sync
            def _(sp):
                sh.loads(sp)
                for g in range(NG):
                    sp.wait_ge(s_gf, g + 3)
                    t0, t1 = g * TU, min((g + 1) * TU, NT - 1)
                    store(sp, out[t0 * P:t1 * P, :].rearrange("(t p) f -> p t f", p=P), X[:, t0:t1, :])
                store(sp, out[(NT - 1) * P:N, :], X[0:TAIL, NT - 1, :])
                sp.wait_ge(stored, total["stored"])

            @block.gpsimd
            def _(pool):
                def trip(g, b):
                    pool.wait_ge(s_gf, g + 1)
                    alone(pool)
                    for k in range(2):
                        nc.gpsimd.tensor_copy(pi[:, b, k, :], pos[k][:, bass.ds(g * TU, TU)]).then_inc(s_gi, 1)
                    pool.wait_ge(s_gi, 2 * (g + 1))
                    alone(pool)
                    for j in range(TU):
                        for k in range(2):
                            pool.indirect_dma_start(rows_[k][:, b, j, :], None, slot_y,
                                                    bass.IndirectOffsetOnAxis(pi[:, b, k, j:j + 1], 0)).then_inc(s_gr[b], 16)
                group_loop(pool, trip)

            @block.tensor
            def _(pe):
                pe.wait_ge(loaded, total["loaded"])
                sh.pe(pe, G0, NG)

            @block.scalar
            def _(act):
                sh.act(act, G0, NG)

            @block.vector
            def _(dve):
                v = chain(dve, c_v, "v")
                dve.sem_inc(s_gf, 2)
                for g in range(NG):
                    b = g % 2
                    dve.wait_ge(s_gr[b], 32 * TU * (g // 2 + 1))
                    for k in range(2):
                        v.wait()
                        for j in range(TU):
                            t = g * TU + j
                            v(nc.vector.scalar_tensor_tensor(out=X[:, t, :], in0=rows_[k][:, b, j, :], scalar=wsel[k][:, t:t + 1],
                                                             in1=X[:, t, :], op0=ALU.mult, op1=ALU.add))
                    v.wait()
                    dve.sem_inc(s_gf, 1)
                    if g % 2 == 1:
                        sh.dve(dve, v, G0 + g // 2)
                total["v"] = v.n


_INS = ["x", "src", "dst",
        "L0_gnn_W_l", "L0_gnn_b_l", "L0_gnn_W_r", "L0_gnn_b_r", "L0_gnn_att", "L0_gnn_bias",
        "L0_ffn_sW1", "L0_ffn_sb1", "L0_ffn_sW2", "L0_ffn_sb2", "L0_ffn_sW3", "L0_ffn_sb3",
        "L0_ffn_eW1", "L0_ffn_eb1", "L0_ffn_eW2", "L0_ffn_eb2", "L0_ffn_eW3", "L0_ffn_eb3", "L0_ffn_gW", "L0_ffn_gb",
        "L1_gnn_W_proj", "L1_gnn_b_proj", "L1_gnn_W_l", "L1_gnn_b_l", "L1_gnn_W_r", "L1_gnn_gamma", "L1_gnn_beta",
        "L1_ffn_Wr", "L1_ffn_W1s", "L1_ffn_b1s", "L1_ffn_W2s", "L1_ffn_b2s", "L1_ffn_W1p", "L1_ffn_b1p",
        "L1_ffn_W2p", "L1_ffn_b2p"]


def kernel(**inputs):
    import numpy as _np
    import concourse.bacc as _bacc
    from concourse import mybir as _mybir
    from concourse.bass_utils import run_bass_kernel_spmd as _run

    nc = _bacc.Bacc("TRN2", target_bir_lowering=False, num_devices=1)
    arrays, aps = {}, {}
    for name in _INS:
        v = _np.ascontiguousarray(inputs[name])
        arrays[f"in_{name}"] = v
        aps[name] = nc.dram_tensor(f"in_{name}", v.shape, _mybir.dt.from_np(v.dtype), kind="ExternalInput").ap()
    out = nc.dram_tensor("out", (N, F), _mybir.dt.float32, kind="ExternalOutput").ap()
    graph_block_kernel(nc, aps, out)
    r = _run(nc, [arrays], core_ids=[0])
    return r.results[0]["out"]
```
